# Optimizing a Trainium2 kernel written in Bass

```python
import numpy as np
import jax
import jax.numpy as jnp

def _softmax(x, axis=-1):
    return jax.nn.softmax(x, axis=axis)

def _gelu(x):
    return jax.nn.gelu(x, approximate=True)

def _silu(x):
    return jax.nn.silu(x)

def _sigmoid(x):
    return jax.nn.sigmoid(x)

def _layernorm(x, axis=-1, eps=1e-05):
    m = jnp.mean(x, axis=axis, keepdims=True)
    v = jnp.var(x, axis=axis, keepdims=True)
    return (x - m) / jnp.sqrt(v + eps)

def _scatter_add(tgt, idx, src, axis=0):
    return tgt.at[idx].add(src)

def _segment_sum(src, seg, n):
    return jax.ops.segment_sum(src, seg, n)
kernel_name = 'mk_perceiver_d2_seqx_r8_18cf1c'

def setup_inputs(seed: int=0):
    np.random.seed(seed)
    _w = jnp.asarray

    def _rec_inputs():
        import jax
        import jax.numpy as jnp
        _rk = jax.random.key(seed)
        x = 7.22e-05 + 1 * jax.random.normal(jax.random.fold_in(_rk, 1), (1, 64, 256), jnp.float32)
        _lenS = 64 - jax.random.randint(jax.random.fold_in(_rk, 7), (1,), 0, max(1, 64 // 4) + 1, jnp.int32)
        _lenS2 = 6272 - jax.random.randint(jax.random.fold_in(_rk, 8), (1,), 0, max(1, 6272 // 4) + 1, jnp.int32)
        _ctx_512P = jax.random.normal(jax.random.fold_in(_rk, 11), (1, 16, 64), jnp.float32)
        _ctx_512c = jax.random.dirichlet(jax.random.fold_in(_rk, 511), 0.3 * jnp.ones((16,), jnp.float32), (1, 6272))
        _ctx_512t = jnp.einsum('bsk,bkd->bsd', _ctx_512c, _ctx_512P)
        _ctx_512t = _ctx_512t * jax.lax.rsqrt(jnp.mean(jnp.square(_ctx_512t)) + 1e-12) * 0.953939
        ctx_512 = -0.000514642 + 1.00011 * (_ctx_512t + 0.3 * jax.random.normal(jax.random.fold_in(_rk, 611), (1, 6272, 64), jnp.float32))
        return (x, ctx_512)
    x, ctx_512 = _rec_inputs()

    def _L0_xattn_setup():
        import jax, jax.numpy as jnp
        import numpy as np
        B, S, H, NH, L = (2, 256, 256, 16, 64)
        HD = H // NH
        key = jax.random.key(seed)
        k1, k2, k3, k4, k5 = jax.random.split(key, 5)
        scale = 0.02
        return {'q': jax.random.normal(k1, (B, S, H), dtype=jnp.float32), 'latent_kv': jax.random.normal(k2, (B, S, L), dtype=jnp.float32), 'Wq': jax.random.normal(k3, (H, H), dtype=jnp.float32) * scale, 'Wkv_expand': jax.random.normal(k4, (2 * H, L), dtype=jnp.float32) * scale, 'Wout': jax.random.normal(k5, (H, H), dtype=jnp.float32) * scale}
    _L0_xattn_all = _L0_xattn_setup()
    _L0_xattn_in = {k: v for k, v in _L0_xattn_all.items() if k in ('Wq', 'Wkv_expand', 'Wout')}
    del _L0_xattn_all

    def _L0_attn_setup():
        import jax, jax.numpy as jnp
        import numpy as np
        D_MODEL = 256
        D_INNER = 512
        LN_EPS = 1e-05
        key = jax.random.key(seed)
        k1, k2, k3, k4 = jax.random.split(key, 4)
        B, S = (2, 512)
        x = jax.random.normal(k1, (B, S, D_MODEL), dtype=jnp.float32)
        gamma = jnp.ones((D_MODEL,), dtype=jnp.float32)
        beta = jnp.zeros((D_MODEL,), dtype=jnp.float32)
        W_in = jax.random.normal(k2, (2 * D_INNER, D_MODEL), dtype=jnp.float32) * 0.02
        W_out = jax.random.normal(k3, (D_MODEL, D_INNER), dtype=jnp.float32) * 0.02
        dt_min, dt_max = (0.001, 0.1)
        dt = jax.random.uniform(k4, (D_INNER,), dtype=jnp.float32) * (dt_max - dt_min) + dt_min
        return {'x': x, 'gamma': gamma, 'beta': beta, 'W_in': W_in, 'W_out': W_out, 'dt': dt}
    _L0_attn_all = _L0_attn_setup()
    _L0_attn_in = {k: v for k, v in _L0_attn_all.items() if k in ('gamma', 'beta', 'W_in', 'W_out', 'dt')}
    del _L0_attn_all

    def _L0_ffn_setup():
        import jax, jax.numpy as jnp
        import numpy as np
        import math
        GOLDEN_CENTER = 1.0 / math.e
        GOLDEN_LOWER = 0.5 - math.log(4.0 / 3.0)
        GOLDEN_UPPER = 0.5
        B, T, D = (4, 128, 256)
        E = 8
        F = 1024 // (E // 2)
        R = 64
        NL = 2

        def _router_weights(x, Wr, temperature):
            logits = jnp.einsum('btd,de->bte', x, Wr)
            inhibition = jax.nn.sigmoid(logits / temperature)
            in_zone = (inhibition >= GOLDEN_LOWER) & (inhibition <= GOLDEN_UPPER)
            distance = jnp.abs(inhibition - GOLDEN_CENTER)
            w = jnp.exp(-distance / 0.1) * in_zone.astype(x.dtype)
            wsum = w.sum(axis=-1, keepdims=True)
            no_expert = wsum < 1e-08
            fb = jnp.exp(-distance / 0.3)
            _, top2 = jax.lax.top_k(fb, 2)
            fb_mask = jax.nn.one_hot(top2, E, dtype=x.dtype).sum(axis=-2)
            fb_w = fb * fb_mask
            fb_w = fb_w / jnp.clip(fb_w.sum(axis=-1, keepdims=True), 1e-08)
            w = jnp.where(no_expert, fb_w, w)
            return w / jnp.clip(w.sum(axis=-1, keepdims=True), 1e-08)
        key = jax.random.key(seed)
        ks = jax.random.split(key, 13)
        s = 0.02
        x = jax.random.normal(ks[0], (B, T, D), dtype=jnp.float32)
        Wg = jax.random.normal(ks[1], (E, D, F), dtype=jnp.float32) * s
        Wu = jax.random.normal(ks[2], (E, D, F), dtype=jnp.float32) * s
        Wd = jax.random.normal(ks[3], (E, F, D), dtype=jnp.float32) * s
        Ga = jax.random.normal(ks[4], (NL, D, R), dtype=jnp.float32) * s
        Gb = jax.random.normal(ks[5], (NL, R, F), dtype=jnp.float32) * s
        Ua = jax.random.normal(ks[6], (NL, D, R), dtype=jnp.float32) * s
        Ub = jax.random.normal(ks[7], (NL, R, F), dtype=jnp.float32) * s
        Da = jax.random.normal(ks[8], (NL, F, R), dtype=jnp.float32) * s
        Db = jax.random.normal(ks[9], (NL, R, D), dtype=jnp.float32) * s
        Wr = jax.random.normal(ks[10], (D, E), dtype=jnp.float32) * s
        temperature = jnp.ones((1,), dtype=jnp.float32)
        return {'x': x, 'Wg': Wg, 'Wu': Wu, 'Wd': Wd, 'Ga': Ga, 'Gb': Gb, 'Ua': Ua, 'Ub': Ub, 'Da': Da, 'Db': Db, 'Wr': Wr, 'temperature': temperature}
    _L0_ffn_all = _L0_ffn_setup()
    _L0_ffn_in = {k: v for k, v in _L0_ffn_all.items() if k in ('Wg', 'Wu', 'Wd', 'Ga', 'Gb', 'Ua', 'Ub', 'Da', 'Db', 'Wr', 'temperature')}
    del _L0_ffn_all

    def _L1_xattn_setup():
        import jax, jax.numpy as jnp
        import numpy as np
        B, S, L = (2, 128, 128)
        DIM_Q, H, K, D_C, D_CQ, R = (256, 16, 128, 64, 192, 64)

        def _rope_tables(length, dim):
            inv = 1.0 / 10000.0 ** (jnp.arange(0, dim, 2, dtype=jnp.float32) / dim)
            f = jnp.arange(length, dtype=jnp.float32)[:, None] * inv[None, :]
            sin = jnp.repeat(jnp.sin(f), 2, axis=-1)
            cos = jnp.repeat(jnp.cos(f), 2, axis=-1)
            return (sin, cos)

        def _rotate_half(x):
            half = x.shape[-1] // 2
            return jnp.concatenate([-x[..., half:], x[..., :half]], axis=-1)

        def _apply_rope(x, sin, cos):
            return x * cos + _rotate_half(x) * sin
        key = jax.random.key(seed)
        ks = jax.random.split(key, 8)
        return {'hidden_q': jax.random.normal(ks[0], (B, S, DIM_Q), jnp.float32), 'kv_c': jax.random.normal(ks[1], (B, L, D_C), jnp.float32), 'Wq': jax.random.normal(ks[2], (H * K, DIM_Q), jnp.float32) / np.sqrt(DIM_Q).astype(np.float32), 'w_kc_q': jax.random.normal(ks[3], (H, K, D_CQ), jnp.float32) / np.sqrt(K).astype(np.float32), 'w_kc_kv': jax.random.normal(ks[4], (H, K, D_C), jnp.float32) / np.sqrt(K).astype(np.float32), 'W_qr': jax.random.normal(ks[5], (H, D_CQ, R), jnp.float32) / np.float32(np.sqrt(D_CQ) * np.sqrt(R)), 'W_kr': jax.random.normal(ks[6], (H, D_C, R), jnp.float32) / np.sqrt(D_C).astype(np.float32), 'Wo': jax.random.normal(ks[7], (DIM_Q, H * K), jnp.float32) / np.sqrt(H * K).astype(np.float32)}
    _L1_xattn_all = _L1_xattn_setup()
    _L1_xattn_in = {k: v for k, v in _L1_xattn_all.items() if k in ('Wq', 'w_kc_q', 'w_kc_kv', 'W_qr', 'W_kr', 'Wo')}
    del _L1_xattn_all

    def _L1_attn_setup():
        import jax, jax.numpy as jnp
        import numpy as np
        N_HEAD = 32
        HEAD_ID = 0
        MASKED_BIAS = -10000.0
        key = jax.random.key(seed)
        k1, k2, k3 = jax.random.split(key, 3)
        B, S, E = (1, 256, 256)
        hidden_states = jax.random.normal(k1, (B, S, E), dtype=jnp.float32)
        W_attn = jax.random.normal(k2, (E, 3 * E), dtype=jnp.float32) * (1.0 / np.sqrt(E))
        b_attn = jnp.zeros((3 * E,), dtype=jnp.float32)
        W_proj = jax.random.normal(k3, (E, E), dtype=jnp.float32) * (1.0 / np.sqrt(E))
        b_proj = jnp.zeros((E,), dtype=jnp.float32)
        return {'hidden_states': hidden_states, 'W_attn': W_attn, 'b_attn': b_attn, 'W_proj': W_proj, 'b_proj': b_proj}
    _L1_attn_all = _L1_attn_setup()
    _L1_attn_in = {k: v for k, v in _L1_attn_all.items() if k in ('W_attn', 'b_attn', 'W_proj', 'b_proj')}
    del _L1_attn_all

    def _L1_ffn_setup():
        import jax, jax.numpy as jnp
        import numpy as np
        B, S, H, E, K, I = (2, 128, 256, 32, 8, 96)
        key = jax.random.key(seed)
        ks = jax.random.split(key, 5)
        scaled = lambda k, shp, fan: jax.random.normal(k, shp, jnp.float32) * fan ** (-0.5)
        return {'hidden_states': jax.random.normal(ks[0], (B, S, H), jnp.float32), 'router_w': scaled(ks[1], (E, H), H), 'w_gate': scaled(ks[2], (E, H, I), H), 'w_up': scaled(ks[3], (E, H, I), H), 'w_down': scaled(ks[4], (E, I, H), I)}
    _L1_ffn_all = _L1_ffn_setup()
    _L1_ffn_in = {k: v for k, v in _L1_ffn_all.items() if k in ('router_w', 'w_gate', 'w_up', 'w_down')}
    del _L1_ffn_all
    return {'x': x, 'ctx_512': ctx_512, 'L0_xattn_Wq': _L0_xattn_in['Wq'], 'L0_xattn_Wkv_expand': _L0_xattn_in['Wkv_expand'], 'L0_xattn_Wout': _L0_xattn_in['Wout'], 'L0_attn_gamma': _L0_attn_in['gamma'], 'L0_attn_beta': _L0_attn_in['beta'], 'L0_attn_W_in': _L0_attn_in['W_in'], 'L0_attn_W_out': _L0_attn_in['W_out'], 'L0_attn_dt': _L0_attn_in['dt'], 'L0_ffn_Wg': _L0_ffn_in['Wg'], 'L0_ffn_Wu': _L0_ffn_in['Wu'], 'L0_ffn_Wd': _L0_ffn_in['Wd'], 'L0_ffn_Ga': _L0_ffn_in['Ga'], 'L0_ffn_Gb': _L0_ffn_in['Gb'], 'L0_ffn_Ua': _L0_ffn_in['Ua'], 'L0_ffn_Ub': _L0_ffn_in['Ub'], 'L0_ffn_Da': _L0_ffn_in['Da'], 'L0_ffn_Db': _L0_ffn_in['Db'], 'L0_ffn_Wr': _L0_ffn_in['Wr'], 'L0_ffn_temperature': _L0_ffn_in['temperature'], 'L1_xattn_Wq': _L1_xattn_in['Wq'], 'L1_xattn_w_kc_q': _L1_xattn_in['w_kc_q'], 'L1_xattn_w_kc_kv': _L1_xattn_in['w_kc_kv'], 'L1_xattn_W_qr': _L1_xattn_in['W_qr'], 'L1_xattn_W_kr': _L1_xattn_in['W_kr'], 'L1_xattn_Wo': _L1_xattn_in['Wo'], 'L1_attn_W_attn': _L1_attn_in['W_attn'], 'L1_attn_b_attn': _L1_attn_in['b_attn'], 'L1_attn_W_proj': _L1_attn_in['W_proj'], 'L1_attn_b_proj': _L1_attn_in['b_proj'], 'L1_ffn_router_w': _L1_ffn_in['router_w'], 'L1_ffn_w_gate': _L1_ffn_in['w_gate'], 'L1_ffn_w_up': _L1_ffn_in['w_up'], 'L1_ffn_w_down': _L1_ffn_in['w_down']}

def reference(x, ctx_512, L0_xattn_Wq, L0_xattn_Wkv_expand, L0_xattn_Wout, L0_attn_gamma, L0_attn_beta, L0_attn_W_in, L0_attn_W_out, L0_attn_dt, L0_ffn_Wg, L0_ffn_Wu, L0_ffn_Wd, L0_ffn_Ga, L0_ffn_Gb, L0_ffn_Ua, L0_ffn_Ub, L0_ffn_Da, L0_ffn_Db, L0_ffn_Wr, L0_ffn_temperature, L1_xattn_Wq, L1_xattn_w_kc_q, L1_xattn_w_kc_kv, L1_xattn_W_qr, L1_xattn_W_kr, L1_xattn_Wo, L1_attn_W_attn, L1_attn_b_attn, L1_attn_W_proj, L1_attn_b_proj, L1_ffn_router_w, L1_ffn_w_gate, L1_ffn_w_up, L1_ffn_w_down):
    import jax
    import jax.numpy as jnp

    def _L0_xattn_ref(q, latent_kv, Wq, Wkv_expand, Wout):
        import jax, jax.numpy as jnp
        import numpy as np
        B, S, H, NH, L = (2, 256, 256, 16, 64)
        HD = H // NH
        b, sq, _ = q.shape
        sk = latent_kv.shape[1]
        qp = q @ Wq.T
        kv = latent_kv @ Wkv_expand.T
        k, v = jnp.split(kv, 2, axis=-1)
        qh = qp.reshape(b, sq, NH, HD).transpose(0, 2, 1, 3)
        kh = k.reshape(b, sk, NH, HD).transpose(0, 2, 1, 3)
        vh = v.reshape(b, sk, NH, HD).transpose(0, 2, 1, 3)
        inv_sqrt_d = 1.0 / jnp.sqrt(jnp.float32(HD))
        scores = jnp.einsum('bhqd,bhkd->bhqk', qh, kh) * inv_sqrt_d
        causal = jnp.tril(jnp.ones((sq, sk), dtype=bool))
        scores = jnp.where(causal, scores, jnp.finfo(scores.dtype).min)
        attn = jax.nn.softmax(scores, axis=-1)
        out = jnp.einsum('bhqk,bhkd->bhqd', attn, vh)
        out = out.transpose(0, 2, 1, 3).reshape(b, sq, H)
        return out @ Wout.T

    def _L0_attn_ref(x, gamma, beta, W_in, W_out, dt):
        import jax, jax.numpy as jnp
        import numpy as np
        D_MODEL = 256
        D_INNER = 512
        LN_EPS = 1e-05
        identity = x
        mu = jnp.mean(x, axis=-1, keepdims=True)
        var = jnp.mean(jnp.square(x - mu), axis=-1, keepdims=True)
        xn = (x - mu) * jax.lax.rsqrt(var + LN_EPS) * gamma + beta
        projected = jnp.einsum('bsd,ed->bse', xn, W_in)
        z, gate = jnp.split(projected, 2, axis=-1)
        z_gated = z * jax.nn.sigmoid(jnp.clip(z, -15.0, 15.0))
        dt_weights = jax.nn.softmax(-dt)
        z_temporal = z_gated * dt_weights
        output = z_temporal * jax.nn.silu(jnp.clip(gate, -15.0, 15.0))
        output = jnp.einsum('bse,de->bsd', output, W_out)
        return output + identity

    def _L0_ffn_ref(x, Wg, Wu, Wd, Ga, Gb, Ua, Ub, Da, Db, Wr, temperature):
        import jax, jax.numpy as jnp
        import numpy as np
        import math
        GOLDEN_CENTER = 1.0 / math.e
        GOLDEN_LOWER = 0.5 - math.log(4.0 / 3.0)
        GOLDEN_UPPER = 0.5
        B, T, D = (4, 128, 256)
        E = 8
        F = 1024 // (E // 2)
        R = 64
        NL = 2

        def _router_weights(x, Wr, temperature):
            logits = jnp.einsum('btd,de->bte', x, Wr)
            inhibition = jax.nn.sigmoid(logits / temperature)
            in_zone = (inhibition >= GOLDEN_LOWER) & (inhibition <= GOLDEN_UPPER)
            distance = jnp.abs(inhibition - GOLDEN_CENTER)
            w = jnp.exp(-distance / 0.1) * in_zone.astype(x.dtype)
            wsum = w.sum(axis=-1, keepdims=True)
            no_expert = wsum < 1e-08
            fb = jnp.exp(-distance / 0.3)
            _, top2 = jax.lax.top_k(fb, 2)
            fb_mask = jax.nn.one_hot(top2, E, dtype=x.dtype).sum(axis=-2)
            fb_w = fb * fb_mask
            fb_w = fb_w / jnp.clip(fb_w.sum(axis=-1, keepdims=True), 1e-08)
            w = jnp.where(no_expert, fb_w, w)
            return w / jnp.clip(w.sum(axis=-1, keepdims=True), 1e-08)
        weights = _router_weights(x, Wr, temperature)
        gate = jnp.einsum('btd,edf->ebtf', x, Wg)
        up = jnp.einsum('btd,edf->ebtf', x, Wu)
        gate = gate.at[:NL].add(jnp.einsum('btd,edr,erf->ebtf', x, Ga, Gb))
        up = up.at[:NL].add(jnp.einsum('btd,edr,erf->ebtf', x, Ua, Ub))
        mid = jax.nn.silu(gate) * up
        out = jnp.einsum('ebtf,efd->ebtd', mid, Wd)
        out = out.at[:NL].add(jnp.einsum('ebtf,efr,erd->ebtd', mid[:NL], Da, Db))
        return jnp.einsum('bte,ebtd->btd', weights, out)

    def _L1_xattn_ref(hidden_q, kv_c, Wq, w_kc_q, w_kc_kv, W_qr, W_kr, Wo):
        import jax, jax.numpy as jnp
        import numpy as np
        B, S, L = (2, 128, 128)
        DIM_Q, H, K, D_C, D_CQ, R = (256, 16, 128, 64, 192, 64)

        def _rope_tables(length, dim):
            inv = 1.0 / 10000.0 ** (jnp.arange(0, dim, 2, dtype=jnp.float32) / dim)
            f = jnp.arange(length, dtype=jnp.float32)[:, None] * inv[None, :]
            sin = jnp.repeat(jnp.sin(f), 2, axis=-1)
            cos = jnp.repeat(jnp.cos(f), 2, axis=-1)
            return (sin, cos)

        def _rotate_half(x):
            half = x.shape[-1] // 2
            return jnp.concatenate([-x[..., half:], x[..., :half]], axis=-1)

        def _apply_rope(x, sin, cos):
            return x * cos + _rotate_half(x) * sin
        Bv, Sv, _ = hidden_q.shape
        _, Lv, _ = kv_c.shape
        q_hk = (hidden_q @ Wq.T).reshape(Bv, Sv, H, K)
        q_big = jnp.einsum('bshk,hkq->bshq', q_hk, w_kc_q)
        sin_q, cos_q = _rope_tables(Sv, D_CQ)
        q_big = _apply_rope(q_big, sin_q[None, :, None, :], cos_q[None, :, None, :])
        sin_k, cos_k = _rope_tables(Lv, D_C)
        kv_r = _apply_rope(kv_c, sin_k[None], cos_k[None])
        q_r = jnp.einsum('bshq,hqr->bhsr', q_big, W_qr)
        k_r = jnp.einsum('bld,hdr->bhlr', kv_r, W_kr)
        scores = jnp.einsum('bhsr,bhlr->bhsl', q_r, k_r)
        attn = jax.nn.softmax(scores, axis=-1)
        ctx_c = jnp.einsum('bhsl,bld->bhsd', attn, kv_r)
        ctx_lat = jnp.einsum('bhsd,hkd->bhsk', ctx_c, w_kc_kv)
        ctx = ctx_lat.transpose(0, 2, 1, 3).reshape(Bv, Sv, H * K)
        return ctx @ Wo.T

    def _L1_attn_ref(hidden_states, W_attn, b_attn, W_proj, b_proj):
        import jax, jax.numpy as jnp
        import numpy as np
        N_HEAD = 32
        HEAD_ID = 0
        MASKED_BIAS = -10000.0
        B, S, E = hidden_states.shape
        H = N_HEAD
        D = E // H
        m = 2.0 ** (-(8.0 / H) * (HEAD_ID + 1))
        qkv = hidden_states @ W_attn + b_attn
        q, k, v = jnp.split(qkv, 3, axis=-1)
        q = q.reshape(B, S, H, D).transpose(0, 2, 1, 3)
        k = k.reshape(B, S, H, D).transpose(0, 2, 1, 3)
        v = v.reshape(B, S, H, D).transpose(0, 2, 1, 3)
        scores = jnp.einsum('bhqd,bhkd->bhqk', q, k) / jnp.sqrt(jnp.float32(D))
        rows = jnp.arange(S)[:, None]
        cols = jnp.arange(S)[None, :]
        causal = cols <= rows
        scores = jnp.where(causal, scores, jnp.float32(MASKED_BIAS))
        alibi = jnp.where(causal, (cols - rows).astype(scores.dtype), 0.0)
        scores = scores + alibi * m
        probs = jax.nn.softmax(scores, axis=-1)
        attn = jnp.einsum('bhqk,bhkd->bhqd', probs, v)
        attn = attn.transpose(0, 2, 1, 3).reshape(B, S, E)
        out = attn @ W_proj + b_proj
        return out

    def _L1_ffn_ref(hidden_states, router_w, w_gate, w_up, w_down):
        import jax, jax.numpy as jnp
        import numpy as np
        B, S, H, E, K, I = (2, 128, 256, 32, 8, 96)
        Bq, Sq, Hd = hidden_states.shape
        x = hidden_states.reshape(-1, Hd)
        logits = x @ router_w.T
        probs = jax.nn.softmax(logits.astype(jnp.float32), axis=-1)
        rw, sel = jax.lax.top_k(probs, K)
        rw = rw / jnp.sum(rw, axis=-1, keepdims=True)
        rw = rw.astype(x.dtype)

        def body(acc, operand):
            e, wg, wu, wd = operand
            w_e = jnp.sum(jnp.where(sel == e, rw, jnp.zeros_like(rw)), axis=-1)
            h = jax.nn.silu(x @ wg) * (x @ wu)
            return (acc + h @ wd * w_e[:, None], None)
        acc0 = jnp.zeros_like(x)
        acc, _ = jax.lax.scan(body, acc0, (jnp.arange(E), w_gate, w_up, w_down))
        return acc.reshape(Bq, Sq, Hd)
    x = x + _L0_xattn_ref(_layernorm(x, axis=-1), ctx_512, L0_xattn_Wq, L0_xattn_Wkv_expand, L0_xattn_Wout)
    x = x + _L0_attn_ref(_layernorm(x, axis=-1), L0_attn_gamma, L0_attn_beta, L0_attn_W_in, L0_attn_W_out, L0_attn_dt)
    x = x + _L0_ffn_ref(_layernorm(x, axis=-1), L0_ffn_Wg, L0_ffn_Wu, L0_ffn_Wd, L0_ffn_Ga, L0_ffn_Gb, L0_ffn_Ua, L0_ffn_Ub, L0_ffn_Da, L0_ffn_Db, L0_ffn_Wr, L0_ffn_temperature)
    x = x + _L1_xattn_ref(_layernorm(x, axis=-1), ctx_512, L1_xattn_Wq, L1_xattn_w_kc_q, L1_xattn_w_kc_kv, L1_xattn_W_qr, L1_xattn_W_kr, L1_xattn_Wo)
    x = x + _L1_attn_ref(_layernorm(x, axis=-1), L1_attn_W_attn, L1_attn_b_attn, L1_attn_W_proj, L1_attn_b_proj)
    x = x + _L1_ffn_ref(_layernorm(x, axis=-1), L1_ffn_router_w, L1_ffn_w_gate, L1_ffn_w_up, L1_ffn_w_down)
    return x

_drawn_inputs = setup_inputs


def setup_inputs(seed=0):
    import zlib

    import numpy as np

    out = dict(_drawn_inputs(seed))
    spreads = {'L0_attn_gamma': (1.0, 0.6),
     'L0_attn_beta': (0.0, 0.8),
     'L1_attn_b_attn': (0.0, 2.0),
     'L1_attn_b_proj': (0.0, 2.0)}
    factors = {'L0_xattn_Wq': 8.0,
     'L0_attn_W_in': 8.0,
     'L0_attn_W_out': 8.0,
     'L0_attn_dt': 8.0,
     'L0_ffn_Wg': 8.0,
     'L0_ffn_Wu': 8.0,
     'L0_ffn_Wd': 8.0,
     'L0_ffn_Ga': 8.0,
     'L0_ffn_Gb': 8.0,
     'L0_ffn_Ua': 8.0,
     'L0_ffn_Ub': 8.0,
     'L0_ffn_Da': 8.0,
     'L0_ffn_Db': 8.0,
     'L0_ffn_Wr': 8.0,
     'L1_xattn_Wq': 8.0,
     'L1_xattn_w_kc_q': 8.0,
     'L1_xattn_w_kc_kv': 7.398,
     'L1_xattn_W_qr': 8.0,
     'L1_xattn_W_kr': 8.0,
     'L1_xattn_Wo': 7.243,
     'L1_ffn_router_w': 5.356,
     'L1_ffn_w_gate': 4.705,
     'L1_ffn_w_up': 4.41,
     'L1_ffn_w_down': 4.468}
    for name, (base, spread) in spreads.items():
        noise = np.random.default_rng([zlib.crc32(name.encode()), seed]).standard_normal(out[name].shape)
        drawn = base * np.exp(spread * noise) if base else spread * noise
        out[name] = jnp.asarray(drawn.astype(out[name].dtype))
    for name, factor in factors.items():
        out[name] = (out[name] * factor).astype(out[name].dtype)
    return out
```

```python
from contextlib import ExitStack
import math

import numpy as np

import concourse.bass as bass
from concourse import mybir

F32 = mybir.dt.float32
F32R = mybir.dt.float32r
ALU = mybir.AluOpType
ACT = mybir.ActivationFunctionType
AX = mybir.AxisListType.X

P = 128
S = 64
D = 256
DC = D // P
EPS = 1e-5
FMAX = float(np.finfo(np.float32).max)

A_HD, A_NH = 16, 16
B_INNER = 512
C_E, C_F, C_R, C_LORA = 8, 256, 64, 2
GOLDEN_CENTER = 1.0 / math.e
GOLDEN_LOWER = 0.5 - math.log(4.0 / 3.0)
GOLDEN_UPPER = 0.5
CTX, L = 6272, 64
NT = CTX // P
X_H, X_K, X_CQ, X_R = 16, 128, 192, 64
X_HALF = X_CQ // 2
E_HD, E_NH = 8, 32
F_E, F_K, F_I = 32, 8, 96

GRP = 2
GH = X_H // GRP
GQ = GH * S
QT = GQ // P
BODY = 7
NPASS = NT // BODY
CHUNK = BODY * P
HALF = CHUNK // 2
HALVES = ((0, 4), (4, BODY))
F_STEPS = F_E // 4
BANK = 512

C_ID, C_CAUS, C_ADDA, C_ADDE, C_PAR, C_BLKA, C_BLKE, C_ROPE, C_ONE, C_NH = (
    0, 128, 192, 256, 320, 322, 330, 346, 602, 666)
C_N = 672


def constants():
    c = np.zeros((P, C_N), np.float32)
    p = np.arange(P)
    row = p % S
    col = np.arange(S)
    seen = col[None, :] <= row[:, None]
    c[:, C_ID:C_ID + P] = np.eye(P)
    c[:, C_CAUS:C_CAUS + S] = seen
    c[:, C_ADDA:C_ADDA + S] = np.where(seen, 0.0, -FMAX)
    slope = 2.0 ** (-(8.0 / E_NH))
    c[:, C_ADDE:C_ADDE + S] = np.where(seen, (col[None, :] - row[:, None]) * slope, -10000.0)
    c[:, C_PAR] = p < S
    c[:, C_PAR + 1] = p >= S
    c[:, C_BLKA:C_BLKA + 8] = (p[:, None] // A_HD) == np.arange(8)[None, :]
    c[:, C_BLKE:C_BLKE + 16] = (p[:, None] // E_HD) == np.arange(16)[None, :]
    sin, cos = rope(S, X_CQ)
    for n, t in enumerate((cos[:, :X_HALF], cos[:, X_HALF:], sin[:, :X_HALF], sin[:, X_HALF:])):
        c[:X_HALF, C_ROPE + n * S:C_ROPE + (n + 1) * S] = t.T
    c[:, C_ONE:C_ONE + S] = 1.0
    c[:, C_NH] = -0.5
    return c


def rope(length, dim, each=2):
    inv = (1.0 / np.float32(10000.0) ** (np.arange(0, dim, 2, dtype=np.float32) / np.float32(dim)))
    f = np.arange(length, dtype=np.float32)[:, None] * inv.astype(np.float32)[None, :]
    return (np.repeat(np.sin(f), each, axis=-1).astype(np.float32),
            np.repeat(np.cos(f), each, axis=-1).astype(np.float32))


SLOT = (0, 1, 2, 0, 1, 2, 1)
SLOT_AGE = (4, 2, 4, 3, 3, 3, 2)
MAX_AFTER = (1, 2, 4, 5)

LOADS = dict(x=1, cst=1, actx=2, awkv=1, awq=1, awo=1, b=3, bw=2, lora=1, cgu=1, cdown=1, ctx=1,
             rope=1, wr=2, wo=2, wq=2, fwr=1, ebias=2, ew=2, fgu=1, fdown=1)


def build(nc, dram, out):
    with ExitStack() as ctx:
        base = -(-nc.sbuf_base // 64) * 64
        width = (nc.sbuf_usable_end - base) // 4 - 16
        ctx.enter_context(nc.sbuf_tensor("arena", [P, width], F32))

        def at(name, col, shape, dtype=F32):
            assert col + math.prod(shape[1:]) <= width, name
            return nc.alloc_sbuf_tensor_at(name, shape, dtype, offset=base + 4 * col)

        R1 = 0
        R2 = 12288
        R3 = 20480
        R4 = 24576
        R5 = 26624
        R6 = 32896
        R7 = 36096
        R8 = 42368
        R9 = 45952
        R10 = 49024
        VEC = R10 + C_N + 3 * D + 2 * P
        WORK = VEC + 512

        l0_gu = at("l0_gu", R1, [P, DC, C_E, 2 * C_F])
        l0_down = at("l0_down", R1 + 8192, [P, DC, C_E, D])
        qhk = at("qhk", R1, [P, X_H, S])
        q_lo = at("q_lo", R1 + 1024, [X_HALF, X_H, S])
        q_hi = at("q_hi", R1 + 2048, [X_HALF, X_H, S])
        q_lo_sin = at("q_lo_sin", R1 + 3072, [X_HALF, X_H, S])
        q_hi_sin = at("q_hi_sin", R1 + 4096, [X_HALF, X_H, S])
        l1_gu = at("l1_gu", R1, [P, DC, F_E, 2 * F_I])
        x_wq = at("x_wq", R2, [P, DC, X_H * X_K])
        x_kcq = at("x_kcq", R2 + 4096, [P, X_H, X_CQ])
        x_kckv = at("x_kckv", R2 + 7168, [P, X_H, L])
        l1_down = at("l1_down", R2, [F_I, F_E, D])
        x_wo = at("x_wo", R3, [P, X_H, D])
        att_a = dict(kbd=at("kbd_a", R4, [P, DC, 8, S]), sc=at("sc_a", R4 + 1024, [P, 8, S]),
                     pt=at("pt_a", R4 + 1536, [P, 4, P]))
        x_qk = at("x_qk", R4, [X_HALF, 2, X_H, L])
        e_w = at("e_w", R4, [P, DC, 3 * D])
        e_wp = at("e_wp", R4 + 1536, [P, DC, D])
        turned = at("turned", R5, [P, NT, L])
        a_wq = at("a_wq", R5 + 3136, [P, DC, D])
        a_wkv = at("a_wkv", R5 + 3648, [L, 2 * D])
        a_wo = at("a_wo", R5 + 4160, [P, DC, D])
        a_ctx = at("a_ctx", R5 + 4672, [L, 2, S])
        dt_row = at("dt_row", R5 + 4800, [P, B_INNER])
        keys = at("keys", R5, [P, CTX], F32R)
        att_e = dict(kbd=at("kbd_e", R5, [P, DC, 16, S]), sc=at("sc_e", R5 + 2048, [P, 16, S]),
                     pt=at("pt_e", R5 + 3072, [P, 8, P]))
        f_mid = at("f_mid", R5 + 4096, [P, 2, 2, F_I])
        f_midT = at("f_midT", R5 + 4480, [F_I, 2, 2, P])
        kv = at("kv", R6, [P, NT, L + 1])
        ctx_sb = at("ctx_sb", R7, [P, NT, L])
        rope_sb = at("rope_sb", R7 + 3136, [P, 2, NT, L // 2])
        probs = at("probs", R7, [P, 3, GQ])
        st_hl = at("st_hl", R7 + 1536, [P, CHUNK], F32R)
        st_h1 = at("st_h1", R7 + 2432, [P, CHUNK], F32R)
        st_kv = at("st_kv", R7 + 3328, [P, BODY, L + 1])
        q_hh = at("q_hh", R7 + 3784, [P, X_H * S], F32R)
        q_lm = at("q_lm", R7 + 4808, [P, X_H * S], F32R)
        x_wqr = at("x_wqr", R8, [P, X_H // 2, X_CQ])
        x_wkr = at("x_wkr", R8 + 1536, [P, X_H // 2, L])
        lora = at("lora", R8 + 2048, [P, 6, D])
        c_mid = at("c_mid", R8, [P, 4, C_F])
        c_midT = at("c_midT", R8 + 1024, [P, 4, 2, P])
        b_win = at("b_win", R9, [P, DC, 2 * B_INNER])
        b_wout = at("b_wout", R9 + 2048, [P, B_INNER // P, D])
        ctx_un = at("ctx_un", R9, [L + 1, GRP, GQ])
        ctx_n = at("ctx_n", R9 + 1024, [L, GRP, GQ])
        den_diag = at("den_diag", R9 + 2048, [P, QT, P])
        key_max = at("key_max", R9 + 2560, [P, QT, NPASS])
        q_max = at("q_max", R9 + 2592, [P, QT])
        den_inv = at("den_inv", R9 + 2600, [P, GRP * QT])
        f_wr = at("f_wr", R9 + 2608, [P, DC, F_E])
        e_bv = at("e_bv", R9 + 2672, [P, D])

        cst = at("cst", R10, [P, C_N])
        res = at("res", R10 + C_N, [S, D])
        nrm = at("nrm", R10 + C_N + D, [S, D])
        nrm2 = at("nrm2", R10 + C_N + 2 * D, [S, D])
        xT = at("xT", R10 + C_N + 3 * D, [P, DC, 2, S])
        vec = at("vec", VEC, [P, 512])
        b_clip = at("b_clip", WORK, [P, 8, S])
        b_sig = at("b_sig", WORK + 512, [P, 8, S])
        b_z = at("b_z", WORK + 1024, [P, 4, S])
        vbd = at("vbd", WORK + 1280, [P, D])
        oT = at("oT", WORK + 1536, [P, P])
        e_bp = at("e_bp", WORK + 1664, [S, D])

        ident = cst[:, C_ID:C_ID + P]
        rope_q = cst[0:X_HALF, C_ROPE:C_ROPE + 4 * S].rearrange("p (n s) -> p n s", n=4)

        used = [0]

        def cols(w, rows=P):
            used[0] += w
            assert used[0] <= 512
            return vec[0:rows, used[0] - w:used[0]]

        stats, mean_var, var_eps, rstd = cols(6, S), cols(2, S), cols(1, S), cols(1, S)
        qT = cols(DC * S).rearrange("p (c s) -> p c s", c=DC)
        row_max, row_sum, row_inv = cols(16), cols(16), cols(16)
        columns = cols(2 * DC + 4 + 2 * DC + DC * C_E)
        gamma, beta, dt_col = columns[:, 0:DC], columns[:, DC:2 * DC], columns[:, 2 * DC:2 * DC + 4]
        e_bias = columns[:, 2 * DC + 4:4 * DC + 4]
        c_wr = columns[:, 4 * DC + 4:].rearrange("p (c e) -> p c e", c=DC)
        dt_e, dt_w = cols(4), cols(4)
        dt_min, dt_sum, dt_inv = cols(1), cols(1), cols(1)
        temp, temp_inv = cols(1), cols(1)
        inh, zone, dist, w_zone, fallback = cols(8), cols(8), cols(8), cols(8), cols(14)
        top, taken, left = cols(8), cols(8), cols(14)
        w_sum, no_expert, w_c = cols(1), cols(1), cols(4)
        f_exp, f_left, w_f = cols(F_E), cols(F_E), cols(F_E // 2)
        f_shift = cols(1)

        ps = ctx.enter_context(nc.psum_tensor("ps", [P, 8 * BANK], F32))

        def bank(b, n=BANK, start=0, rows=slice(0, P)):
            return ps[rows, b * BANK + start:b * BANK + start + n]

        sems = {}

        def ev(name):
            if name not in sems:
                sems[name] = ctx.enter_context(nc.semaphore(name))
            return sems[name]

        def loaded(eng, name):
            eng.wait_ge(ev("ld_" + name), 16 * LOADS[name])

        steps = {"dve": 0}

        def link(eng, ins):
            steps["dve"] += 1
            ins.then_inc(ev("dve_step"), 1)
            eng.wait_ge(ev("dve_step"), steps["dve"])

        att = {
            "a": dict(att_a, hd=A_HD, nh=8, blk=C_BLKA, add=C_ADDA, scale=A_HD ** -0.5, wo=a_wo),
            "e": dict(att_e, hd=E_HD, nh=16, blk=C_BLKE, add=C_ADDE,
                      scale=float(np.float32(1.0) / np.sqrt(np.float32(E_HD))), wo=e_wp),
        }

        block = ctx.enter_context(nc.Block())

        @block.sync
        def _(sp):
            def load(name, dst, src):
                sp.dma_start(dst, src).then_inc(ev("ld_" + name), 16)

            load("x", res[:, :], dram["x"])
            load("cst", cst[:, :], dram["cst"])
            load("actx", a_ctx[:, 0, :], dram["ctx_t"])
            load("actx", a_ctx[:, 1, :], dram["ctx_t"])
            load("awkv", a_wkv[:, :], dram["a_wkv"])
            load("awq", a_wq[:, :, :], dram["a_wq"])
            load("b", dt_row[:, :], dram["dt"].partition_broadcast(P))
            load("b", columns, dram["columns"])
            load("b", temp, dram["temp"].partition_broadcast(P))
            load("awo", a_wo[:, :, :], dram["a_wo"])
            load("bw", b_win[:, :, :], dram["b_win"])
            load("bw", b_wout[:, :, :], dram["b_wout"])
            load("lora", lora[:, :, :], dram["lora"])
            load("cgu", l0_gu[:, :, :, :], dram["c_gu"])
            load("cdown", l0_down[:, :, :, :], dram["c_down"])
            load("ctx", ctx_sb[:, :, :], dram["ctx"])
            load("rope", rope_sb[:, :, :, :], dram["rope"])
            load("wr", x_wqr[:, :, :], dram["x_wqr"])
            load("wr", x_wkr[:, :, :], dram["x_wkr"])
            load("wo", x_kckv[:, :, :], dram["x_kckv"])
            load("wo", x_wo[:, :, :], dram["x_wo"])
            load("wq", x_wq[:, :, :], dram["x_wq"])
            load("wq", x_kcq[:, :, :], dram["x_kcq"])
            sp.wait_ge(ev("b_done"), 1)
            load("fwr", f_wr[:, :, :], dram["f_wr"])
            load("ebias", e_bv[:, :], dram["e_b"][2 * D:3 * D].partition_broadcast(P))
            load("ebias", e_bp[:, :], dram["e_bp"].partition_broadcast(S))
            sp.wait_ge(ev("q_low"), GRP)
            load("ew", e_w[:, :, :], dram["e_w"])
            load("ew", e_wp[:, :, :], dram["e_wp"])
            load("fgu", l1_gu[:, :, :, :], dram["f_gu"])
            load("fdown", l1_down[:, :, :], dram["f_down"])
            sp.wait_ge(ev("result"), 1)
            sp.dma_start(out, res[:, :]).then_inc(ev("stored"), 16)
            sp.wait_ge(ev("stored"), 16)

        @block.gpsimd
        def _(pool):
            def norm_scale(t):
                pool.wait_ge(ev(t + "_var"), 1)
                pool.tensor_tensor(rstd, var_eps, cst[0:S, C_NH:C_NH + 1], ALU.pow).then_inc(ev(t + "_rstd"), 1)

            loaded(pool, "cst")
            norm_scale("a")
            norm_scale("b")
            norm_scale("b2")
            norm_scale("c")
            loaded(pool, "ctx")
            loaded(pool, "rope")
            pool.memset(kv[:, :, L:L + 1], 1.0).then_inc(ev("kv_ones"), 1)
            half = L // 2
            pairs = ctx_sb[:, :, :].rearrange("p t (f e) -> p t f e", e=2)
            sin, cos = rope_sb[:, 0, :, :], rope_sb[:, 1, :, :]
            pool.tensor_tensor(kv[:, :, 0:L].rearrange("p t (f e) -> p t f e", e=2), pairs,
                               cos.unsqueeze(3).broadcast_to([P, NT, half, 2]), ALU.mult).then_inc(ev("rope_cos"), 1)
            for a, b in ((0, half), (half, 0)):
                pool.tensor_tensor(
                    turned[:, :, a:a + half].rearrange("p t (f e) -> p t f e", e=2),
                    ctx_sb[:, :, b:b + half].rearrange("p t (f e) -> p t f e", e=2),
                    sin[:, :, a // 2:a // 2 + half // 2].unsqueeze(3).broadcast_to([P, NT, half // 2, 2]),
                    ALU.mult).then_inc(ev("rope_sin"), 1)
            pool.wait_ge(ev("rope_cos"), 1)
            pool.wait_ge(ev("rope_sin"), 2)
            pool.tensor_tensor(kv[:, :, 0:half], kv[:, :, 0:half], turned[:, :, 0:half],
                               ALU.subtract).then_inc(ev("roped"), 1)
            pool.tensor_tensor(kv[:, :, half:L], kv[:, :, half:L], turned[:, :, half:L],
                               ALU.add).then_inc(ev("roped"), 1)
            norm_scale("d")
            norm_scale("e")
            norm_scale("f")

        @block.scalar
        def _(act):
            def softmax_exp(t):
                sc = att[t]["sc"]
                act.wait_ge(ev(t + "_shifted"), 1)
                act.activation(sc[:, :, :], sc[:, :, :], ACT.Exp).then_inc(ev(t + "_exp"), 1)

            def probs_turned(t):
                pairs = att[t]["nh"] // 2
                act.wait_ge(ev(t + "_probsT_psum"), 1)
                act.activation(att[t]["pt"][:, :, :], bank(6, pairs * P).rearrange("p (j q) -> p j q", j=pairs),
                               ACT.Copy).then_inc(ev(t + "_probsT"), 1)

            act.wait_ge(ev("dt_min"), 1)
            act.activation(dt_e, dt_col, ACT.Exp, bias=dt_min, scale=-1.0).then_inc(ev("dt_exp"), 1)
            act.activation(dt_row[:, :], dt_row[:, :], ACT.Exp, bias=dt_min, scale=-1.0,
                           accum_out=dt_sum).then_inc(ev("dt_exp"), 1)
            softmax_exp("a")
            act.preload_act_table(ACT.Sigmoid)
            probs_turned("a")

            act.wait_ge(ev("b_clipped"), 1)
            act.activation(b_sig[:, :, :], b_clip[:, :, :], ACT.Sigmoid).then_inc(ev("b_sigmoid"), 1)

            act.wait_ge(ev("c_logits"), 1)
            act.wait_ge(ev("temp_inv"), 1)
            act.activation(inh, bank(1, C_E), ACT.Sigmoid, scale=temp_inv).then_inc(ev("c_inh"), 1)
            act.preload_act_table(ACT.Exp)
            for n in range(4):
                act.wait_ge(ev("qk_fold_psum"), n + 1)
                act.activation(x_qk[:, n // 2, 8 * (n % 2):8 * (n % 2) + 8, :],
                               bank(2 + n, rows=slice(0, X_HALF)).rearrange("p (h d) -> p h d", h=8),
                               ACT.Copy).then_inc(ev("qk_fold"), 1)
            act.wait_ge(ev("c_dist"), 1)
            act.activation(w_zone, dist, ACT.Exp, scale=-1.0 / 0.1).then_inc(ev("c_exp"), 1)
            act.activation(fallback[:, 0:C_E], dist, ACT.Exp, scale=-1.0 / 0.3).then_inc(ev("c_exp"), 1)
            act.preload_act_table(ACT.Silu)
            act.wait_ge(ev("qk_fold_psum"), 4)
            act.wait_ge(ev("lora_psum"), 8)
            for j in range(C_E // 2):
                act.wait_ge(ev("c_gu"), j + 1)
                act.activation(c_mid[:, j, :], bank(2 + j, C_F), ACT.Silu).then_inc(ev("c_silu"), 1)
            act.preload_act_table(ACT.Exp)
            for n in range(2):
                act.wait_ge(ev("c_midT_psum"), n + 1)
                act.activation(c_midT[:, 2 * n:2 * n + 2, :, :],
                               bank(6 + n).rearrange("p (j f q) -> p j f q", j=2, f=2),
                               ACT.Copy).then_inc(ev("c_midT"), 1)

            for n in range(X_H // 2):
                act.wait_ge(ev("wo_fold_psum"), n + 1)
                act.activation(x_wo[0:L, 2 * n:2 * n + 2, :],
                               bank(4 + n % 2, rows=slice(0, L)).rearrange("p (h d) -> p h d", h=2),
                               ACT.Copy).then_inc(ev("wo_fold"), 1)
            for n in range(-(-NT // 4)):
                w = min(4, NT - 4 * n) * P
                act.wait_ge(ev("keysT"), n + 1)
                act.activation(keys[0:L, n * BANK:n * BANK + w], bank(6 + n % 2, w, rows=slice(0, L)),
                               ACT.Copy).then_inc(ev("keys_high"), 1)

            for n in range(2):
                act.wait_ge(ev("qhk_psum"), n + 1)
                act.activation(qhk[:, 8 * n:8 * n + 8, :], bank(1 + n).rearrange("p (h s) -> p h s", h=8),
                               ACT.Copy).then_inc(ev("qhk"), 1)
            for g in range(GRP):
                q, at_q = bank(1 + g, GQ, rows=slice(0, L)), slice(g * GQ, (g + 1) * GQ)
                act.wait_ge(ev("q_psum"), g + 1)
                act.activation(q_hh[0:L, at_q], q, ACT.Copy).then_inc(ev("q_high"), 1)
                act.activation(q_hh[L:2 * L, at_q], q, ACT.Copy).then_inc(ev("q_high"), 1)

            for g in range(GRP):
                def exps(i):
                    for j in range(BODY):
                        t = i * BODY + (g * NT + j)
                        act.wait_ge(ev("scores"), t + 1)
                        if not (isinstance(t, int) and t < SLOT_AGE[j]):
                            act.wait_ge(ev("weighted"), t + (1 - SLOT_AGE[j]))
                        act.activation(probs[:, SLOT[j], :], bank(1 + SLOT[j], GQ),
                                       ACT.Exp).then_inc(ev("probs"), 1)

                exps(0)
                with act.Fori(1, NPASS) as i:
                    exps(i)
                act.wait_ge(ev("weighted"), (g + 1) * NT)
                act.activation(ctx_un[:, g, :], bank(4 * g, GQ, rows=slice(0, L + 1)),
                               ACT.Copy).then_inc(ev("ctx_un"), 1)

            softmax_exp("e")
            probs_turned("e")

            act.wait_ge(ev("f_shift"), 1)
            act.activation(f_exp, bank(1, F_E), ACT.Exp, bias=f_shift).then_inc(ev("f_exp"), 1)
            act.preload_act_table(ACT.Silu)

            for u in range(F_STEPS):
                b = u % 2
                act.wait_ge(ev("f_gu"), u + 1)
                if u >= 2:
                    act.wait_ge(ev("f_midT_psum"), u - 1)
                gates = bank(2 + b, 4 * F_I).rearrange("p (j g f) -> p j g f", j=2, g=2)[:, :, 0, :]
                act.activation(f_mid[:, b, :, :], gates, ACT.Silu).then_inc(ev("f_silu"), 1)

        @block.vector
        def _(dve):
            def norm(t, src, dst):
                link(dve, dve.bn_stats(stats, src))
                link(dve, dve.bn_aggr(mean_var, stats))
                dve.tensor_scalar(var_eps, mean_var[:, 1:2], EPS, None, ALU.add).then_inc(ev(t + "_var"), 1)
                dve.wait_ge(ev(t + "_rstd"), 1)
                dve.tensor_scalar(dst, src, mean_var[:, 0:1], rstd, ALU.subtract,
                                  ALU.mult).then_inc(ev(t + "_norm"), 1)

            def turned_twice(t):
                dve.wait_ge(ev(t + "_xT_psum"), 1)
                src = bank(0, 2 * S).rearrange("p (c s) -> p c s", c=DC).unsqueeze(2)
                dve.tensor_copy(xT[:, :, :, :], src.broadcast_to([P, DC, 2, S])).then_inc(ev(t + "_xT"), 1)

            def head_blocks(t):
                a = att[t]
                nh, hd, kbd = a["nh"], a["hd"], a["kbd"]
                blk = cst[:, a["blk"]:a["blk"] + nh].unsqueeze(2).broadcast_to([P, nh, S])
                dve.wait_ge(ev(t + "_k_psum"), 1)
                for c in range(DC):
                    k = bank(1, S, c * S).unsqueeze(1).broadcast_to([P, nh, S])
                    if t == "e":
                        ins = dve.scalar_tensor_tensor(kbd[:, c, :, :], k, e_bias[:, DC + c:DC + c + 1], blk,
                                                       ALU.add, ALU.mult)
                    else:
                        ins = dve.tensor_tensor(kbd[:, c, :, :], k, blk, ALU.mult)
                    ins.then_inc(ev(t + "_kbd"), 1)
                par = cst[:, C_PAR:C_PAR + 2].unsqueeze(1).unsqueeze(3).broadcast_to([P, nh, 2, hd])
                split = "p (j e d) -> p j e d"
                dve.wait_ge(ev(t + "_v_psum"), 1)
                v = bank(2, D)
                if t == "e":
                    link(dve, dve.tensor_tensor(vbd[:, :], v, e_bv[:, :], ALU.add))
                    v = vbd[:, :]
                dve.tensor_tensor(vbd[:, :].rearrange(split, e=2, d=hd), v.rearrange(split, e=2, d=hd), par,
                                  ALU.mult).then_inc(ev(t + "_vbd"), 1)

            def queries(t):
                dve.wait_ge(ev(t + "_q_psum"), 1)
                if t == "e":
                    for c in range(DC):
                        dve.tensor_scalar(qT[:, c, :], bank(3, S, c * S), e_bias[:, c:c + 1], None,
                                          ALU.add).then_inc(ev(t + "_q"), 1)
                else:
                    dve.tensor_copy(qT, bank(3, DC * S).rearrange("p (c s) -> p c s", c=DC)).then_inc(ev(t + "_q"), 1)

            def softmax(t):
                a = att[t]
                nh, sc, hd = a["nh"], a["sc"], a["hd"]
                n = nh * S

                def mask(col):
                    return cst[:, col:col + S].unsqueeze(1).broadcast_to([P, nh, S])

                def each(v):
                    return v[:, 0:nh].unsqueeze(2).broadcast_to([P, nh, S])

                dve.wait_ge(ev(t + "_scores"), DC)
                link(dve, dve.scalar_tensor_tensor(sc[:, :, :], ps[:, 4 * BANK:4 * BANK + n].rearrange(
                    "p (h k) -> p h k", h=nh), a["scale"], mask(C_CAUS), ALU.mult, ALU.mult))
                link(dve, dve.tensor_tensor(sc[:, :, :], sc[:, :, :], mask(a["add"]), ALU.add))
                link(dve, dve.tensor_reduce(row_max[:, 0:nh], sc[:, :, :], AX, ALU.max))
                dve.tensor_tensor(sc[:, :, :], sc[:, :, :], each(row_max),
                                  ALU.subtract).then_inc(ev(t + "_shifted"), 1)
                dve.wait_ge(ev(t + "_exp"), 1)
                link(dve, dve.tensor_reduce(row_sum[:, 0:nh], sc[:, :, :], AX, ALU.add))
                link(dve, dve.reciprocal(row_inv[:, 0:nh], row_sum[:, 0:nh]))
                dve.wait_ge(ev(t + "_o_psum"), 1)
                dve.tensor_tensor(oT[:, :].rearrange("p (h d) -> p h d", h=nh),
                                  bank(0, P).rearrange("p (h d) -> p h d", h=nh),
                                  row_inv[:, 0:nh].unsqueeze(2).broadcast_to([P, nh, hd]),
                                  ALU.mult).then_inc(ev(t + "_o"), 1)
                dve.wait_ge(ev(t + "_oT_psum"), 1)
                dve.tensor_copy(oT[:, :], bank(1, P)).then_inc(ev(t + "_oT"), 1)

            def add_halves(done, count, b, last):
                dve.wait_ge(ev(done), count)
                link(dve, dve.tensor_tensor(res[:, :], bank(b, D, rows=slice(0, S)), res[:, :], ALU.add))
                ins = dve.tensor_tensor(res[:, :], bank(b, D, rows=slice(S, 2 * S)), res[:, :], ALU.add)
                if last:
                    ins.then_inc(ev("result"), 1)
                else:
                    link(dve, ins)

            loaded(dve, "x")
            norm("a", res[:, :], nrm[:, :])
            loaded(dve, "cst")
            head_blocks("a")
            turned_twice("a")
            queries("a")
            loaded(dve, "b")
            dve.tensor_reduce(dt_min, dt_row[:, :], AX, ALU.min).then_inc(ev("dt_min"), 1)
            dve.reciprocal(temp_inv, temp).then_inc(ev("temp_inv"), 1)
            softmax("a")
            dve.wait_ge(ev("dt_exp"), 2)
            link(dve, dve.reciprocal(dt_inv, dt_sum))
            link(dve, dve.tensor_scalar(dt_w, dt_e, dt_inv, None, ALU.mult))
            dve.wait_ge(ev("a_out"), 1)
            link(dve, dve.tensor_tensor(res[:, :], bank(2, D, rows=slice(0, S)), res[:, :], ALU.add))

            norm("b", res[:, :], nrm[:, :])
            dve.wait_ge(ev("b_norm"), 1)
            norm("b2", nrm[:, :], nrm2[:, :])
            link(dve, dve.tensor_tensor(res[:, :], res[:, :], nrm[:, :], ALU.add))
            dve.wait_ge(ev("b_xT_psum"), 1)
            for c in range(DC):
                dve.tensor_scalar(xT[:, c, 0, :], bank(0, S, c * S), gamma[:, c:c + 1], beta[:, c:c + 1],
                                  ALU.mult, ALU.add).then_inc(ev("b_xT"), 1)
            proj = bank(1, 8 * S).rearrange("p (c s) -> p c s", c=8)
            dve.wait_ge(ev("b_proj"), 1)
            dve.tensor_scalar(b_clip[:, :, :], proj, -15.0, 15.0, ALU.max, ALU.min).then_inc(ev("b_clipped"), 1)
            link(dve, dve.tensor_tensor(b_z[:, :, :], proj[:, 0:4, :],
                                        dt_w.unsqueeze(2).broadcast_to([P, 4, S]), ALU.mult))
            dve.wait_ge(ev("b_clipped"), 1)
            link(dve, dve.tensor_tensor(b_z[:, :, :], b_z[:, :, :], b_clip[:, 4:8, :], ALU.mult))
            dve.wait_ge(ev("b_sigmoid"), 1)
            link(dve, dve.tensor_tensor(b_z[:, :, :], b_z[:, :, :], b_sig[:, 0:4, :], ALU.mult))
            dve.tensor_tensor(b_z[:, :, :], b_z[:, :, :], b_sig[:, 4:8, :], ALU.mult).then_inc(ev("b_gated"), 1)
            dve.wait_ge(ev("b_out"), 1)
            ins = dve.tensor_tensor(res[:, :], bank(0, D, rows=slice(0, S)), res[:, :], ALU.add)
            ins.then_inc(ev("b_done"), 1)
            dve.wait_ge(ev("b_done"), 1)

            norm("c", res[:, :], nrm[:, :])
            turned_twice("c")
            loaded(dve, "cgu")
            loaded(dve, "cdown")
            for e in range(C_LORA):
                for d in range(DC):
                    dve.wait_ge(ev("lora_psum"), 1 + e * DC + d)
                    dve.tensor_tensor(l0_gu[:, d, e, :], bank(2 + e * DC + d), l0_gu[:, d, e, :],
                                      ALU.add).then_inc(ev("lora_in"), 1)
            for e in range(C_LORA):
                for d in range(DC):
                    dve.wait_ge(ev("lora_psum"), 5 + e * DC + d)
                    dve.tensor_tensor(l0_down[:, d, e, :], bank(6 + e, D, d * D), l0_down[:, d, e, :],
                                      ALU.add).then_inc(ev("lora_in"), 1)
            dve.wait_ge(ev("c_inh"), 1)
            dve.tensor_scalar(zone, inh, GOLDEN_LOWER, None, ALU.is_ge).then_inc(ev("c_zone"), 1)
            link(dve, dve.tensor_scalar(dist, inh, GOLDEN_CENTER, None, ALU.subtract))
            dve.scalar_tensor_tensor(dist, dist, -1.0, dist, ALU.mult, ALU.max).then_inc(ev("c_dist"), 1)
            dve.wait_ge(ev("c_zone"), 1)
            link(dve, dve.scalar_tensor_tensor(zone, inh, GOLDEN_UPPER, zone, ALU.is_le, ALU.mult))
            link(dve, dve.memset(fallback[:, C_E:14], -1.0))
            link(dve, dve.memset(taken, -1.0))
            dve.wait_ge(ev("c_exp"), 2)
            link(dve, dve.scalar_tensor_tensor(w_zone, w_zone, 1.0, zone, ALU.mult, ALU.mult, accum_out=w_sum))
            link(dve, dve.max(top, fallback))
            link(dve, dve.tensor_scalar(no_expert, w_sum, 1e-8, None, ALU.is_lt))
            link(dve, dve.tensor_copy(taken[:, 0:2], top[:, 0:2]))
            link(dve, dve.match_replace(left, taken, fallback, -2.0))
            link(dve, dve.scalar_tensor_tensor(left[:, 0:C_E], left[:, 0:C_E], -1.5, fallback[:, 0:C_E],
                                               ALU.is_lt, ALU.mult, accum_out=w_sum))
            link(dve, dve.tensor_scalar(w_sum, w_sum, 1e-8, None, ALU.max))
            link(dve, dve.reciprocal(w_sum, w_sum))
            link(dve, dve.tensor_scalar(left[:, 0:C_E], left[:, 0:C_E], w_sum, no_expert, ALU.mult, ALU.mult))
            link(dve, dve.tensor_scalar(no_expert, no_expert, -1.0, 1.0, ALU.mult, ALU.add))
            link(dve, dve.scalar_tensor_tensor(w_zone, w_zone, no_expert, left[:, 0:C_E], ALU.mult, ALU.add,
                                               accum_out=w_sum))
            link(dve, dve.tensor_scalar(w_sum, w_sum, 1e-8, None, ALU.max))
            link(dve, dve.reciprocal(w_sum, w_sum))
            for half in range(2):
                r = slice(half * S, half * S + S)
                link(dve, dve.tensor_scalar(w_c[r, :], w_zone.rearrange("p (j e) -> p e j", e=2)[r, half, :], w_sum[r, :], None, ALU.mult))
            for j in range(C_E // 2):
                dve.wait_ge(ev("c_silu"), j + 1)
                dve.scalar_tensor_tensor(c_mid[:, j, :], c_mid[:, j, :], w_c[:, j:j + 1], bank(2 + j, C_F, C_F),
                                         ALU.mult, ALU.mult).then_inc(ev("c_mid"), 1)
            add_halves("c_sum", 1, 0, False)

            norm("d", res[:, :], nrm[:, :])
            for n in range(-(-NT // 4)):
                w = min(4, NT - 4 * n) * P
                dve.wait_ge(ev("keys_high"), n + 1)
                dve.tensor_tensor(keys[L:2 * L, n * BANK:n * BANK + w], bank(6 + n % 2, w, rows=slice(0, L)),
                                  keys[0:L, n * BANK:n * BANK + w].bitcast(F32),
                                  ALU.subtract).then_inc(ev("keys_low"), 1)
            turned_twice("d")
            for n in range(2):
                hs = slice(8 * n, 8 * n + 8)

                def tab(k):
                    return rope_q[:, k, :].unsqueeze(1).broadcast_to([X_HALF, 8, S])

                lo, hi = (bank(b + n, rows=slice(0, X_HALF)).rearrange("p (h s) -> p h s", h=8) for b in (3, 5))
                dve.wait_ge(ev("qbig_psum"), n + 1)
                dve.tensor_tensor(q_lo[:, hs, :], lo, tab(0), ALU.mult).then_inc(ev("q_rot"), 1)
                dve.tensor_tensor(q_hi[:, hs, :], hi, tab(1), ALU.mult).then_inc(ev("q_rot"), 1)
                dve.tensor_tensor(q_hi_sin[:, hs, :], hi, tab(2), ALU.mult).then_inc(ev("q_rot"), 1)
                dve.tensor_tensor(q_lo_sin[:, hs, :], lo, tab(3), ALU.mult).then_inc(ev("q_rot"), 1)
                dve.wait_ge(ev("q_rot"), 4 * (n + 1))
                dve.tensor_tensor(q_lo[:, hs, :], q_lo[:, hs, :], q_hi_sin[:, hs, :],
                                  ALU.subtract).then_inc(ev("q_roped"), 1)
                dve.tensor_tensor(q_hi[:, hs, :], q_hi[:, hs, :], q_lo_sin[:, hs, :],
                                  ALU.add).then_inc(ev("q_roped"), 1)
            for g in range(GRP):
                at_q = slice(g * GQ, (g + 1) * GQ)
                dve.wait_ge(ev("q_high"), 2 * (g + 1))
                dve.tensor_tensor(q_lm[0:L, at_q], bank(1 + g, GQ, rows=slice(0, L)),
                                  q_hh[0:L, at_q].bitcast(F32), ALU.subtract).then_inc(ev("q_low"), 1)
            dve.memset(st_h1[L:L + 1, :].bitcast(F32), 1.0).then_inc(ev("st_ones"), 1)

            def stage(g, i, half):
                a, b = HALVES[half]
                src = bass.ds(i * CHUNK + a * P, (b - a) * P) if not isinstance(i, int) else \
                    slice(i * CHUNK + a * P, i * CHUNK + b * P)
                kv_src = bass.ds(i * BODY + a, b - a) if not isinstance(i, int) else \
                    slice(i * BODY + a, i * BODY + b)
                free = i * BODY + (g * NT - (BODY - b))
                if not isinstance(free, int) or free > 0:
                    dve.wait_ge(ev("weighted"), free)
                dve.tensor_copy(st_hl[:, a * P:b * P], keys[:, src].bitcast(F32)).then_inc(ev("staged"), 1)
                dve.tensor_copy(st_h1[0:L, a * P:b * P], keys[0:L, src].bitcast(F32)).then_inc(ev("staged"), 1)
                dve.tensor_copy(st_kv[:, a:b, :], kv[:, kv_src, :]).then_inc(ev("staged"), 1)

            def maximum(g, i, j):
                n = i * QT + (g * QT * NPASS + j)
                two = ps[:, (4 + 2 * (j % 2)) * BANK:(6 + 2 * (j % 2)) * BANK].rearrange("p (b k) -> p b k", b=2)
                dst = key_max[:, j, bass.ds(i, 1)] if not isinstance(i, int) else key_max[:, j, i:i + 1]
                dve.wait_ge(ev("max_scores"), n + 1)
                dve.tensor_reduce(dst, two[:, :, 0:HALF], mybir.AxisListType.XY, ALU.max).then_inc(ev("key_max"), 1)

            def shift(g):
                dve.wait_ge(ev("key_max"), (g + 1) * QT * NPASS)
                dve.tensor_reduce(q_max[:, :], key_max[:, :, :], AX, ALU.max).then_inc(ev("q_max"), 1)
                dve.wait_ge(ev("q_max_row"), g + 1)
                dve.tensor_scalar(q_lm[L:L + 1, g * GQ:(g + 1) * GQ], bank(5, GQ, rows=slice(L, L + 1)), -1.0,
                                  None, ALU.mult).then_inc(ev("q_shift"), 1)

            dve.wait_ge(ev("kv_ones"), 1)
            dve.wait_ge(ev("roped"), 2)
            for j in range(QT):
                maximum(0, 0, j)
            with dve.Fori(1, NPASS) as i:
                for j in range(QT):
                    maximum(0, i, j)
            stage(0, 0, 0)
            shift(0)
            for g in range(GRP):
                def turn(i):
                    stage(g, i, 1)
                    for j in range(QT):
                        if j == QT - 1 and not (isinstance(i, int) and i == NPASS - 1):
                            stage(g, i + 1, 0)
                        if g + 1 < GRP:
                            maximum(g + 1, i, j)

                turn(0)
                with dve.Fori(1, NPASS - 1) as i:
                    turn(i)
                turn(NPASS - 1)
                if g + 1 < GRP:
                    stage(g + 1, 0, 0)
                    shift(g + 1)

            dve.wait_ge(ev("den_psum"), 1)
            link(dve, dve.reciprocal(den_inv[:, :], bank(5, GRP * QT)))
            for g in range(GRP):
                if g:
                    dve.wait_ge(ev("den_row"), g)
                dve.tensor_tensor(den_diag[:, :, :], ident.unsqueeze(1).broadcast_to([P, QT, P]),
                                  den_inv[:, g * QT:(g + 1) * QT].unsqueeze(2).broadcast_to([P, QT, P]),
                                  ALU.mult).then_inc(ev("den_diag"), 1)
            for g in range(GRP):
                dve.wait_ge(ev("den_row"), g + 1)
                dve.tensor_tensor(ctx_n[:, g, :], bank(2 + g, GQ, rows=slice(0, L)), ctx_un[0:L, g, :],
                                  ALU.mult).then_inc(ev("ctx_n"), 1)
            add_halves("d_sum", 1, 7, False)

            norm("e", res[:, :], nrm[:, :])
            loaded(dve, "ebias")
            link(dve, dve.tensor_tensor(res[:, :], res[:, :], e_bp[:, :], ALU.add))
            turned_twice("e")
            queries("e")
            head_blocks("e")
            softmax("e")
            dve.wait_ge(ev("e_out"), 1)
            link(dve, dve.tensor_tensor(res[:, :], bank(2, D, rows=slice(0, S)), res[:, :], ALU.add))

            norm("f", res[:, :], nrm[:, :])
            turned_twice("f")
            dve.wait_ge(ev("f_logits"), 1)
            link(dve, dve.tensor_reduce(f_shift, bank(1, F_E), AX, ALU.max))
            dve.tensor_scalar(f_shift, f_shift, -1.0, None, ALU.mult).then_inc(ev("f_shift"), 1)
            dve.wait_ge(ev("f_exp"), 1)
            link(dve, dve.max(top, f_exp))
            link(dve, dve.match_replace(f_left, top, f_exp, -1.0))
            link(dve, dve.scalar_tensor_tensor(f_left, f_left, 0.0, f_exp, ALU.is_lt, ALU.mult, accum_out=w_sum))
            link(dve, dve.reciprocal(w_sum, w_sum))
            for half in range(2):
                r = slice(half * S, half * S + S)
                link(dve, dve.tensor_scalar(w_f[r, :], f_left.rearrange("p (j e) -> p e j", e=2)[r, half, :], w_sum[r, :], None, ALU.mult))

            for u in range(F_STEPS):
                b = u % 2
                dve.wait_ge(ev("f_silu"), u + 1)
                for j in range(2):
                    dve.scalar_tensor_tensor(f_mid[:, b, j, :], f_mid[:, b, j, :], w_f[:, 2 * u + j:2 * u + j + 1],
                                             bank(2 + b, F_I, (2 * j + 1) * F_I), ALU.mult,
                                             ALU.mult).then_inc(ev("f_mid"), 1)
                dve.wait_ge(ev("f_midT_psum"), u + 1)
                if u >= 2:
                    dve.wait_ge(ev("f_down"), u - 1)
                dve.tensor_copy(f_midT[:, b, :, :], bank(6 + b, 2 * P, rows=slice(0, F_I)).rearrange(
                    "p (j q) -> p j q", j=2)).then_inc(ev("f_midT"), 1)
            add_halves("f_down", F_STEPS, 0, True)

        @block.tensor
        def _(pe):
            def turn_x(t, src, event):
                pe.wait_ge(ev(event), 1)
                for c in range(DC):
                    ins = pe.transpose(bank(0, S, c * S), src[:, c * P:(c + 1) * P], ident[0:S, 0:S])
                ins.then_inc(ev(t + "_xT_psum"), 1)

            def small_attention(t):
                a = att[t]
                nh, hd, pt = a["nh"], a["hd"], a["pt"]
                pairs = nh // 2
                pe.wait_ge(ev(t + "_q"), DC if t == "e" else 1)
                for c in range(DC):
                    pe.wait_ge(ev(t + "_kbd"), c + 1)
                    kc = a["kbd"][:, c, :, :].rearrange("p h k -> p (h k)")
                    for k in range(nh * S // BANK):
                        ins = pe.matmul(bank(4 + k, rows=slice(c * S, c * S + S)), qT[:, c, :],
                                        kc[:, k * BANK:(k + 1) * BANK], start=True, stop=True)
                    ins.then_inc(ev(t + "_scores"), 1)
                pe.wait_ge(ev(t + "_exp"), 1)
                sc = a["sc"][:, :, :].rearrange("p h k -> p (h k)")
                for j in range(pairs):
                    ins = pe.transpose(bank(6, P, j * P), sc[:, j * P:(j + 1) * P], ident)
                ins.then_inc(ev(t + "_probsT_psum"), 1)
                pe.wait_ge(ev(t + "_probsT"), 1)
                pe.wait_ge(ev(t + "_vbd"), 1)
                w = 2 * hd
                for j in range(pairs):
                    for c in range(DC):
                        ins = pe.matmul(bank(0, w, j * w, rows=slice(c * S, c * S + S)), pt[:, j, c * S:c * S + S],
                                        vbd[:, c * P + j * w:c * P + (j + 1) * w], start=True, stop=True)
                ins.then_inc(ev(t + "_o_psum"), 1)
                pe.wait_ge(ev(t + "_o"), 1)
                pe.transpose(bank(1, P), oT[:, :], ident).then_inc(ev(t + "_oT_psum"), 1)
                pe.wait_ge(ev(t + "_oT"), 1)
                if t == "a":
                    loaded(pe, "awo")
                for c in range(DC):
                    ins = pe.matmul(bank(2, D, rows=slice(0, S)), oT[:, c * S:(c + 1) * S], a["wo"][:, c, :],
                                    start=(c == 0), stop=(c == DC - 1))
                ins.then_inc(ev(t + "_out"), 1)

            loaded(pe, "actx")
            loaded(pe, "awkv")
            for c in range(DC):
                ins = pe.matmul(bank(1, S, c * S), a_wkv[:, c * P:(c + 1) * P], a_ctx[:, 0, :],
                                start=True, stop=True)
            ins.then_inc(ev("a_k_psum"), 1)
            pe.matmul(bank(2, D), a_ctx[:, :, :].rearrange("p e s -> p (e s)"), a_wkv[:, D:2 * D],
                      start=True, stop=True).then_inc(ev("a_v_psum"), 1)
            loaded(pe, "cst")
            turn_x("a", nrm, "a_norm")
            loaded(pe, "awq")
            pe.wait_ge(ev("a_xT"), 1)
            for c in range(DC):
                for d in range(DC):
                    ins = pe.matmul(bank(3, S, c * S), a_wq[:, d, c * P:(c + 1) * P], xT[:, d, 0, :],
                                    start=(d == 0), stop=(d == DC - 1))
            ins.then_inc(ev("a_q_psum"), 1)
            small_attention("a")

            turn_x("b", nrm2, "b2_norm")
            loaded(pe, "bw")
            pe.wait_ge(ev("b_xT"), DC)
            for e in range(2 * B_INNER // P):
                for d in range(DC):
                    ins = pe.matmul(bank(1, S, e * S), b_win[:, d, e * P:(e + 1) * P], xT[:, d, 0, :],
                                    start=(d == 0), stop=(d == DC - 1))
            ins.then_inc(ev("b_proj"), 1)
            pe.wait_ge(ev("b_gated"), 1)
            for e in range(B_INNER // P):
                ins = pe.matmul(bank(0, D, rows=slice(0, S)), b_z[:, e, :], b_wout[:, e, :],
                                start=(e == 0), stop=(e == B_INNER // P - 1))
            ins.then_inc(ev("b_out"), 1)

            loaded(pe, "lora")
            for e in range(C_LORA):
                r = slice(e * C_R, (e + 1) * C_R)
                for d in range(DC):
                    for k in range(2):
                        ins = pe.matmul(bank(2 + e * DC + d, C_F, k * C_F),
                                        lora[r, 2 * k, d * P:(d + 1) * P], lora[r, 2 * k + 1, :],
                                        start=True, stop=True)
                    ins.then_inc(ev("lora_psum"), 1)
            for e in range(C_LORA):
                r = slice(e * C_R, (e + 1) * C_R)
                for d in range(DC):
                    pe.matmul(bank(6 + e, D, d * D), lora[r, 4, d * P:(d + 1) * P], lora[r, 5, :],
                              start=True, stop=True).then_inc(ev("lora_psum"), 1)

            turn_x("c", nrm, "c_norm")
            pe.wait_ge(ev("c_xT"), 1)
            for d in range(DC):
                ins = pe.matmul(bank(1, C_E), xT[:, d, :, :].rearrange("p e s -> p (e s)"), c_wr[:, d, :],
                                start=(d == 0), stop=(d == DC - 1))
            ins.then_inc(ev("c_logits"), 1)
            loaded(pe, "wr")
            for n in range(4):
                half, hh = n // 2, n % 2
                r = slice(hh * S, hh * S + S)
                pe.wait_ge(ev("lora_in"), n + 1)
                for h in range(8):
                    ins = pe.matmul(bank(2 + n, L, h * L, rows=slice(0, X_HALF)),
                                    x_wqr[r, h, half * X_HALF:(half + 1) * X_HALF], x_wkr[r, h, :],
                                    start=True, stop=True)
                ins.then_inc(ev("qk_fold_psum"), 1)
            pe.wait_ge(ev("lora_in"), 8)
            for j in range(C_E // 2):
                pe.wait_ge(ev("qk_fold"), j + 1)
                for d in range(DC):
                    for e in range(2):
                        ins = pe.matmul(bank(2 + j, rows=slice(e * S, e * S + S)), xT[:, d, 0, :],
                                        l0_gu[:, d, 2 * j + e, :], start=(d == 0), stop=(d == DC - 1))
                ins.then_inc(ev("c_gu"), 1)
            for n in range(2):
                for j in range(2 * n, 2 * n + 2):
                    pe.wait_ge(ev("c_mid"), j + 1)
                    for f in range(2):
                        ins = pe.transpose(bank(6 + n, P, (j % 2) * 2 * P + f * P), c_mid[:, j, f * P:(f + 1) * P],
                                           ident)
                ins.then_inc(ev("c_midT_psum"), 1)
            for j in range(C_E // 2):
                pe.wait_ge(ev("c_midT"), j // 2 + 1)
                for f in range(2):
                    for e in range(2):
                        ins = pe.matmul(bank(0, D, rows=slice(e * S, e * S + S)), c_midT[:, j, f, e * S:e * S + S],
                                        l0_down[:, f, 2 * j + e, :], start=(j + f == 0),
                                        stop=(j == C_E // 2 - 1 and f == 1))
            ins.then_inc(ev("c_sum"), 1)

            loaded(pe, "wo")
            for n in range(X_H // 2):
                if n >= 2:
                    pe.wait_ge(ev("wo_fold"), n - 1)
                for h in range(2 * n, 2 * n + 2):
                    ins = pe.matmul(bank(4 + n % 2, D, (h % 2) * D, rows=slice(0, L)), x_kckv[:, h, :],
                                    x_wo[:, h, :], start=True, stop=True)
                ins.then_inc(ev("wo_fold_psum"), 1)
            pe.wait_ge(ev("roped"), 2)
            for n in range(-(-NT // 4)):
                if n >= 2:
                    pe.wait_ge(ev("keys_low"), n - 1)
                for t in range(4 * n, min(4 * n + 4, NT)):
                    ins = pe.transpose(bank(6 + n % 2, P, (t % 4) * P, rows=slice(0, L)), kv[:, t, 0:L], ident)
                ins.then_inc(ev("keysT"), 1)

            turn_x("d", nrm, "d_norm")
            loaded(pe, "wq")
            pe.wait_ge(ev("d_xT"), 1)
            for h in range(X_H):
                for d in range(DC):
                    ins = pe.matmul(bank(1 + h // 8, S, (h % 8) * S), x_wq[:, d, h * X_K:(h + 1) * X_K],
                                    xT[:, d, 0, :], start=(d == 0), stop=(d == DC - 1))
                if h % 8 == 7:
                    ins.then_inc(ev("qhk_psum"), 1)
            pe.wait_ge(ev("keys_low"), -(-NT // 4))
            for h in range(X_H):
                if h % 8 == 0:
                    pe.wait_ge(ev("qhk"), h // 8 + 1)
                for half, b in ((0, 3), (1, 5)):
                    ins = pe.matmul(bank(b + h // 8, S, (h % 8) * S, rows=slice(0, X_HALF)),
                                    x_kcq[:, h, half * X_HALF:(half + 1) * X_HALF], qhk[:, h, :],
                                    start=True, stop=True)
                if h % 8 == 7:
                    ins.then_inc(ev("qbig_psum"), 1)
            for h in range(X_H):
                if h % 8 == 0:
                    pe.wait_ge(ev("q_roped"), 2 * (h // 8 + 1))
                for half, q in ((0, q_lo), (1, q_hi)):
                    ins = pe.matmul(bank(1 + h // 8, S, (h % 8) * S, rows=slice(0, L)), x_qk[:, half, h, :],
                                    q[:, h, :], start=(half == 0), stop=(half == 1))
                if h % 8 == 7:
                    ins.then_inc(ev("q_psum"), 1)

            def max_scores(g, i, j):
                n = i * QT + (g * QT * NPASS + j)
                if not isinstance(n, int) or n >= 2:
                    pe.wait_ge(ev("key_max"), n - 1)
                q = q_hh[:, g * GQ + j * P:g * GQ + (j + 1) * P]
                for k in range(2):
                    src = bass.ds(i * CHUNK + k * HALF, HALF) if not isinstance(i, int) else \
                        slice(i * CHUNK + k * HALF, i * CHUNK + (k + 1) * HALF)
                    ins = pe.matmul(bank(4 + 2 * (j % 2) + k, HALF), q, keys[:, src], start=True, stop=True)
                ins.then_inc(ev("max_scores"), 1)

            def max_row(g):
                pe.wait_ge(ev("q_max"), g + 1)
                for j in range(QT):
                    ins = pe.matmul(bank(5, P, j * P, rows=slice(L, L + 1)), q_max[:, j:j + 1], ident,
                                    start=True, stop=True)
                ins.then_inc(ev("q_max_row"), 1)

            pe.wait_ge(ev("q_high"), 2 * GRP)
            for j in range(QT):
                max_scores(0, 0, j)
            with pe.Fori(1, NPASS) as i:
                for j in range(QT):
                    max_scores(0, i, j)
            max_row(0)
            for g in range(GRP):
                at_q = slice(g * GQ, (g + 1) * GQ)

                def weight(t, j, first, last):
                    pe.wait_ge(ev("probs"), t + 1)
                    pe.matmul(bank(4 * g, GQ, rows=slice(0, L + 1)), st_kv[:, j, :], probs[:, SLOT[j], :],
                              start=first, stop=last).then_inc(ev("weighted"), 1)

                def passes(i):
                    first = isinstance(i, int) and i == 0
                    for j in range(BODY):
                        t = i * BODY + (g * NT + j)
                        if j in (0, 4):
                            pe.wait_ge(ev("staged"), i * 6 + (g * 6 * NPASS + (3 if j == 0 else 6)))
                        if not (isinstance(t, int) and t < SLOT_AGE[j]):
                            pe.wait_ge(ev("probs"), t + (1 - SLOT_AGE[j]))
                        sc = bank(1 + SLOT[j], GQ)
                        pe.matmul(sc, st_hl[:, j * P:(j + 1) * P], q_hh[:, at_q], start=True, stop=False)
                        pe.matmul(sc, st_h1[0:L + 1, j * P:(j + 1) * P], q_lm[0:L + 1, at_q], start=False,
                                  stop=True).then_inc(ev("scores"), 1)
                        if not (first and j == 0):
                            weight(t - 1, (j - 1) % BODY, first and j == 1, False)
                        if g + 1 < GRP and j in MAX_AFTER:
                            max_scores(g + 1, i, MAX_AFTER.index(j))

                pe.wait_ge(ev("q_shift"), g + 1)
                if g == 0:
                    pe.wait_ge(ev("st_ones"), 1)
                passes(0)
                with pe.Fori(1, NPASS) as i:
                    passes(i)
                weight((g + 1) * NT - 1, BODY - 1, False, True)
                if g + 1 < GRP:
                    max_row(g + 1)

            pe.wait_ge(ev("ctx_un"), GRP)
            one = cst[L:L + 1, C_ONE:C_ONE + 1]
            for n in range(GRP * QT):
                ins = pe.matmul(bank(5, 1, n), ctx_un[L:L + 1, n // QT, (n % QT) * P:(n % QT + 1) * P], one,
                                start=True, stop=True)
            ins.then_inc(ev("den_psum"), 1)
            for g in range(GRP):
                pe.wait_ge(ev("den_diag"), g + 1)
                pe.matmul(bank(2 + g, GQ, rows=slice(0, L)), cst[:, C_ONE:C_ONE + L],
                          den_diag[:, :, :].rearrange("p j q -> p (j q)"), start=True,
                          stop=True).then_inc(ev("den_row"), 1)
            for g in range(GRP):
                pe.wait_ge(ev("ctx_n"), g + 1)
                for h in range(GH):
                    r = slice((h % 2) * S, (h % 2) * S + S)
                    ins = pe.matmul(bank(7, D, rows=r), ctx_n[:, g, h * S:(h + 1) * S], x_wo[0:L, g * GH + h, :],
                                    start=(g == 0 and h < 2), stop=(g == GRP - 1 and h >= GH - 2))
            ins.then_inc(ev("d_sum"), 1)

            turn_x("e", nrm, "e_norm")
            loaded(pe, "ew")
            pe.wait_ge(ev("e_xT"), 1)
            for name, b, col in (("q", 3, 0), ("k", 1, D)):
                for c in range(DC):
                    for d in range(DC):
                        ins = pe.matmul(bank(b, S, c * S), e_w[:, d, col + c * P:col + (c + 1) * P],
                                        xT[:, d, 0, :], start=(d == 0), stop=(d == DC - 1))
                ins.then_inc(ev(f"e_{name}_psum"), 1)
            for d in range(DC):
                ins = pe.matmul(bank(2, D), xT[:, d, :, :].rearrange("p e s -> p (e s)"), e_w[:, d, 2 * D:3 * D],
                                start=(d == 0), stop=(d == DC - 1))
            ins.then_inc(ev("e_v_psum"), 1)
            small_attention("e")

            turn_x("f", nrm, "f_norm")
            loaded(pe, "fwr")
            pe.wait_ge(ev("f_xT"), 1)
            for d in range(DC):
                ins = pe.matmul(bank(1, F_E), xT[:, d, :, :].rearrange("p e s -> p (e s)"), f_wr[:, d, :],
                                start=(d == 0), stop=(d == DC - 1))
            ins.then_inc(ev("f_logits"), 1)
            loaded(pe, "fgu")
            loaded(pe, "fdown")

            def gate_up(u):
                if u >= 2:
                    pe.wait_ge(ev("f_mid"), 2 * u - 2)
                for j in range(2):
                    for d in range(DC):
                        for e in range(2):
                            ins = pe.matmul(bank(2 + u % 2, 2 * F_I, j * 2 * F_I, rows=slice(e * S, e * S + S)),
                                            xT[:, d, 0, :], l1_gu[:, d, 4 * u + 2 * j + e, :],
                                            start=(d == 0), stop=(d == DC - 1))
                ins.then_inc(ev("f_gu"), 1)

            def turn_mid(u):
                if u >= 2:
                    pe.wait_ge(ev("f_midT"), u - 1)
                for j in range(2):
                    pe.wait_ge(ev("f_mid"), 2 * u + j + 1)
                    ins = pe.transpose(bank(6 + u % 2, P, j * P, rows=slice(0, F_I)), f_mid[:, u % 2, j, :], ident)
                ins.then_inc(ev("f_midT_psum"), 1)

            def down(u):
                pe.wait_ge(ev("f_midT"), u + 1)
                for j in range(2):
                    for e in range(2):
                        ins = pe.matmul(bank(0, D, rows=slice(e * S, e * S + S)), f_midT[:, u % 2, j, e * S:e * S + S],
                                        l1_down[:, 4 * u + 2 * j + e, :], start=(u + j == 0),
                                        stop=(u == F_STEPS - 1 and j == 1))
                ins.then_inc(ev("f_down"), 1)

            gate_up(0)
            for u in range(F_STEPS):
                if u + 1 < F_STEPS:
                    gate_up(u + 1)
                if u:
                    down(u - 1)
                turn_mid(u)
            down(F_STEPS - 1)


def kernel(**inputs):
    import concourse.bacc as _bacc
    from concourse.bass_utils import run_bass_kernel_spmd as _run

    a = {k: np.asarray(v) for k, v in inputs.items()}

    def rows(w):
        return w.reshape((w.shape[0] // P, P) + w.shape[1:]).swapaxes(0, 1)

    def halves(w):
        n = w.shape[0] // 2
        return w.reshape(2, n, *w.shape[1:]).transpose(0, 2, 1, 3).reshape(2 * w.shape[1], n, w.shape[2])

    sin, cos = rope(CTX, L, 1)
    table = np.stack([sin, cos])
    lora = np.stack([a["L0_ffn_Ga"].swapaxes(1, 2), a["L0_ffn_Gb"], a["L0_ffn_Ua"].swapaxes(1, 2),
                     a["L0_ffn_Ub"], a["L0_ffn_Da"].swapaxes(1, 2), a["L0_ffn_Db"]], 1)
    data = {
        "x": a["x"][0],
        "cst": constants(),
        "ctx_t": a["ctx_512"][0, :S].T,
        "a_wkv": a["L0_xattn_Wkv_expand"].T,
        "a_wq": rows(a["L0_xattn_Wq"].T),
        "a_wo": rows(a["L0_xattn_Wout"].T),
        "dt": a["L0_attn_dt"],
        "columns": np.concatenate([rows(a[k]) for k in ("L0_attn_gamma", "L0_attn_beta", "L0_attn_dt")] +
                                  [rows(a["L1_attn_b_attn"][:2 * D]), rows(a["L0_ffn_Wr"]).reshape(P, DC * C_E)], 1),
        "temp": a["L0_ffn_temperature"],
        "b_win": rows(a["L0_attn_W_in"].T),
        "b_wout": rows(a["L0_attn_W_out"].T),
        "lora": lora.transpose(0, 2, 1, 3).reshape(P, 6, D),
        "c_gu": rows(np.concatenate([a["L0_ffn_Wg"], a["L0_ffn_Wu"]], 2).swapaxes(0, 1)),
        "c_down": rows(a["L0_ffn_Wd"].swapaxes(0, 1)),
        "ctx": a["ctx_512"][0].reshape(P, NT, L),
        "rope": table.reshape(2, P, NT, L // 2).swapaxes(0, 1),
        "x_wqr": halves(a["L1_xattn_W_qr"].swapaxes(1, 2)),
        "x_wkr": halves(a["L1_xattn_W_kr"].swapaxes(1, 2)),
        "x_kckv": a["L1_xattn_w_kc_kv"].swapaxes(0, 1),
        "x_wo": rows(a["L1_xattn_Wo"].T),
        "x_wq": rows(a["L1_xattn_Wq"].T),
        "x_kcq": a["L1_xattn_w_kc_q"].swapaxes(0, 1),
        "f_wr": rows(a["L1_ffn_router_w"].T),
        "e_b": a["L1_attn_b_attn"],
        "e_bp": a["L1_attn_b_proj"],
        "e_w": rows(a["L1_attn_W_attn"]),
        "e_wp": rows(a["L1_attn_W_proj"]),
        "f_gu": rows(np.concatenate([a["L1_ffn_w_gate"], a["L1_ffn_w_up"]], 2).swapaxes(0, 1)),
        "f_down": a["L1_ffn_w_down"].swapaxes(0, 1),
    }
    data = {k: np.ascontiguousarray(v) for k, v in data.items()}
    nc = _bacc.Bacc("TRN2", target_bir_lowering=False, num_devices=1)
    dram = {k: nc.dram_tensor(k, v.shape, F32, kind="ExternalInput").ap() for k, v in data.items()}
    out = nc.dram_tensor("out", (S, D), F32, kind="ExternalOutput").ap()
    build(nc, dram, out)
    r = _run(nc, [data], core_ids=[0])
    return r.results[0]["out"].reshape(1, S, D)
```

```python
from contextlib import ExitStack
import math

import numpy as np

import concourse.bass as bass
from concourse import mybir

F32 = mybir.dt.float32
F32R = mybir.dt.float32r
BF16 = mybir.dt.bfloat16
ALU = mybir.AluOpType
ACT = mybir.ActivationFunctionType
AX = mybir.AxisListType.X

P = 128
S = 64
D = 256
DC = D // P
EPS = 1e-5
FMAX = float(np.finfo(np.float32).max)

A_HD, A_NH = 16, 16
B_INNER = 512
C_E, C_F, C_R, C_LORA = 8, 256, 64, 2
GOLDEN_CENTER = 1.0 / math.e
GOLDEN_LOWER = 0.5 - math.log(4.0 / 3.0)
GOLDEN_UPPER = 0.5
CTX, L = 6272, 64
NT = CTX // P
X_H, X_K, X_CQ, X_R = 16, 128, 192, 64
X_HALF = X_CQ // 2
E_HD, E_NH = 8, 32
F_E, F_K, F_I = 32, 8, 96

GRP = 2
GH = X_H // GRP
GQ = GH * S
QT = GQ // P
BODY = 7
NPASS = NT // BODY
KEYS_FIRST = 8
KGROUPS = -(-NT // 4)
CHUNK = BODY * P
HALF = CHUNK // 2
HALVES = ((0, 4), (4, BODY))
F_STEPS = F_E // 4
BANK = 512

C_ID, C_CAUS, C_ADDA, C_ADDE, C_PAR, C_BLKA, C_BLKE, C_ROPE, C_ONE, C_NH = (
    0, 128, 192, 256, 320, 322, 330, 346, 602, 666)
C_N = 672


def constants():
    c = np.zeros((P, C_N), np.float32)
    p = np.arange(P)
    row = p % S
    col = np.arange(S)
    seen = col[None, :] <= row[:, None]
    c[:, C_ID:C_ID + P] = np.eye(P)
    c[:, C_CAUS:C_CAUS + S] = seen
    c[:, C_ADDA:C_ADDA + S] = np.where(seen, 0.0, -FMAX)
    slope = 2.0 ** (-(8.0 / E_NH))
    c[:, C_ADDE:C_ADDE + S] = np.where(seen, (col[None, :] - row[:, None]) * slope, -10000.0)
    c[:, C_PAR] = p < S
    c[:, C_PAR + 1] = p >= S
    c[:, C_BLKA:C_BLKA + 8] = (p[:, None] // A_HD) == np.arange(8)[None, :]
    c[:, C_BLKE:C_BLKE + 16] = (p[:, None] // E_HD) == np.arange(16)[None, :]
    sin, cos = rope(S, X_CQ)
    for n, t in enumerate((cos[:, :X_HALF], cos[:, X_HALF:], sin[:, :X_HALF], sin[:, X_HALF:])):
        c[:X_HALF, C_ROPE + n * S:C_ROPE + (n + 1) * S] = t.T
    c[:, C_ONE:C_ONE + S] = 1.0
    c[:, C_NH] = -0.5
    return c


def rope(length, dim, each=2):
    inv = (1.0 / np.float32(10000.0) ** (np.arange(0, dim, 2, dtype=np.float32) / np.float32(dim)))
    f = np.arange(length, dtype=np.float32)[:, None] * inv.astype(np.float32)[None, :]
    return (np.repeat(np.sin(f), each, axis=-1).astype(np.float32),
            np.repeat(np.cos(f), each, axis=-1).astype(np.float32))


SLOT = (0, 1, 2, 0, 1, 2, 1)
SLOT_AGE = (4, 2, 4, 3, 3, 3, 2)
SPLIT = (0, 1, 2, 3, 0, 1, 2)
SPLIT_AGE = (3, 3, 3, 7, 4, 4, 4)
C_PAIR = (1, 2, 3, 0)
QK_BANK = (5, 3, 4, 6)
QHK_BANK = (6, 1)
QBIG_BANK = ((2, 4), (0, 3))
Q_BANK = (2, 1)
LAG = 2
MAX_AFTER = (1, 1, 1, 1, 1, 1, 2)

NORMS = ("a", "b", "b2", "c", "d", "e", "f")

W = dict(start=18, a_norm=0, xT=4, a_softmax=3, a_probs=3, a_o=2, a_oT=2, b_norm=10, b_gate=4, keys=3,
         max=6, max_row=4, den=5, e_norm=13, e_softmax=26, e_probs=5, e_o=2, e_oT=2, f_norm=12)

LOADS = dict(x=1, cst=1, actx=2, awkv=1, awq=1, awo=1, b=3, bw=2, lora=1, cgu=1, cdown=1, ctx=1,
             rope=1, wr=2, wo=2, wq=1, kcq=1, fwr=1, ebias=2, ew=2, fgu=1, fdown=1)


def build(nc, dram, out):
    with ExitStack() as ctx:
        base = -(-nc.sbuf_base // 64) * 64
        width = (nc.sbuf_usable_end - base) // 4 - 16
        ctx.enter_context(nc.sbuf_tensor("arena", [P, width], F32))

        def at(name, col, shape, dtype=F32):
            assert col + math.prod(shape[1:]) <= width, name
            return nc.alloc_sbuf_tensor_at(name, shape, dtype, offset=base + 4 * col)

        R1 = 0
        R2 = 12288
        R3 = 20480
        R4 = 24576
        R5 = 26624
        R6 = 32896
        R7 = 36096
        R8 = 42368
        R9 = 45952
        R10 = 49024
        VEC = R10 + C_N + 3 * D + 2 * P
        WORK = VEC + 512

        l0_gu = at("l0_gu", R1, [P, DC, C_E, 2 * C_F])
        l0_down = at("l0_down", R1 + 8192, [P, DC, C_E, D])
        qhk = at("qhk", R1, [P, X_H, S])
        q_lo = at("q_lo", R1 + 1024, [X_HALF, X_H, S])
        q_hi = at("q_hi", R1 + 2048, [X_HALF, X_H, S])
        q_lo_sin = at("q_lo_sin", R1 + 3072, [X_HALF, X_H, S])
        q_hi_sin = at("q_hi_sin", R1 + 4096, [X_HALF, X_H, S])
        l1_gu = at("l1_gu", R1, [P, DC, F_E, 2 * F_I])
        x_wq = at("x_wq", R2, [P, DC, X_H * X_K])
        x_kcq = at("x_kcq", R2 + 4096, [P, X_H, X_CQ])
        x_kckv = at("x_kckv", R2 + 7168, [P, X_H, L])
        l1_down = at("l1_down", R2, [F_I, F_E, D])
        x_wo = at("x_wo", R3, [P, X_H, D])
        att_a = dict(kbd=at("kbd_a", R4, [P, DC, 8, S]), sc=at("sc_a", R4 + 1024, [P, 8, S]),
                     pt=at("pt_a", R4 + 1536, [P, 4, P]))
        x_qk = at("x_qk", R4, [X_HALF, 2, X_H, L])
        e_w = at("e_w", R4, [P, DC, 3 * D])
        e_wp = at("e_wp", R4 + 1536, [P, DC, D])
        turned = at("turned", R5, [P, NT, L])
        a_wq = at("a_wq", R5 + 3136, [P, DC, D])
        a_wkv = at("a_wkv", R5 + 3648, [L, 2 * D])
        a_wo = at("a_wo", R5 + 4160, [P, DC, D])
        a_ctx = at("a_ctx", R5 + 4672, [L, 2, S])
        dt_row = at("dt_row", R5 + 4800, [P, B_INNER])
        keys = at("keys", R5, [P, CTX], F32R)
        att_e = dict(kbd=at("kbd_e", R5, [P, DC, 16, S]), sc=at("sc_e", R5 + 2048, [P, 16, S]),
                     pt=at("pt_e", R5 + 3072, [P, 8, P]))
        f_mid = at("f_mid", R5 + 4096, [P, 2, 2, F_I])
        f_midT = at("f_midT", R5 + 4480, [F_I, 2, 2, P])
        kv = at("kv", R6, [P, NT, L])
        ctx_sb = at("ctx_sb", R7, [P, NT, L])
        rope_sb = at("rope_sb", R7 + 3136, [P, 2, NT, L // 2])
        probs = at("probs", R7, [P, 3, GQ])
        st_hl = at("st_hl", R7 + 1536, [P, CHUNK], F32R)
        st_h1 = at("st_h1", R7 + 2432, [P, CHUNK], F32R)
        q_hh = at("q_hh", R7 + 3328, [P, X_H * S], F32R)
        q_lm = at("q_lm", R7 + 4352, [P, X_H * S], F32R)
        probs_h = at("probs_h", R7 + 5376, [P, 4, GQ], F32R)
        probs_l = at("probs_l", R7 + 7424, [P, 4, GQ], F32R)
        x_wqr = at("x_wqr", R8, [P, X_H // 2, X_CQ])
        x_wkr = at("x_wkr", R8 + 1536, [P, X_H // 2, L])
        lora = at("lora", R8 + 2048, [P, 6, D])
        c_mid = at("c_mid", R8, [P, 4, C_F])
        c_midT = at("c_midT", R8 + 1024, [P, 4, 2, P])
        b_win = at("b_win", R9, [P, DC, 2 * B_INNER])
        b_wout = at("b_wout", R9 + 2048, [P, B_INNER // P, D])
        ctx_un = at("ctx_un", R9, [L + 1, GRP, GQ])
        ctx_n = at("ctx_n", R9 + 1024, [L, GRP, GQ])
        den_diag = at("den_diag", R9 + 2048, [P, QT, P])
        key_max = at("key_max", R9 + 2560, [P, QT, 2 * NPASS])
        q_max = at("q_max", R9 + 2616, [P, QT])
        den_inv = at("den_inv", R9 + 2624, [P, GRP * QT])
        f_wr = at("f_wr", R9 + 2632, [P, DC, F_E])
        e_bv = at("e_bv", R9 + 2696, [P, D])

        cst = at("cst", R10, [P, C_N])
        res = at("res", R10 + C_N, [S, D])
        nrm = at("nrm", R10 + C_N + D, [S, D])
        nrm2 = at("nrm2", R10 + C_N + 2 * D, [S, D])
        xT = at("xT", R10 + C_N + 3 * D, [P, DC, 2, S])
        vec = at("vec", VEC, [P, 512])
        b_clip = at("b_clip", WORK, [P, 8, S])
        b_sig = at("b_sig", WORK + 512, [P, 8, S])
        b_z = at("b_z", WORK + 1024, [P, 4, S])
        st_kvh = at("st_kvh", WORK, [P, BODY, L + 1], F32R)
        st_kv = at("st_kv", WORK + 1024, [P, BODY, L])
        st_kvl = at("st_kvl", WORK + 512, [P, BODY, L + 1], F32R)
        vbd = at("vbd", WORK + 1280, [P, D])
        oT = at("oT", WORK + 1536, [P, P])
        e_bp = at("e_bp", WORK + 1664, [S, D])

        warm_data = at("warm_data", R6 + NT * L, [P, P], BF16)

        ident = cst[:, C_ID:C_ID + P]
        rope_q = cst[0:X_HALF, C_ROPE:C_ROPE + 4 * S].rearrange("p (n s) -> p n s", n=4)

        used = [0]

        def cols(w, rows=P):
            used[0] += w
            assert used[0] <= 512
            return vec[0:rows, used[0] - w:used[0]]

        stats, mean_var, var_eps, rstd = cols(6, S), cols(2, S), cols(1, S), cols(1, S)
        qT = cols(DC * S).rearrange("p (c s) -> p c s", c=DC)
        row_max, row_sum, row_inv = cols(16), cols(16), cols(16)
        columns = cols(2 * DC + 4 + 2 * DC + DC * C_E)
        gamma, beta, dt_col = columns[:, 0:DC], columns[:, DC:2 * DC], columns[:, 2 * DC:2 * DC + 4]
        e_bias = columns[:, 2 * DC + 4:4 * DC + 4]
        c_wr = columns[:, 4 * DC + 4:].rearrange("p (c e) -> p c e", c=DC)
        dt_e, dt_w = cols(4), cols(4)
        dt_min, dt_sum, dt_inv = cols(1), cols(1), cols(1)
        temp, temp_inv = cols(1), cols(1)
        inh, zone, dist, w_zone, fallback = cols(8), cols(8), cols(8), cols(8), cols(14)
        top, taken, left = cols(8), cols(8), cols(14)
        w_sum, no_expert, w_c = cols(1), cols(1), cols(4)
        f_exp, f_left, w_f = cols(F_E), cols(F_E), cols(F_E // 2)
        f_shift = cols(1)

        ps = ctx.enter_context(nc.psum_tensor("ps", [P, 8 * BANK], F32))

        def bank(b, n=BANK, start=0, rows=slice(0, P)):
            return ps[rows, b * BANK + start:b * BANK + start + n]

        sems = {}

        def ev(name):
            if name not in sems:
                sems[name] = ctx.enter_context(nc.semaphore(name))
            return sems[name]

        def loaded(eng, name):
            eng.wait_ge(ev("ld_" + name), 16 * LOADS[name])

        steps = {"dve": 0}

        def link(eng, ins):
            steps["dve"] += 1
            ins.then_inc(ev("dve_step"), 1)
            eng.wait_ge(ev("dve_step"), steps["dve"])

        att = {
            "a": dict(att_a, hd=A_HD, nh=8, blk=C_BLKA, add=C_ADDA, scale=A_HD ** -0.5, wo=a_wo),
            "e": dict(att_e, hd=E_HD, nh=16, blk=C_BLKE, add=C_ADDE,
                      scale=float(np.float32(1.0) / np.sqrt(np.float32(E_HD))), wo=e_wp),
        }

        block = ctx.enter_context(nc.Block())

        @block.sync
        def _(sp):
            def load(name, dst, src):
                sp.dma_start(dst, src).then_inc(ev("ld_" + name), 16)

            load("x", res[:, :], dram["x"])
            load("cst", cst[:, :], dram["cst"])
            load("actx", a_ctx[:, 0, :], dram["ctx_t"])
            load("actx", a_ctx[:, 1, :], dram["ctx_t"])
            load("awkv", a_wkv[:, :], dram["a_wkv"])
            load("awq", a_wq[:, :, :], dram["a_wq"])
            load("b", dt_row[:, :], dram["dt"].partition_broadcast(P))
            load("b", columns, dram["columns"])
            load("b", temp, dram["temp"].partition_broadcast(P))
            load("awo", a_wo[:, :, :], dram["a_wo"])
            load("wr", x_wqr[:, :, :], dram["x_wqr"])
            load("wr", x_wkr[:, :, :], dram["x_wkr"])
            load("bw", b_win[:, :, :], dram["b_win"])
            load("bw", b_wout[:, :, :], dram["b_wout"])
            load("lora", lora[:, :, :], dram["lora"])
            load("ctx", ctx_sb[:, :, :], dram["ctx"])
            load("rope", rope_sb[:, :, :, :], dram["rope"])
            load("cgu", l0_gu[:, :, :, :], dram["c_gu"])
            load("cdown", l0_down[:, :, :, :], dram["c_down"])
            load("wq", x_wq[:, :, :], dram["x_wq"])
            load("kcq", x_kcq[:, :, :], dram["x_kcq"])
            load("wo", x_kckv[:, :, :], dram["x_kckv"])
            load("wo", x_wo[:, :, :], dram["x_wo"])
            sp.wait_ge(ev("b_done"), 1)
            load("fwr", f_wr[:, :, :], dram["f_wr"])
            load("ebias", e_bv[:, :], dram["e_b"][2 * D:3 * D].partition_broadcast(P))
            load("ebias", e_bp[:, :], dram["e_bp"].partition_broadcast(S))
            sp.wait_ge(ev("q_low"), GRP)
            sp.wait_ge(ev("wo_fold_psum"), X_H // 2)
            load("ew", e_w[:, :, :], dram["e_w"])
            load("ew", e_wp[:, :, :], dram["e_wp"])
            load("fgu", l1_gu[:, :, :, :], dram["f_gu"])
            load("fdown", l1_down[:, :, :], dram["f_down"])
            sp.wait_ge(ev("result"), 1)
            sp.dma_start(out, res[:, :]).then_inc(ev("stored"), 16)
            sp.wait_ge(ev("stored"), 16)

        @block.gpsimd
        def _(pool):
            def norm_scale(t):
                pool.wait_ge(ev("variance"), 1 + NORMS.index(t))
                pool.tensor_tensor(rstd, var_eps, cst[0:S, C_NH:C_NH + 1], ALU.pow).then_inc(ev("rstd"), 1)

            loaded(pool, "cst")
            norm_scale("a")
            norm_scale("b")
            norm_scale("b2")
            norm_scale("c")
            loaded(pool, "ctx")
            loaded(pool, "rope")
            half = L // 2
            pairs = ctx_sb[:, :, :].rearrange("p t (f e) -> p t f e", e=2)
            sin, cos = rope_sb[:, 0, :, :], rope_sb[:, 1, :, :]
            pool.tensor_tensor(kv[:, :, :].rearrange("p t (f e) -> p t f e", e=2), pairs,
                               cos.unsqueeze(3).broadcast_to([P, NT, half, 2]), ALU.mult).then_inc(ev("rope_cos"), 1)
            for a, b in ((0, half), (half, 0)):
                pool.tensor_tensor(
                    turned[:, :, a:a + half].rearrange("p t (f e) -> p t f e", e=2),
                    ctx_sb[:, :, b:b + half].rearrange("p t (f e) -> p t f e", e=2),
                    sin[:, :, a // 2:a // 2 + half // 2].unsqueeze(3).broadcast_to([P, NT, half // 2, 2]),
                    ALU.mult).then_inc(ev("rope_sin"), 1)
            pool.wait_ge(ev("rope_cos"), 1)
            pool.wait_ge(ev("rope_sin"), 2)
            pool.tensor_tensor(kv[:, :, 0:half], kv[:, :, 0:half], turned[:, :, 0:half],
                               ALU.subtract).then_inc(ev("roped"), 1)
            pool.tensor_tensor(kv[:, :, half:L], kv[:, :, half:L], turned[:, :, half:L],
                               ALU.add).then_inc(ev("roped"), 1)
            norm_scale("d")

            def stage_kv(g, i, half):
                a, b = HALVES[half]
                n = i * 2 + (g * 2 * NPASS + half)
                src = kv[:, bass.ds(i * BODY + a, b - a), :] if not isinstance(i, int) else \
                    kv[:, i * BODY + a:i * BODY + b, :]
                free = i * BODY + (g * NT - (BODY - b))
                if not isinstance(free, int) or free > 0:
                    pool.wait_ge(ev("weighted"), free)
                pool.tensor_copy(st_kv[:, a:b, :], src).then_inc(ev("kv_staging"), 1)
                pool.tensor_copy(st_kvh[:, a:b, 0:L], src).then_inc(ev("kv_staging"), 1)
                pool.wait_ge(ev("kv_staging"), 2 * n + 2)
                pool.tensor_tensor(st_kvl[:, a:b, 0:L], st_kv[:, a:b, :], st_kvh[:, a:b, 0:L].bitcast(F32),
                                   ALU.subtract).then_inc(ev("kv_staged"), 1)

            pool.wait_ge(ev("b_done"), 1)
            pool.memset(st_kvh[:, :, L:L + 1].bitcast(F32), 1.0).then_inc(ev("kv_ones"), 1)
            pool.memset(st_kvl[:, :, L:L + 1].bitcast(F32), 0.0).then_inc(ev("kv_ones"), 1)
            for g in range(GRP):
                for half in range(2):
                    stage_kv(g, 0, half)
                with pool.Fori(1, NPASS) as i:
                    for half in range(2):
                        stage_kv(g, i, half)
            norm_scale("e")
            norm_scale("f")

        @block.scalar
        def _(act):
            def softmax_exp(t):
                sc = att[t]["sc"]
                act.wait_ge(ev(t + "_shifted"), 1)
                act.activation(sc[:, :, :], sc[:, :, :], ACT.Exp).then_inc(ev(t + "_exp"), 1)

            def probs_turned(t):
                pairs = att[t]["nh"] // 2
                act.wait_ge(ev(t + "_probsT_psum"), 1)
                act.activation(att[t]["pt"][:, :, :], bank(6, pairs * P).rearrange("p (j q) -> p j q", j=pairs),
                               ACT.Copy).then_inc(ev(t + "_probsT"), 1)

            act.wait_ge(ev("dt_min"), 1)
            act.activation(dt_e, dt_col, ACT.Exp, bias=dt_min, scale=-1.0).then_inc(ev("dt_exp"), 1)
            act.activation(dt_row[:, :], dt_row[:, :], ACT.Exp, bias=dt_min, scale=-1.0,
                           accum_out=dt_sum).then_inc(ev("dt_exp"), 1)
            softmax_exp("a")
            act.preload_act_table(ACT.Sigmoid)
            probs_turned("a")
            for n in range(4):
                if n == 3:
                    act.wait_ge(ev("b_clipped"), 1)
                    act.activation(b_sig[:, :, :], b_clip[:, :, :], ACT.Sigmoid).then_inc(ev("b_sigmoid"), 1)
                act.wait_ge(ev("qk_fold_psum"), n + 1)
                act.activation(x_qk[:, n // 2, 8 * (n % 2):8 * (n % 2) + 8, :],
                               bank(QK_BANK[n], rows=slice(0, X_HALF)).rearrange("p (h d) -> p h d", h=8),
                               ACT.Copy).then_inc(ev("qk_fold"), 1)

            act.wait_ge(ev("c_logits"), 1)
            act.wait_ge(ev("temp_inv"), 1)
            act.activation(inh, bank(1, C_E), ACT.Sigmoid, scale=temp_inv).then_inc(ev("c_inh"), 1)
            act.preload_act_table(ACT.Exp)
            act.wait_ge(ev("c_dist"), 1)
            act.activation(w_zone, dist, ACT.Exp, scale=-1.0 / 0.1).then_inc(ev("c_exp"), 1)
            act.activation(fallback[:, 0:C_E], dist, ACT.Exp, scale=-1.0 / 0.3).then_inc(ev("c_exp"), 1)
            act.preload_act_table(ACT.Silu)
            act.wait_ge(ev("lora_psum"), 8)
            for j in range(C_E // 2):
                act.wait_ge(ev("c_gu"), j + 1)
                act.activation(c_mid[:, j, :], bank(2 + j, C_F), ACT.Silu).then_inc(ev("c_silu"), 1)
            act.preload_act_table(ACT.Exp)

            def keys_high(n):
                w = min(4, NT - 4 * n) * P
                act.wait_ge(ev("keysT"), n + 1)
                act.activation(keys[0:L, n * BANK:n * BANK + w], bank(n % 2, w, rows=slice(0, L)),
                               ACT.Copy).then_inc(ev("keys_high"), 1)

            for n in range(2):
                keys_high(n)
            for n in range(2):
                act.wait_ge(ev("c_midT_psum"), n + 1)
                act.activation(c_midT[:, 2 * n:2 * n + 2, :, :],
                               bank(2 + n).rearrange("p (j f q) -> p j f q", j=2, f=2),
                               ACT.Copy).then_inc(ev("c_midT"), 1)
            for n in range(2, KGROUPS):
                keys_high(n)
                if n - 2 < X_H // 2:
                    act.wait_ge(ev("wo_fold_psum"), n - 1)
                    act.activation(x_wo[0:L, 2 * (n - 2):2 * (n - 2) + 2, :],
                                   bank(2 + n % 2, rows=slice(0, L)).rearrange("p (h d) -> p h d", h=2),
                                   ACT.Copy).then_inc(ev("wo_fold"), 1)

            for n in range(2):
                act.wait_ge(ev("qhk_psum"), n + 1)
                act.activation(qhk[:, 8 * n:8 * n + 8, :], bank(QHK_BANK[n]).rearrange("p (h s) -> p h s", h=8),
                               ACT.Copy).then_inc(ev("qhk"), 1)
            for g in range(GRP):
                q, at_q = bank(Q_BANK[g], GQ, rows=slice(0, L)), slice(g * GQ, (g + 1) * GQ)
                act.wait_ge(ev("q_psum"), g + 1)
                act.activation(q_hh[0:L, at_q], q, ACT.Copy).then_inc(ev("q_high"), 1)
                act.activation(q_hh[L:2 * L, at_q], q, ACT.Copy).then_inc(ev("q_high"), 1)

            for g in range(GRP):
                def exps(i):
                    for j in range(BODY):
                        t = i * BODY + (g * NT + j)
                        scores = bank(1 + SLOT[j], GQ)
                        act.wait_ge(ev("scores"), t + 1)
                        if not (isinstance(t, int) and t < SPLIT_AGE[j]):
                            act.wait_ge(ev("weighted"), t + (1 - SPLIT_AGE[j]))
                        act.activation(probs_h[:, SPLIT[j], :], scores, ACT.Exp).then_inc(ev("probs_high"), 1)
                        if not (isinstance(t, int) and t < SLOT_AGE[j]):
                            act.wait_ge(ev("probs_low"), t + (1 - SLOT_AGE[j]))
                        act.activation(probs[:, SLOT[j], :], scores, ACT.Exp).then_inc(ev("probs"), 1)

                exps(0)
                with act.Fori(1, NPASS) as i:
                    exps(i)
                act.wait_ge(ev("weighted"), (g + 1) * NT)
                act.activation(ctx_un[:, g, :], bank(4 * g, GQ, rows=slice(0, L + 1)),
                               ACT.Copy).then_inc(ev("ctx_un"), 1)

            softmax_exp("e")
            probs_turned("e")

            act.wait_ge(ev("f_shift"), 1)
            act.activation(f_exp, bank(1, F_E), ACT.Exp, bias=f_shift).then_inc(ev("f_exp"), 1)
            act.preload_act_table(ACT.Silu)

            for u in range(F_STEPS):
                b = u % 2
                act.wait_ge(ev("f_gu"), u + 1)
                if u >= 2:
                    act.wait_ge(ev("f_midT_psum"), u - 1)
                gates = bank(2 + b, 4 * F_I).rearrange("p (j g f) -> p j g f", j=2, g=2)[:, :, 0, :]
                act.activation(f_mid[:, b, :, :], gates, ACT.Silu).then_inc(ev("f_silu"), 1)

        @block.vector
        def _(dve):
            def norm(t, src, dst):
                link(dve, dve.bn_stats(stats, src))
                link(dve, dve.bn_aggr(mean_var, stats))
                dve.tensor_scalar(var_eps, mean_var[:, 1:2], EPS, None, ALU.add).then_inc(ev("variance"), 1)
                dve.wait_ge(ev("rstd"), 1 + NORMS.index(t))
                dve.tensor_scalar(dst, src, mean_var[:, 0:1], rstd, ALU.subtract,
                                  ALU.mult).then_inc(ev("norm"), 1)

            def turned_twice(t, b=0):
                dve.wait_ge(ev(t + "_xT_psum"), 1)
                src = bank(b, 2 * S).rearrange("p (c s) -> p c s", c=DC).unsqueeze(2)
                dve.tensor_copy(xT[:, :, :, :], src.broadcast_to([P, DC, 2, S])).then_inc(ev(t + "_xT"), 1)

            def head_blocks(t):
                a = att[t]
                nh, hd, kbd = a["nh"], a["hd"], a["kbd"]
                blk = cst[:, a["blk"]:a["blk"] + nh].unsqueeze(2).broadcast_to([P, nh, S])
                dve.wait_ge(ev(t + "_k_psum"), 1)
                for c in range(DC):
                    k = bank(1, S, c * S).unsqueeze(1).broadcast_to([P, nh, S])
                    if t == "e":
                        ins = dve.scalar_tensor_tensor(kbd[:, c, :, :], k, e_bias[:, DC + c:DC + c + 1], blk,
                                                       ALU.add, ALU.mult)
                    else:
                        ins = dve.tensor_tensor(kbd[:, c, :, :], k, blk, ALU.mult)
                    ins.then_inc(ev(t + "_kbd"), 1)
                par = cst[:, C_PAR:C_PAR + 2].unsqueeze(1).unsqueeze(3).broadcast_to([P, nh, 2, hd])
                split = "p (j e d) -> p j e d"
                dve.wait_ge(ev(t + "_v_psum"), 1)
                v = bank(2, D)
                if t == "e":
                    link(dve, dve.tensor_tensor(vbd[:, :], v, e_bv[:, :], ALU.add))
                    v = vbd[:, :]
                dve.tensor_tensor(vbd[:, :].rearrange(split, e=2, d=hd), v.rearrange(split, e=2, d=hd), par,
                                  ALU.mult).then_inc(ev(t + "_vbd"), 1)

            def queries(t):
                dve.wait_ge(ev(t + "_q_psum"), 1)
                if t == "e":
                    for c in range(DC):
                        dve.tensor_scalar(qT[:, c, :], bank(3, S, c * S), e_bias[:, c:c + 1], None,
                                          ALU.add).then_inc(ev(t + "_q"), 1)
                else:
                    dve.tensor_copy(qT, bank(3, DC * S).rearrange("p (c s) -> p c s", c=DC)).then_inc(ev(t + "_q"), 1)

            def softmax(t):
                a = att[t]
                nh, sc, hd = a["nh"], a["sc"], a["hd"]
                n = nh * S

                def mask(col):
                    return cst[:, col:col + S].unsqueeze(1).broadcast_to([P, nh, S])

                def each(v):
                    return v[:, 0:nh].unsqueeze(2).broadcast_to([P, nh, S])

                dve.wait_ge(ev(t + "_scores"), DC)
                link(dve, dve.scalar_tensor_tensor(sc[:, :, :], ps[:, 4 * BANK:4 * BANK + n].rearrange(
                    "p (h k) -> p h k", h=nh), a["scale"], mask(C_CAUS), ALU.mult, ALU.mult))
                link(dve, dve.tensor_tensor(sc[:, :, :], sc[:, :, :], mask(a["add"]), ALU.add))
                link(dve, dve.tensor_reduce(row_max[:, 0:nh], sc[:, :, :], AX, ALU.max))
                dve.tensor_tensor(sc[:, :, :], sc[:, :, :], each(row_max),
                                  ALU.subtract).then_inc(ev(t + "_shifted"), 1)
                dve.wait_ge(ev(t + "_exp"), 1)
                link(dve, dve.tensor_reduce(row_sum[:, 0:nh], sc[:, :, :], AX, ALU.add))
                link(dve, dve.reciprocal(row_inv[:, 0:nh], row_sum[:, 0:nh]))
                dve.wait_ge(ev(t + "_o_psum"), 1)
                dve.tensor_tensor(oT[:, :].rearrange("p (h d) -> p h d", h=nh),
                                  bank(0, P).rearrange("p (h d) -> p h d", h=nh),
                                  row_inv[:, 0:nh].unsqueeze(2).broadcast_to([P, nh, hd]),
                                  ALU.mult).then_inc(ev(t + "_o"), 1)
                dve.wait_ge(ev(t + "_oT_psum"), 1)
                dve.tensor_copy(oT[:, :], bank(1, P)).then_inc(ev(t + "_oT"), 1)

            def add_halves(done, count, b, last):
                dve.wait_ge(ev(done), count)
                link(dve, dve.tensor_tensor(res[:, :], bank(b, D, rows=slice(0, S)), res[:, :], ALU.add))
                ins = dve.tensor_tensor(res[:, :], bank(b, D, rows=slice(S, 2 * S)), res[:, :], ALU.add)
                if last:
                    ins.then_inc(ev("result"), 1)
                else:
                    link(dve, ins)

            dve.memset(warm_data[:, :], 1.0).then_inc(ev("warm_data"), 1)

            loaded(dve, "x")
            norm("a", res[:, :], nrm[:, :])
            loaded(dve, "cst")
            head_blocks("a")
            turned_twice("a")
            queries("a")
            loaded(dve, "b")
            dve.tensor_reduce(dt_min, dt_row[:, :], AX, ALU.min).then_inc(ev("dt_min"), 1)
            dve.reciprocal(temp_inv, temp).then_inc(ev("temp_inv"), 1)
            softmax("a")
            dve.wait_ge(ev("dt_exp"), 2)
            link(dve, dve.reciprocal(dt_inv, dt_sum))
            link(dve, dve.tensor_scalar(dt_w, dt_e, dt_inv, None, ALU.mult))
            dve.wait_ge(ev("a_out"), 1)
            link(dve, dve.tensor_tensor(res[:, :], bank(2, D, rows=slice(0, S)), res[:, :], ALU.add))

            norm("b", res[:, :], nrm[:, :])
            dve.wait_ge(ev("norm"), 1 + NORMS.index("b"))
            norm("b2", nrm[:, :], nrm2[:, :])
            link(dve, dve.tensor_tensor(res[:, :], res[:, :], nrm[:, :], ALU.add))
            dve.wait_ge(ev("b_xT_psum"), 1)
            for c in range(DC):
                dve.tensor_scalar(xT[:, c, 0, :], bank(0, S, c * S), gamma[:, c:c + 1], beta[:, c:c + 1],
                                  ALU.mult, ALU.add).then_inc(ev("b_xT"), 1)
            proj = bank(1, 8 * S).rearrange("p (c s) -> p c s", c=8)
            dve.wait_ge(ev("b_proj"), 1)
            dve.tensor_scalar(b_clip[:, :, :], proj, -15.0, 15.0, ALU.max, ALU.min).then_inc(ev("b_clipped"), 1)
            link(dve, dve.tensor_tensor(b_z[:, :, :], proj[:, 0:4, :],
                                        dt_w.unsqueeze(2).broadcast_to([P, 4, S]), ALU.mult))
            dve.wait_ge(ev("b_clipped"), 1)
            link(dve, dve.tensor_tensor(b_z[:, :, :], b_z[:, :, :], b_clip[:, 4:8, :], ALU.mult))
            dve.wait_ge(ev("b_sigmoid"), 1)
            link(dve, dve.tensor_tensor(b_z[:, :, :], b_z[:, :, :], b_sig[:, 0:4, :], ALU.mult))
            dve.tensor_tensor(b_z[:, :, :], b_z[:, :, :], b_sig[:, 4:8, :], ALU.mult).then_inc(ev("b_gated"), 1)
            dve.wait_ge(ev("b_out"), 1)
            ins = dve.tensor_tensor(res[:, :], bank(0, D, rows=slice(0, S)), res[:, :], ALU.add)
            ins.then_inc(ev("b_done"), 1)
            dve.wait_ge(ev("b_done"), 1)

            norm("c", res[:, :], nrm[:, :])
            turned_twice("c")
            loaded(dve, "cgu")
            for e in range(C_LORA):
                for d in range(DC):
                    dve.wait_ge(ev("lora_psum"), 1 + e * DC + d)
                    dve.tensor_tensor(l0_gu[:, d, e, :], bank(2 + e * DC + d), l0_gu[:, d, e, :],
                                      ALU.add).then_inc(ev("lora_in"), 1)
            dve.wait_ge(ev("c_inh"), 1)
            dve.tensor_scalar(zone, inh, GOLDEN_LOWER, None, ALU.is_ge).then_inc(ev("c_zone"), 1)
            link(dve, dve.tensor_scalar(dist, inh, GOLDEN_CENTER, None, ALU.subtract))
            dve.scalar_tensor_tensor(dist, dist, -1.0, dist, ALU.mult, ALU.max).then_inc(ev("c_dist"), 1)
            dve.wait_ge(ev("c_zone"), 1)
            link(dve, dve.scalar_tensor_tensor(zone, inh, GOLDEN_UPPER, zone, ALU.is_le, ALU.mult))
            link(dve, dve.memset(fallback[:, C_E:14], -1.0))
            link(dve, dve.memset(taken, -1.0))
            dve.wait_ge(ev("c_exp"), 2)
            link(dve, dve.scalar_tensor_tensor(w_zone, w_zone, 1.0, zone, ALU.mult, ALU.mult, accum_out=w_sum))
            link(dve, dve.max(top, fallback))
            link(dve, dve.tensor_scalar(no_expert, w_sum, 1e-8, None, ALU.is_lt))
            link(dve, dve.tensor_copy(taken[:, 0:2], top[:, 0:2]))
            link(dve, dve.match_replace(left, taken, fallback, -2.0))
            link(dve, dve.scalar_tensor_tensor(left[:, 0:C_E], left[:, 0:C_E], -1.5, fallback[:, 0:C_E],
                                               ALU.is_lt, ALU.mult, accum_out=w_sum))
            link(dve, dve.tensor_scalar(w_sum, w_sum, 1e-8, None, ALU.max))
            link(dve, dve.reciprocal(w_sum, w_sum))
            link(dve, dve.tensor_scalar(left[:, 0:C_E], left[:, 0:C_E], w_sum, no_expert, ALU.mult, ALU.mult))
            link(dve, dve.tensor_scalar(no_expert, no_expert, -1.0, 1.0, ALU.mult, ALU.add))
            link(dve, dve.scalar_tensor_tensor(w_zone, w_zone, no_expert, left[:, 0:C_E], ALU.mult, ALU.add,
                                               accum_out=w_sum))
            link(dve, dve.tensor_scalar(w_sum, w_sum, 1e-8, None, ALU.max))
            link(dve, dve.reciprocal(w_sum, w_sum))
            for half in range(2):
                r = slice(half * S, half * S + S)
                link(dve, dve.tensor_scalar(w_c[r, :], w_zone.rearrange("p (j e) -> p e j", e=2)[r, half, :], w_sum[r, :], None, ALU.mult))
            for j in range(C_E // 2):
                dve.wait_ge(ev("c_silu"), j + 1)
                dve.scalar_tensor_tensor(c_mid[:, j, :], c_mid[:, j, :], w_c[:, C_PAIR[j]:C_PAIR[j] + 1], bank(2 + j, C_F, C_F),
                                         ALU.mult, ALU.mult).then_inc(ev("c_mid"), 1)

            def keys_low(n):
                w = min(4, NT - 4 * n) * P
                dve.wait_ge(ev("keys_high"), n + 1)
                dve.tensor_tensor(keys[L:2 * L, n * BANK:n * BANK + w], bank(n % 2, w, rows=slice(0, L)),
                                  keys[0:L, n * BANK:n * BANK + w].bitcast(F32),
                                  ALU.subtract).then_inc(ev("keys_low"), 1)

            for n in range(KEYS_FIRST):
                keys_low(n)
            loaded(dve, "cdown")
            for e in range(C_LORA):
                for d in range(DC):
                    dve.wait_ge(ev("lora_psum"), 5 + e * DC + d)
                    dve.tensor_tensor(l0_down[:, d, e, :], bank(6 + e, D, d * D), l0_down[:, d, e, :],
                                      ALU.add).then_inc(ev("lora_in"), 1)
            add_halves("c_sum", 1, 4, False)

            norm("d", res[:, :], nrm[:, :])
            for n in range(KEYS_FIRST, KGROUPS):
                keys_low(n)
            turned_twice("d", 5)
            for n in range(2):
                hs = slice(8 * n, 8 * n + 8)

                def tab(k):
                    return rope_q[:, k, :].unsqueeze(1).broadcast_to([X_HALF, 8, S])

                lo, hi = (bank(b, rows=slice(0, X_HALF)).rearrange("p (h s) -> p h s", h=8) for b in QBIG_BANK[n])
                dve.wait_ge(ev("qbig_psum"), n + 1)
                dve.tensor_tensor(q_lo[:, hs, :], lo, tab(0), ALU.mult).then_inc(ev("q_rot"), 1)
                dve.tensor_tensor(q_hi[:, hs, :], hi, tab(1), ALU.mult).then_inc(ev("q_rot"), 1)
                dve.tensor_tensor(q_hi_sin[:, hs, :], hi, tab(2), ALU.mult).then_inc(ev("q_rot"), 1)
                dve.tensor_tensor(q_lo_sin[:, hs, :], lo, tab(3), ALU.mult).then_inc(ev("q_rot"), 1)
                dve.wait_ge(ev("q_rot"), 4 * (n + 1))
                dve.tensor_tensor(q_lo[:, hs, :], q_lo[:, hs, :], q_hi_sin[:, hs, :],
                                  ALU.subtract).then_inc(ev("q_roped"), 1)
                dve.tensor_tensor(q_hi[:, hs, :], q_hi[:, hs, :], q_lo_sin[:, hs, :],
                                  ALU.add).then_inc(ev("q_roped"), 1)

            def queries_low(g):
                at_q = slice(g * GQ, (g + 1) * GQ)
                dve.wait_ge(ev("q_high"), 2 * (g + 1))
                dve.tensor_tensor(q_lm[0:L, at_q], bank(Q_BANK[g], GQ, rows=slice(0, L)),
                                  q_hh[0:L, at_q].bitcast(F32), ALU.subtract).then_inc(ev("q_low"), 1)

            queries_low(0)
            dve.memset(st_h1[L:L + 1, :].bitcast(F32), 1.0).then_inc(ev("st_ones"), 1)

            def stage(g, i, half):
                a, b = HALVES[half]
                src = bass.ds(i * CHUNK + a * P, (b - a) * P) if not isinstance(i, int) else \
                    slice(i * CHUNK + a * P, i * CHUNK + b * P)
                free = i * BODY + (g * NT - (BODY - b))
                if not isinstance(free, int) or free > 0:
                    dve.wait_ge(ev("scores"), free)
                dve.tensor_copy(st_hl[:, a * P:b * P], keys[:, src].bitcast(F32)).then_inc(ev("staged"), 1)
                dve.tensor_copy(st_h1[0:L, a * P:b * P], keys[0:L, src].bitcast(F32)).then_inc(ev("staged"), 1)

            def maximum(g, i, m):
                n = i * 2 * QT + (g * 2 * QT * NPASS + m)
                j, k = m // 2, m % 2
                dst = key_max[:, j, bass.ds(i * 2 + k, 1)] if not isinstance(i, int) else \
                    key_max[:, j, 2 * i + k:2 * i + k + 1]
                dve.wait_ge(ev("max_scores"), n + 1)
                dve.tensor_reduce(dst, bank(4 + m % 4, HALF), AX, ALU.max).then_inc(ev("key_max"), 1)

            def low(g, i, j):
                t = i * BODY + (g * NT + j)
                dve.wait_ge(ev("probs"), t + 1)
                dve.tensor_tensor(probs_l[:, SPLIT[j], :], probs[:, SLOT[j], :],
                                  probs_h[:, SPLIT[j], :].bitcast(F32), ALU.subtract).then_inc(ev("probs_low"), 1)

            def shift(g):
                dve.wait_ge(ev("key_max"), (g + 1) * 2 * QT * NPASS)
                dve.tensor_reduce(q_max[:, :], key_max[:, :, :], AX, ALU.max).then_inc(ev("q_max"), 1)
                dve.wait_ge(ev("q_max_row"), g + 1)
                dve.tensor_scalar(q_lm[L:L + 1, g * GQ:(g + 1) * GQ], bank(5, GQ, rows=slice(L, L + 1)), -1.0,
                                  None, ALU.mult).then_inc(ev("q_shift"), 1)

            for m in range(2 * QT):
                maximum(0, 0, m)
            queries_low(1)
            with dve.Fori(1, NPASS) as i:
                for m in range(2 * QT):
                    maximum(0, i, m)
            stage(0, 0, 0)
            shift(0)
            for g in range(GRP):
                def turn(i):
                    m = 0
                    for j in range(BODY):
                        if j == 1:
                            stage(g, i, 1)
                        if j == 5 and not (isinstance(i, int) and i == NPASS - 1):
                            stage(g, i + 1, 0)
                        low(g, i, j)
                        if g + 1 < GRP:
                            for _ in range(MAX_AFTER[j]):
                                maximum(g + 1, i, m)
                                m += 1

                turn(0)
                with dve.Fori(1, NPASS - 1) as i:
                    turn(i)
                turn(NPASS - 1)
                if g + 1 < GRP:
                    stage(g + 1, 0, 0)
                    shift(g + 1)

            dve.wait_ge(ev("den_psum"), 1)
            link(dve, dve.reciprocal(den_inv[:, :], bank(5, GRP * QT)))
            for g in range(GRP):
                if g:
                    dve.wait_ge(ev("den_row"), g)
                dve.tensor_tensor(den_diag[:, :, :], ident.unsqueeze(1).broadcast_to([P, QT, P]),
                                  den_inv[:, g * QT:(g + 1) * QT].unsqueeze(2).broadcast_to([P, QT, P]),
                                  ALU.mult).then_inc(ev("den_diag"), 1)
            for g in range(GRP):
                dve.wait_ge(ev("den_row"), g + 1)
                dve.tensor_tensor(ctx_n[:, g, :], bank(2 + g, GQ, rows=slice(0, L)), ctx_un[0:L, g, :],
                                  ALU.mult).then_inc(ev("ctx_n"), 1)
            add_halves("d_sum", 1, 7, False)

            norm("e", res[:, :], nrm[:, :])
            loaded(dve, "ebias")
            link(dve, dve.tensor_tensor(res[:, :], res[:, :], e_bp[:, :], ALU.add))
            turned_twice("e")
            queries("e")
            head_blocks("e")
            softmax("e")
            dve.wait_ge(ev("e_out"), 1)
            link(dve, dve.tensor_tensor(res[:, :], bank(2, D, rows=slice(0, S)), res[:, :], ALU.add))

            norm("f", res[:, :], nrm[:, :])
            turned_twice("f")
            dve.wait_ge(ev("f_logits"), 1)
            link(dve, dve.tensor_reduce(f_shift, bank(1, F_E), AX, ALU.max))
            dve.tensor_scalar(f_shift, f_shift, -1.0, None, ALU.mult).then_inc(ev("f_shift"), 1)
            dve.wait_ge(ev("f_exp"), 1)
            link(dve, dve.max(top, f_exp))
            link(dve, dve.match_replace(f_left, top, f_exp, -1.0))
            link(dve, dve.scalar_tensor_tensor(f_left, f_left, 0.0, f_exp, ALU.is_lt, ALU.mult, accum_out=w_sum))
            link(dve, dve.reciprocal(w_sum, w_sum))
            for half in range(2):
                r = slice(half * S, half * S + S)
                link(dve, dve.tensor_scalar(w_f[r, :], f_left.rearrange("p (j e) -> p e j", e=2)[r, half, :], w_sum[r, :], None, ALU.mult))

            for u in range(F_STEPS):
                b = u % 2
                dve.wait_ge(ev("f_silu"), u + 1)
                for j in range(2):
                    dve.scalar_tensor_tensor(f_mid[:, b, j, :], f_mid[:, b, j, :], w_f[:, 2 * u + j:2 * u + j + 1],
                                             bank(2 + b, F_I, (2 * j + 1) * F_I), ALU.mult,
                                             ALU.mult).then_inc(ev("f_mid"), 1)
                dve.wait_ge(ev("f_midT_psum"), u + 1)
                if u >= 2:
                    dve.wait_ge(ev("f_down"), u - 1)
                dve.tensor_copy(f_midT[:, b, :, :], bank(6 + b, 2 * P, rows=slice(0, F_I)).rearrange(
                    "p (j q) -> p j q", j=2)).then_inc(ev("f_midT"), 1)
            add_halves("f_down", F_STEPS, 0, True)

        @block.tensor
        def _(pe):
            def keep_warm(n, b):
                for _ in range(n):
                    pe.matmul(bank(b), warm_data[:, :], warm_data[:, :].unsqueeze(1).broadcast_to([P, BANK // P, P]),
                              start=True, stop=True)

            def turn_x(t, src, norm, b=0, warm=(0, 7)):
                pe.wait_ge(ev("norm"), 1 + NORMS.index(norm))
                for c in range(DC):
                    ins = pe.transpose(bank(b, S, c * S), src[:, c * P:(c + 1) * P], ident[0:S, 0:S])
                ins.then_inc(ev(t + "_xT_psum"), 1)
                keep_warm(*warm)

            def small_attention(t):
                a = att[t]
                nh, hd, pt = a["nh"], a["hd"], a["pt"]
                pairs = nh // 2
                pe.wait_ge(ev(t + "_q"), DC if t == "e" else 1)
                for c in range(DC):
                    pe.wait_ge(ev(t + "_kbd"), c + 1)
                    kc = a["kbd"][:, c, :, :].rearrange("p h k -> p (h k)")
                    for k in range(nh * S // BANK):
                        ins = pe.matmul(bank(4 + k, rows=slice(c * S, c * S + S)), qT[:, c, :],
                                        kc[:, k * BANK:(k + 1) * BANK], start=True, stop=True)
                    ins.then_inc(ev(t + "_scores"), 1)
                if t == "a":
                    fold_keys(0)
                keep_warm(W[t + "_softmax"], 3)
                pe.wait_ge(ev(t + "_exp"), 1)
                sc = a["sc"][:, :, :].rearrange("p h k -> p (h k)")
                for j in range(pairs):
                    ins = pe.transpose(bank(6, P, j * P), sc[:, j * P:(j + 1) * P], ident)
                ins.then_inc(ev(t + "_probsT_psum"), 1)
                keep_warm(W[t + "_probs"], 3)
                pe.wait_ge(ev(t + "_probsT"), 1)
                pe.wait_ge(ev(t + "_vbd"), 1)
                w = 2 * hd
                for j in range(pairs):
                    for c in range(DC):
                        ins = pe.matmul(bank(0, w, j * w, rows=slice(c * S, c * S + S)), pt[:, j, c * S:c * S + S],
                                        vbd[:, c * P + j * w:c * P + (j + 1) * w], start=True, stop=True)
                ins.then_inc(ev(t + "_o_psum"), 1)
                keep_warm(W[t + "_o"], 3)
                pe.wait_ge(ev(t + "_o"), 1)
                pe.transpose(bank(1, P), oT[:, :], ident).then_inc(ev(t + "_oT_psum"), 1)
                keep_warm(W[t + "_oT"], 3)
                pe.wait_ge(ev(t + "_oT"), 1)
                if t == "a":
                    loaded(pe, "awo")
                for c in range(DC):
                    ins = pe.matmul(bank(2, D, rows=slice(0, S)), oT[:, c * S:(c + 1) * S], a["wo"][:, c, :],
                                    start=(c == 0), stop=(c == DC - 1))
                ins.then_inc(ev(t + "_out"), 1)

            def fold_keys(n):
                half, hh = n // 2, n % 2
                r = slice(hh * S, hh * S + S)
                loaded(pe, "wr")
                for h in range(8):
                    ins = pe.matmul(bank(QK_BANK[n], L, h * L, rows=slice(0, X_HALF)),
                                    x_wqr[r, h, half * X_HALF:(half + 1) * X_HALF], x_wkr[r, h, :],
                                    start=True, stop=True)
                ins.then_inc(ev("qk_fold_psum"), 1)

            pe.wait_ge(ev("warm_data"), 1)
            keep_warm(W["start"], 7)
            loaded(pe, "actx")
            loaded(pe, "awkv")
            for c in range(DC):
                ins = pe.matmul(bank(1, S, c * S), a_wkv[:, c * P:(c + 1) * P], a_ctx[:, 0, :],
                                start=True, stop=True)
            ins.then_inc(ev("a_k_psum"), 1)
            pe.matmul(bank(2, D), a_ctx[:, :, :].rearrange("p e s -> p (e s)"), a_wkv[:, D:2 * D],
                      start=True, stop=True).then_inc(ev("a_v_psum"), 1)
            loaded(pe, "cst")
            keep_warm(W["a_norm"], 7)
            turn_x("a", nrm, "a", warm=(W["xT"], 7))
            loaded(pe, "awq")
            pe.wait_ge(ev("a_xT"), 1)
            for c in range(DC):
                for d in range(DC):
                    ins = pe.matmul(bank(3, S, c * S), a_wq[:, d, c * P:(c + 1) * P], xT[:, d, 0, :],
                                    start=(d == 0), stop=(d == DC - 1))
            ins.then_inc(ev("a_q_psum"), 1)
            small_attention("a")
            fold_keys(1)
            fold_keys(2)
            keep_warm(W["b_norm"], 7)

            turn_x("b", nrm2, "b2", warm=(W["xT"], 7))
            loaded(pe, "bw")
            pe.wait_ge(ev("b_xT"), DC)
            for e in range(2 * B_INNER // P):
                for d in range(DC):
                    ins = pe.matmul(bank(1, S, e * S), b_win[:, d, e * P:(e + 1) * P], xT[:, d, 0, :],
                                    start=(d == 0), stop=(d == DC - 1))
            ins.then_inc(ev("b_proj"), 1)
            fold_keys(3)
            keep_warm(W["b_gate"], 7)
            pe.wait_ge(ev("b_gated"), 1)
            for e in range(B_INNER // P):
                ins = pe.matmul(bank(0, D, rows=slice(0, S)), b_z[:, e, :], b_wout[:, e, :],
                                start=(e == 0), stop=(e == B_INNER // P - 1))
            ins.then_inc(ev("b_out"), 1)

            loaded(pe, "lora")
            pe.wait_ge(ev("qk_fold"), 4)
            for e in range(C_LORA):
                r = slice(e * C_R, (e + 1) * C_R)
                for d in range(DC):
                    for k in range(2):
                        ins = pe.matmul(bank(2 + e * DC + d, C_F, k * C_F),
                                        lora[r, 2 * k, d * P:(d + 1) * P], lora[r, 2 * k + 1, :],
                                        start=True, stop=True)
                    ins.then_inc(ev("lora_psum"), 1)
            for e in range(C_LORA):
                r = slice(e * C_R, (e + 1) * C_R)
                for d in range(DC):
                    pe.matmul(bank(6 + e, D, d * D), lora[r, 4, d * P:(d + 1) * P], lora[r, 5, :],
                              start=True, stop=True).then_inc(ev("lora_psum"), 1)
            turn_x("c", nrm, "c")
            pe.wait_ge(ev("c_xT"), 1)
            for d in range(DC):
                ins = pe.matmul(bank(1, C_E), xT[:, d, :, :].rearrange("p e s -> p (e s)"), c_wr[:, d, :],
                                start=(d == 0), stop=(d == DC - 1))
            ins.then_inc(ev("c_logits"), 1)
            for j in range(C_E // 2):
                pe.wait_ge(ev("lora_in"), j + 1)
                for d in range(DC):
                    for e in range(2):
                        ins = pe.matmul(bank(2 + j, rows=slice(e * S, e * S + S)), xT[:, d, 0, :],
                                        l0_gu[:, d, 2 * C_PAIR[j] + e, :], start=(d == 0), stop=(d == DC - 1))
                ins.then_inc(ev("c_gu"), 1)

            def turn_keys(n):
                if n >= 2:
                    pe.wait_ge(ev("keys_low"), n - 1)
                for t in range(4 * n, min(4 * n + 4, NT)):
                    ins = pe.transpose(bank(n % 2, P, (t % 4) * P, rows=slice(0, L)), kv[:, t, :], ident)
                ins.then_inc(ev("keysT"), 1)

            pe.wait_ge(ev("roped"), 2)
            pe.wait_ge(ev("c_inh"), 1)
            for n in range(2):
                turn_keys(n)
            for n in range(2):
                pe.wait_ge(ev("c_mid"), 2 * n + 2)
                for j in range(2 * n, 2 * n + 2):
                    for f in range(2):
                        ins = pe.transpose(bank(2 + n, P, (j % 2) * 2 * P + f * P), c_mid[:, j, f * P:(f + 1) * P],
                                           ident)
                ins.then_inc(ev("c_midT_psum"), 1)
            def fold_output(n):
                loaded(pe, "wo")
                pe.wait_ge(ev("c_midT"), 2)
                if n >= 2:
                    pe.wait_ge(ev("wo_fold"), n - 1)
                for h in range(2):
                    ins = pe.matmul(bank(2 + n % 2, D, h * D, rows=slice(0, L)), x_kckv[:, 2 * n + h, :],
                                    x_wo[:, 2 * n + h, :], start=True, stop=True)
                ins.then_inc(ev("wo_fold_psum"), 1)

            for n in range(2, KEYS_FIRST):
                turn_keys(n)
                fold_output(n - 2)
            pe.wait_ge(ev("lora_in"), 8)
            for j in range(C_E // 2):
                pe.wait_ge(ev("c_midT"), j // 2 + 1)
                for f in range(2):
                    for e in range(2):
                        ins = pe.matmul(bank(4, D, rows=slice(e * S, e * S + S)), c_midT[:, j, f, e * S:e * S + S],
                                        l0_down[:, f, 2 * C_PAIR[j] + e, :], start=(j + f == 0),
                                        stop=(j == C_E // 2 - 1 and f == 1))
            ins.then_inc(ev("c_sum"), 1)
            for n in range(KEYS_FIRST, KGROUPS):
                turn_keys(n)
                if n - 2 < X_H // 2:
                    fold_output(n - 2)
                else:
                    keep_warm(W["keys"], 7)

            turn_x("d", nrm, "d", 5, warm=(W["xT"], 7))
            loaded(pe, "wq")
            pe.wait_ge(ev("d_xT"), 1)
            for h in range(X_H):
                for d in range(DC):
                    ins = pe.matmul(bank(QHK_BANK[h // 8], S, (h % 8) * S), x_wq[:, d, h * X_K:(h + 1) * X_K],
                                    xT[:, d, 0, :], start=(d == 0), stop=(d == DC - 1))
                if h % 8 == 7:
                    ins.then_inc(ev("qhk_psum"), 1)
            loaded(pe, "kcq")
            pe.wait_ge(ev("keys_low"), KGROUPS)
            pe.wait_ge(ev("wo_fold"), X_H // 2)
            for h in range(X_H):
                if h % 8 == 0:
                    pe.wait_ge(ev("qhk"), h // 8 + 1)
                for half in range(2):
                    ins = pe.matmul(bank(QBIG_BANK[h // 8][half], S, (h % 8) * S, rows=slice(0, X_HALF)),
                                    x_kcq[:, h, half * X_HALF:(half + 1) * X_HALF], qhk[:, h, :],
                                    start=True, stop=True)
                if h % 8 == 7:
                    ins.then_inc(ev("qbig_psum"), 1)

            def last_queries(g):
                pe.wait_ge(ev("q_roped"), 2 * (g + 1))
                for h in range(g * GH, (g + 1) * GH):
                    for half, q in ((0, q_lo), (1, q_hi)):
                        ins = pe.matmul(bank(Q_BANK[g], S, (h % GH) * S, rows=slice(0, L)), x_qk[:, half, h, :],
                                        q[:, h, :], start=(half == 0), stop=(half == 1))
                ins.then_inc(ev("q_psum"), 1)

            last_queries(0)

            def max_scores(g, i, m):
                n = i * 2 * QT + (g * 2 * QT * NPASS + m)
                j, k = m // 2, m % 2
                if not isinstance(n, int) or n >= 4:
                    pe.wait_ge(ev("key_max"), n - 3)
                src = bass.ds(i * CHUNK + k * HALF, HALF) if not isinstance(i, int) else \
                    slice(i * CHUNK + k * HALF, i * CHUNK + (k + 1) * HALF)
                pe.matmul(bank(4 + m % 4, HALF), q_hh[:, g * GQ + j * P:g * GQ + (j + 1) * P], keys[:, src],
                          start=True, stop=True).then_inc(ev("max_scores"), 1)

            def max_row(g):
                pe.wait_ge(ev("q_max"), g + 1)
                for j in range(QT):
                    ins = pe.matmul(bank(5, P, j * P, rows=slice(L, L + 1)), q_max[:, j:j + 1], ident,
                                    start=True, stop=True)
                ins.then_inc(ev("q_max_row"), 1)

            pe.wait_ge(ev("q_high"), 2)
            for m in range(4):
                max_scores(0, 0, m)
            last_queries(1)
            for m in range(4, 2 * QT):
                max_scores(0, 0, m)
            with pe.Fori(1, NPASS) as i:
                for m in range(2 * QT):
                    max_scores(0, i, m)
            keep_warm(W["max"], 0)
            max_row(0)
            keep_warm(W["max_row"], 0)
            pe.wait_ge(ev("q_low"), GRP)
            for g in range(GRP):
                at_q = slice(g * GQ, (g + 1) * GQ)

                def weight(t, j, first, last):
                    acc, p_h, p_l = bank(4 * g, GQ, rows=slice(0, L + 1)), probs_h[:, SPLIT[j], :], probs_l[:, SPLIT[j], :]
                    pe.wait_ge(ev("probs_high"), t + 1)
                    pe.matmul(acc, st_kvh[:, j, :], p_h, start=first, stop=False)
                    pe.matmul(acc, st_kvl[:, j, :], p_h, start=False, stop=False)
                    pe.wait_ge(ev("probs_low"), t + 1)
                    pe.matmul(acc, st_kvh[:, j, :], p_l, start=False, stop=last).then_inc(ev("weighted"), 1)

                def passes(i):
                    first = isinstance(i, int) and i == 0
                    m = 0
                    for j in range(BODY):
                        t = i * BODY + (g * NT + j)
                        if j in (0, 4):
                            pe.wait_ge(ev("staged"), i * 4 + (g * 4 * NPASS + (2 if j == 0 else 4)))
                        if not (isinstance(t, int) and t < SLOT_AGE[j]):
                            pe.wait_ge(ev("probs"), t + (1 - SLOT_AGE[j]))
                        sc = bank(1 + SLOT[j], GQ)
                        pe.matmul(sc, st_hl[:, j * P:(j + 1) * P], q_hh[:, at_q], start=True, stop=False)
                        pe.matmul(sc, st_h1[0:L + 1, j * P:(j + 1) * P], q_lm[0:L + 1, at_q], start=False,
                                  stop=True).then_inc(ev("scores"), 1)
                        if not (first and j < LAG):
                            if (j - LAG) % BODY in (0, 4):
                                pe.wait_ge(ev("kv_staged"), i * 2 + (g * 2 * NPASS + (1 if j == LAG else 2)))
                            weight(t - LAG, (j - LAG) % BODY, first and j == LAG, False)
                        if g + 1 < GRP:
                            for _ in range(MAX_AFTER[j]):
                                max_scores(g + 1, i, m)
                                m += 1

                pe.wait_ge(ev("q_shift"), g + 1)
                if g == 0:
                    pe.wait_ge(ev("st_ones"), 1)
                    pe.wait_ge(ev("kv_ones"), 2)
                passes(0)
                with pe.Fori(1, NPASS) as i:
                    passes(i)
                for j in range(BODY - LAG, BODY):
                    weight(g * NT + NT - BODY + j, j, False, j == BODY - 1)
                if g + 1 < GRP:
                    max_row(g + 1)

            pe.wait_ge(ev("ctx_un"), GRP)
            one = cst[L:L + 1, C_ONE:C_ONE + 1]
            for n in range(GRP * QT):
                ins = pe.matmul(bank(5, 1, n), ctx_un[L:L + 1, n // QT, (n % QT) * P:(n % QT + 1) * P], one,
                                start=True, stop=True)
            ins.then_inc(ev("den_psum"), 1)
            keep_warm(W["den"], 6)
            for g in range(GRP):
                pe.wait_ge(ev("den_diag"), g + 1)
                pe.matmul(bank(2 + g, GQ, rows=slice(0, L)), cst[:, C_ONE:C_ONE + L],
                          den_diag[:, :, :].rearrange("p j q -> p (j q)"), start=True,
                          stop=True).then_inc(ev("den_row"), 1)
            for g in range(GRP):
                pe.wait_ge(ev("ctx_n"), g + 1)
                for h in range(GH):
                    r = slice((h % 2) * S, (h % 2) * S + S)
                    ins = pe.matmul(bank(7, D, rows=r), ctx_n[:, g, h * S:(h + 1) * S], x_wo[0:L, g * GH + h, :],
                                    start=(g == 0 and h < 2), stop=(g == GRP - 1 and h >= GH - 2))
            ins.then_inc(ev("d_sum"), 1)

            keep_warm(W["e_norm"], 6)
            turn_x("e", nrm, "e", warm=(W["xT"], 6))
            loaded(pe, "ew")
            pe.wait_ge(ev("e_xT"), 1)
            for name, b, col in (("q", 3, 0), ("k", 1, D)):
                for c in range(DC):
                    for d in range(DC):
                        ins = pe.matmul(bank(b, S, c * S), e_w[:, d, col + c * P:col + (c + 1) * P],
                                        xT[:, d, 0, :], start=(d == 0), stop=(d == DC - 1))
                ins.then_inc(ev(f"e_{name}_psum"), 1)
            for d in range(DC):
                ins = pe.matmul(bank(2, D), xT[:, d, :, :].rearrange("p e s -> p (e s)"), e_w[:, d, 2 * D:3 * D],
                                start=(d == 0), stop=(d == DC - 1))
            ins.then_inc(ev("e_v_psum"), 1)
            small_attention("e")

            keep_warm(W["f_norm"], 5)
            turn_x("f", nrm, "f", warm=(W["xT"], 5))
            loaded(pe, "fwr")
            pe.wait_ge(ev("f_xT"), 1)
            for d in range(DC):
                ins = pe.matmul(bank(1, F_E), xT[:, d, :, :].rearrange("p e s -> p (e s)"), f_wr[:, d, :],
                                start=(d == 0), stop=(d == DC - 1))
            ins.then_inc(ev("f_logits"), 1)
            loaded(pe, "fgu")
            loaded(pe, "fdown")

            def gate_up(u):
                if u >= 2:
                    pe.wait_ge(ev("f_mid"), 2 * u - 2)
                for j in range(2):
                    for d in range(DC):
                        for e in range(2):
                            ins = pe.matmul(bank(2 + u % 2, 2 * F_I, j * 2 * F_I, rows=slice(e * S, e * S + S)),
                                            xT[:, d, 0, :], l1_gu[:, d, 4 * u + 2 * j + e, :],
                                            start=(d == 0), stop=(d == DC - 1))
                ins.then_inc(ev("f_gu"), 1)

            def turn_mid(u):
                if u >= 2:
                    pe.wait_ge(ev("f_midT"), u - 1)
                for j in range(2):
                    pe.wait_ge(ev("f_mid"), 2 * u + j + 1)
                    ins = pe.transpose(bank(6 + u % 2, P, j * P, rows=slice(0, F_I)), f_mid[:, u % 2, j, :], ident)
                ins.then_inc(ev("f_midT_psum"), 1)

            def down(u):
                pe.wait_ge(ev("f_midT"), u + 1)
                for j in range(2):
                    for e in range(2):
                        ins = pe.matmul(bank(0, D, rows=slice(e * S, e * S + S)), f_midT[:, u % 2, j, e * S:e * S + S],
                                        l1_down[:, 4 * u + 2 * j + e, :], start=(u + j == 0),
                                        stop=(u == F_STEPS - 1 and j == 1))
                ins.then_inc(ev("f_down"), 1)

            gate_up(0)
            for u in range(F_STEPS):
                if u + 1 < F_STEPS:
                    gate_up(u + 1)
                if u:
                    down(u - 1)
                turn_mid(u)
            down(F_STEPS - 1)


def kernel(**inputs):
    import concourse.bacc as _bacc
    from concourse.bass_utils import run_bass_kernel_spmd as _run

    a = {k: np.asarray(v) for k, v in inputs.items()}

    def rows(w):
        return w.reshape((w.shape[0] // P, P) + w.shape[1:]).swapaxes(0, 1)

    def halves(w):
        n = w.shape[0] // 2
        return w.reshape(2, n, *w.shape[1:]).transpose(0, 2, 1, 3).reshape(2 * w.shape[1], n, w.shape[2])

    sin, cos = rope(CTX, L, 1)
    table = np.stack([sin, cos])
    lora = np.stack([a["L0_ffn_Ga"].swapaxes(1, 2), a["L0_ffn_Gb"], a["L0_ffn_Ua"].swapaxes(1, 2),
                     a["L0_ffn_Ub"], a["L0_ffn_Da"].swapaxes(1, 2), a["L0_ffn_Db"]], 1)
    data = {
        "x": a["x"][0],
        "cst": constants(),
        "ctx_t": a["ctx_512"][0, :S].T,
        "a_wkv": a["L0_xattn_Wkv_expand"].T,
        "a_wq": rows(a["L0_xattn_Wq"].T),
        "a_wo": rows(a["L0_xattn_Wout"].T),
        "dt": a["L0_attn_dt"],
        "columns": np.concatenate([rows(a[k]) for k in ("L0_attn_gamma", "L0_attn_beta", "L0_attn_dt")] +
                                  [rows(a["L1_attn_b_attn"][:2 * D]), rows(a["L0_ffn_Wr"]).reshape(P, DC * C_E)], 1),
        "temp": a["L0_ffn_temperature"],
        "b_win": rows(a["L0_attn_W_in"].T),
        "b_wout": rows(a["L0_attn_W_out"].T),
        "lora": lora.transpose(0, 2, 1, 3).reshape(P, 6, D),
        "c_gu": rows(np.concatenate([a["L0_ffn_Wg"], a["L0_ffn_Wu"]], 2).swapaxes(0, 1)),
        "c_down": rows(a["L0_ffn_Wd"].swapaxes(0, 1)),
        "ctx": a["ctx_512"][0].reshape(P, NT, L),
        "rope": table.reshape(2, P, NT, L // 2).swapaxes(0, 1),
        "x_wqr": halves(a["L1_xattn_W_qr"].swapaxes(1, 2)),
        "x_wkr": halves(a["L1_xattn_W_kr"].swapaxes(1, 2)),
        "x_kckv": a["L1_xattn_w_kc_kv"].swapaxes(0, 1),
        "x_wo": rows(a["L1_xattn_Wo"].T),
        "x_wq": rows(a["L1_xattn_Wq"].T),
        "x_kcq": a["L1_xattn_w_kc_q"].swapaxes(0, 1),
        "f_wr": rows(a["L1_ffn_router_w"].T),
        "e_b": a["L1_attn_b_attn"],
        "e_bp": a["L1_attn_b_proj"],
        "e_w": rows(a["L1_attn_W_attn"]),
        "e_wp": rows(a["L1_attn_W_proj"]),
        "f_gu": rows(np.concatenate([a["L1_ffn_w_gate"], a["L1_ffn_w_up"]], 2).swapaxes(0, 1)),
        "f_down": a["L1_ffn_w_down"].swapaxes(0, 1),
    }
    data = {k: np.ascontiguousarray(v) for k, v in data.items()}
    nc = _bacc.Bacc("TRN2", target_bir_lowering=False, num_devices=1)
    dram = {k: nc.dram_tensor(k, v.shape, F32, kind="ExternalInput").ap() for k, v in data.items()}
    out = nc.dram_tensor("out", (S, D), F32, kind="ExternalOutput").ap()
    build(nc, dram, out)
    r = _run(nc, [data], core_ids=[0])
    return r.results[0]["out"].reshape(1, S, D)
```

```python
from contextlib import ExitStack
import math

import numpy as np

import concourse.bass as bass
from concourse import mybir

F32 = mybir.dt.float32
F32R = mybir.dt.float32r
BF16 = mybir.dt.bfloat16
ALU = mybir.AluOpType
ACT = mybir.ActivationFunctionType
AX = mybir.AxisListType.X

P = 128
S = 64
D = 256
DC = D // P
EPS = 1e-5
FMAX = float(np.finfo(np.float32).max)
HUGE = 1e30

A_HD, A_NH = 16, 16
B_INNER = 512
C_E, C_F, C_R, C_LORA = 8, 256, 64, 2
GOLDEN_CENTER = 1.0 / math.e
GOLDEN_LOWER = 0.5 - math.log(4.0 / 3.0)
GOLDEN_UPPER = 0.5
CTX, L = 6272, 64
NT = CTX // P
X_H, X_K, X_CQ, X_R = 16, 128, 192, 64
X_HALF = X_CQ // 2
E_HD, E_NH = 8, 32
F_E, F_K, F_I = 32, 8, 96

GRP = 2
GH = X_H // GRP
GQ = GH * S
QT = GQ // P
BODY = 7
NPASS = NT // BODY
KGROUPS = -(-NT // 4)
KEYS_FIRST = 4
KEYS_HALF = 8
KEYS_LAST = 11
CHUNK = BODY * P
HALF = CHUNK // 2
HALVES = ((0, 4), (4, BODY))
F_STEPS = F_E // 4
BANK = 512

C_ID, C_ADDA, C_CAPA, C_ADDE, C_CAPE, C_PAR, C_BLKA, C_BLKE, C_ROPE, C_ONE, C_NH = (
    0, 128, 192, 256, 320, 384, 386, 394, 410, 666, 667)
C_N = 672


def constants():
    c = np.zeros((P, C_N), np.float32)
    p = np.arange(P)
    row = p % S
    col = np.arange(S)
    seen = col[None, :] <= row[:, None]
    c[:, C_ID:C_ID + P] = np.eye(P)
    c[:, C_ADDA:C_ADDA + S] = np.where(seen, 0.0, HUGE)
    c[:, C_CAPA:C_CAPA + S] = np.where(seen, FMAX, -FMAX)
    slope = 2.0 ** (-(8.0 / E_NH))
    c[:, C_ADDE:C_ADDE + S] = np.where(seen, (col[None, :] - row[:, None]) * slope, HUGE)
    c[:, C_CAPE:C_CAPE + S] = np.where(seen, FMAX, -10000.0)
    c[:, C_PAR] = p < S
    c[:, C_PAR + 1] = p >= S
    c[:, C_BLKA:C_BLKA + 8] = (p[:, None] // A_HD) == np.arange(8)[None, :]
    c[:, C_BLKE:C_BLKE + 16] = (p[:, None] // E_HD) == np.arange(16)[None, :]
    sin, cos = rope(S, X_CQ)
    for n, t in enumerate((cos[:, :X_HALF], cos[:, X_HALF:], sin[:, :X_HALF], sin[:, X_HALF:])):
        c[:X_HALF, C_ROPE + n * S:C_ROPE + (n + 1) * S] = t.T
    c[:, C_ONE] = 1.0
    c[:, C_NH] = -0.5
    return c


def rope(length, dim, each=2):
    inv = (1.0 / np.float32(10000.0) ** (np.arange(0, dim, 2, dtype=np.float32) / np.float32(dim)))
    f = np.arange(length, dtype=np.float32)[:, None] * inv.astype(np.float32)[None, :]
    return (np.repeat(np.sin(f), each, axis=-1).astype(np.float32),
            np.repeat(np.cos(f), each, axis=-1).astype(np.float32))


SLOT = (0, 1, 2, 0, 1, 2, 1)
SLOT_AGE = (4, 2, 4, 3, 3, 3, 2)
SPLIT = (0, 1, 2, 3, 0, 1, 2)
SPLIT_AGE = (3, 3, 3, 7, 4, 4, 4)
C_PAIR = (1, 2, 3, 0)
QK_BANK = (5, 3, 4, 5)
QHK_BANK = (6, 7)
QBIG_BANK = ((2, 3), (3, 0))
Q_BANK = (2, 3)
PEELED = 4
FOLD_BEFORE = tuple(8 + 5 * k // 2 for k in range(X_H // 2))
QUERIES_BEFORE = 29
FOLD_BANK = (1, 2)
MAX_BANK = (6, 7, 4, 5)
LOW_POOL = (3, 4)
LAG = 2
MAX_AFTER = (1, 1, 1, 1, 2, 1, 1)

NORMS = ("a", "b", "b2", "c", "d", "e", "f")



def low_parts(g, i, j):
    if g == 0 and j in LOW_POOL:
        return "probs_low_pool", i * len(LOW_POOL) + (LOW_POOL.index(j) + 1)
    each = BODY - len(LOW_POOL)
    if g == 0:
        return "probs_low", i * each + (1 + sum(k not in LOW_POOL for k in range(j)))
    return "probs_low", i * BODY + (each * NPASS + j + 1)


W = dict(start=11, xT=3, d_xT=6, a_softmax=3, a_probs=3, a_o=2, a_oT=2, b_norm=9, b_gate=4, c_norm=12,
         max=6, next_max=5, d_norm=10, max_row=1, e_norm=5, e_xT=2, e_softmax=14, e_probs=1, e_o=2, e_oT=2, f_norm=11)

LOADS = dict(x=1, cst=1, actx=2, awkv=1, awq=1, awo=1, b=3, bw=2, cgu_first=1, lora=3, cgu=1, cdown=1, ctx=1,
             rope=1, wr=2, wo=2, wq=1, kcq=1, fwr=1, ebias=2, ew=2, fgu=1, fdown=1)


def build(nc, dram, out):
    with ExitStack() as ctx:
        base = -(-nc.sbuf_base // 64) * 64
        width = (nc.sbuf_usable_end - base) // 4 - 16
        ctx.enter_context(nc.sbuf_tensor("arena", [P, width], F32))

        def at(name, col, shape, dtype=F32):
            assert col + math.prod(shape[1:]) <= width, name
            return nc.alloc_sbuf_tensor_at(name, shape, dtype, offset=base + 4 * col)

        R1 = 0
        R2 = 12288
        R3 = 20480
        R4 = 24576
        R5 = 26624
        R6 = 32896
        R7 = 36096
        R8 = 42368
        R9 = 45952
        R10 = 49024
        VEC = R10 + C_N + 3 * D + 2 * P
        WORK = VEC + 512

        l0_gu = at("l0_gu", R1, [P, DC, C_E, 2 * C_F])
        l0_down = at("l0_down", R1 + 8192, [P, DC, C_E, D])
        qhk = at("qhk", R1, [P, X_H, S])
        q_lo = at("q_lo", R1 + 1024, [X_HALF, X_H, S])
        q_hi = at("q_hi", R1 + 2048, [X_HALF, X_H, S])
        q_lo_sin = at("q_lo_sin", R1 + 3072, [X_HALF, X_H, S])
        q_hi_sin = at("q_hi_sin", R1 + 4096, [X_HALF, X_H, S])
        q_full = at("q_full", R1 + 6144, [L, GRP, GQ])
        q_wide = at("q_wide", R1 + 5120, [X_HALF, 2, GH, S])
        l1_gu = at("l1_gu", R1, [P, DC, F_E // 2, 4 * F_I])
        x_wq = at("x_wq", R2, [P, DC, X_H * X_K])
        x_kcq = at("x_kcq", R2 + 4096, [P, X_H, X_CQ])
        x_kckv = at("x_kckv", R2 + 7168, [P, X_H, L])
        l1_down = at("l1_down", R2, [F_I, F_E, D])
        x_wo = at("x_wo", R3, [P, X_H, D])
        att_a = dict(kbd=at("kbd_a", R4, [P, DC, 8, S]), sc=at("sc_a", R4 + 1024, [P, 8, S]),
                     pt=at("pt_a", R4 + 1536, [P, 4, P]))
        x_qk = at("x_qk", R4, [X_HALF, 2, X_H, L])
        e_w = at("e_w", R4, [P, DC, 3 * D])
        e_wp = at("e_wp", R4 + 1536, [P, DC, D])
        turned = at("turned", R5, [P, NT, L])
        a_wq = at("a_wq", R5 + 3136, [P, DC, D])
        a_wkv = at("a_wkv", R5 + 3648, [L, 2 * D])
        a_wo = at("a_wo", R5 + 4160, [P, DC, D])
        a_ctx = at("a_ctx", R5 + 4672, [L, 2, S])
        dt_row = at("dt_row", R5 + 4800, [P, B_INNER])
        keys = at("keys", R5, [P, CTX], F32R)
        att_e = dict(kbd=at("kbd_e", R5, [P, DC, 16, S]), sc=at("sc_e", R5 + 2048, [P, 16, S]),
                     pt=at("pt_e", R5 + 3072, [P, 8, P]))
        f_mid = at("f_mid", R5 + 4096, [P, 2, 2, F_I])
        f_midT = at("f_midT", R5 + 4480, [F_I, 2, 2, P])
        kv = at("kv", R6, [P, NT, L])
        ctx_sb = at("ctx_sb", R7, [P, NT, L])
        rope_sb = at("rope_sb", R7 + 3136, [P, 2, NT, L // 2])
        probs = at("probs", R7, [P, 3, GQ])
        st_hl = at("st_hl", R7 + 1536, [P, CHUNK], F32R)
        st_h1 = at("st_h1", R7 + 2432, [P, CHUNK], F32R)
        q_hh = at("q_hh", R7 + 3328, [P, X_H * S], F32R)
        q_lm = at("q_lm", R7 + 4352, [P, X_H * S], F32R)
        probs_h = at("probs_h", R7 + 5376, [P, 4, GQ], F32R)
        probs_l = at("probs_l", R7 + 7424, [P, 4, GQ], F32R)
        x_wqr = at("x_wqr", R8, [P, X_H // 2, X_CQ])
        x_wkr = at("x_wkr", R8 + 1536, [P, X_H // 2, L])
        lora_in = at("lora_in", R8 + 2048, [P, DC, C_LORA, 2, C_R])
        lora_mid = at("lora_mid", R8 + 2560, [P, DC, C_LORA, C_R])
        lora_out = at("lora_out", R8 + 2816, [P, 3, D])
        c_mid = at("c_mid", R8, [P, 4, C_F])
        c_midT = at("c_midT", R8 + 1024, [P, 4, 2, P])
        b_win = at("b_win", R9, [P, DC, 2 * B_INNER])
        b_wout = at("b_wout", R9 + 2048, [P, B_INNER // P, D])
        ctx_un = at("ctx_un", R9, [L + 1, GRP, GQ])
        ctx_n = at("ctx_n", R9 + 1024, [L, GRP, GQ])
        key_max = at("key_max", R9 + 2560, [P, QT, 2 * NPASS])
        q_max = at("q_max", R9 + 2616, [P, QT])
        q_max_split = at("q_max_split", R9 + 2632, [P, QT, 2], F32R)
        den_inv = at("den_inv", R9 + 2624, [P, QT])
        f_wr = at("f_wr", R9 + 2640, [P, DC, F_E])
        e_bv = at("e_bv", R9 + 2704, [P, D])

        cst = at("cst", R10, [P, C_N])
        res = at("res", R10 + C_N, [S, D])
        nrm = at("nrm", R10 + C_N + D, [S, D])
        nrm2 = at("nrm2", R10 + C_N + 2 * D, [S, D])
        xT = at("xT", R10 + C_N + 3 * D, [P, DC, 2, S])
        vec = at("vec", VEC, [P, 512])
        b_clip = at("b_clip", WORK, [P, 8, S])
        b_sig = at("b_sig", WORK + 512, [P, 8, S])
        b_z = at("b_z", WORK + 1024, [P, 4, S])
        st_kvh = at("st_kvh", WORK, [P, BODY, L + 1], F32R)
        st_kv = at("st_kv", WORK + 1024, [P, BODY, L])
        st_kvl = at("st_kvl", WORK + 512, [P, BODY, L + 1], F32R)
        vbd = at("vbd", WORK + 1280, [P, D])
        lora_x = at("lora_x", WORK + 1280, [P, 2, S])
        lora_m = at("lora_m", WORK + 1408, [P, S])
        oT = at("oT", WORK + 1536, [P, P])
        e_bp = at("e_bp", WORK + 1664, [S, D])

        warm_data = at("warm_data", R6 + NT * L, [P, P], BF16)

        ident = cst[:, C_ID:C_ID + P]
        rope_q = cst[0:X_HALF, C_ROPE:C_ROPE + 4 * S].rearrange("p (n s) -> p n s", n=4)

        used = [0]

        def cols(w, rows=P):
            used[0] += w
            assert used[0] <= 512
            return vec[0:rows, used[0] - w:used[0]]

        stats, mean_var, var_eps, rstd = cols(6, S), cols(2, S), cols(1, S), cols(1, S)
        qT = cols(DC * S).rearrange("p (c s) -> p c s", c=DC)
        row_max, row_sum, row_inv = cols(16), cols(16), cols(16)
        columns = cols(2 * DC + 4 + 2 * DC + DC * C_E)
        gamma, beta, dt_col = columns[:, 0:DC], columns[:, DC:2 * DC], columns[:, 2 * DC:2 * DC + 4]
        e_bias = columns[:, 2 * DC + 4:4 * DC + 4]
        c_wr = columns[:, 4 * DC + 4:].rearrange("p (c e) -> p c e", c=DC)
        dt_e, dt_w = cols(4), cols(4)
        dt_min, dt_sum, dt_inv = cols(1), cols(1), cols(1)
        temp, temp_inv = cols(1), cols(1)
        inh, zone, dist, w_zone, fallback = cols(8), cols(8), cols(8), cols(8), cols(14)
        top, taken, left = cols(8), cols(8), cols(14)
        w_sum, no_expert, w_c = cols(1), cols(1), cols(4)
        f_exp, f_left, w_f = cols(F_E), cols(F_E), cols(F_E // 2)
        f_shift = cols(1)

        ps = ctx.enter_context(nc.psum_tensor("ps", [P, 8 * BANK], F32))

        def bank(b, n=BANK, start=0, rows=slice(0, P)):
            return ps[rows, b * BANK + start:b * BANK + start + n]

        sems = {}

        def ev(name):
            if name not in sems:
                sems[name] = ctx.enter_context(nc.semaphore(name))
            return sems[name]

        def loaded(eng, name):
            eng.wait_ge(ev("ld_" + name), 16 * LOADS[name])

        steps = {"dve": 0}

        def mark(ins):
            steps["dve"] += 1
            ins.then_inc(ev("dve_step"), 1)
            return steps["dve"]

        def link(eng, ins):
            eng.wait_ge(ev("dve_step"), mark(ins))

        att = {
            "a": dict(att_a, hd=A_HD, nh=8, blk=C_BLKA, add=C_ADDA, cap=C_CAPA, scale=A_HD ** -0.5, wo=a_wo),
            "e": dict(att_e, hd=E_HD, nh=16, blk=C_BLKE, add=C_ADDE, cap=C_CAPE,
                      scale=float(np.float32(1.0) / np.sqrt(np.float32(E_HD))), wo=e_wp),
        }

        block = ctx.enter_context(nc.Block())

        @block.sync
        def _(sp):
            def load(name, dst, src):
                sp.dma_start(dst, src).then_inc(ev("ld_" + name), 16)

            load("x", res[:, :], dram["x"])
            load("cst", cst[:, :], dram["cst"])
            load("actx", a_ctx[:, 0, :], dram["ctx_t"])
            load("actx", a_ctx[:, 1, :], dram["ctx_t"])
            load("awkv", a_wkv[:, :], dram["a_wkv"])
            load("awq", a_wq[:, :, :], dram["a_wq"])
            load("b", dt_row[:, :], dram["dt"].partition_broadcast(P))
            load("b", columns, dram["columns"])
            load("b", temp, dram["temp"].partition_broadcast(P))
            load("awo", a_wo[:, :, :], dram["a_wo"])
            load("wr", x_wqr[:, :, :], dram["x_wqr"])
            load("wr", x_wkr[:, :, :], dram["x_wkr"])
            load("bw", b_win[:, :, :], dram["b_win"])
            load("bw", b_wout[:, :, :], dram["b_wout"])
            load("ctx", ctx_sb[:, :, :], dram["ctx"])
            load("rope", rope_sb[:, :, :, :], dram["rope"])
            load("cgu_first", l0_gu[:, :, 0:C_E // 2, :], dram["c_gu"][:, :, 0:C_E // 2, :])
            load("lora", lora_in[:, :, :, :, :], dram["lora_in"])
            load("lora", lora_mid[:, :, :, :], dram["lora_mid"])
            load("lora", lora_out[:, :, :], dram["lora_out"])
            load("cgu", l0_gu[:, :, C_E // 2:C_E, :], dram["c_gu"][:, :, C_E // 2:C_E, :])
            load("cdown", l0_down[:, :, :, :], dram["c_down"])
            load("wq", x_wq[:, :, :], dram["x_wq"])
            load("kcq", x_kcq[:, :, :], dram["x_kcq"])
            load("wo", x_kckv[:, :, :], dram["x_kckv"])
            load("wo", x_wo[:, :, :], dram["x_wo"])
            sp.wait_ge(ev("b_done"), 1)
            load("fwr", f_wr[:, :, :], dram["f_wr"])
            load("ebias", e_bv[:, :], dram["e_b"][2 * D:3 * D].partition_broadcast(P))
            load("ebias", e_bp[:, :], dram["e_bp"].partition_broadcast(S))
            sp.wait_ge(ev("q_low"), GRP)
            sp.wait_ge(ev("wo_fold_psum"), X_H // 2)
            load("ew", e_w[:, :, :], dram["e_w"])
            load("ew", e_wp[:, :, :], dram["e_wp"])
            load("fgu", l1_gu[:, :, :, :], dram["f_gu"])
            load("fdown", l1_down[:, :, :], dram["f_down"])
            sp.wait_ge(ev("result"), 1)
            sp.dma_start(out, res[:, :]).then_inc(ev("stored"), 16)
            sp.wait_ge(ev("stored"), 16)

        @block.gpsimd
        def _(pool):
            def norm_scale(t):
                pool.wait_ge(ev("variance"), 1 + NORMS.index(t))
                pool.tensor_tensor(rstd, var_eps, cst[0:S, C_NH:C_NH + 1], ALU.pow).then_inc(ev("rstd"), 1)

            loaded(pool, "cst")
            norm_scale("a")
            norm_scale("b")
            norm_scale("b2")
            loaded(pool, "ctx")
            loaded(pool, "rope")
            half = L // 2
            pairs = ctx_sb[:, :, :].rearrange("p t (f e) -> p t f e", e=2)
            sin, cos = rope_sb[:, 0, :, :], rope_sb[:, 1, :, :]
            pool.tensor_tensor(kv[:, :, :].rearrange("p t (f e) -> p t f e", e=2), pairs,
                               cos.unsqueeze(3).broadcast_to([P, NT, half, 2]), ALU.mult).then_inc(ev("rope_cos"), 1)
            for a, b in ((0, half), (half, 0)):
                pool.tensor_tensor(
                    turned[:, :, a:a + half].rearrange("p t (f e) -> p t f e", e=2),
                    ctx_sb[:, :, b:b + half].rearrange("p t (f e) -> p t f e", e=2),
                    sin[:, :, a // 2:a // 2 + half // 2].unsqueeze(3).broadcast_to([P, NT, half // 2, 2]),
                    ALU.mult).then_inc(ev("rope_sin"), 1)
                if a == 0:
                    norm_scale("c")
            pool.wait_ge(ev("rope_cos"), 1)
            pool.wait_ge(ev("rope_sin"), 2)
            pool.tensor_tensor(kv[:, :, 0:half], kv[:, :, 0:half], turned[:, :, 0:half],
                               ALU.subtract).then_inc(ev("roped"), 1)
            pool.tensor_tensor(kv[:, :, half:L], kv[:, :, half:L], turned[:, :, half:L],
                               ALU.add).then_inc(ev("roped"), 1)
            norm_scale("d")

            def stage_kv(g, i, half):
                a, b = HALVES[half]
                n = i * 2 + (g * 2 * NPASS + half)
                src = kv[:, bass.ds(i * BODY + a, b - a), :] if not isinstance(i, int) else \
                    kv[:, i * BODY + a:i * BODY + b, :]
                free = i * BODY + (g * NT - (BODY - b))
                if not isinstance(free, int) or free > 0:
                    pool.wait_ge(ev("weighted"), free)
                pool.tensor_copy(st_kv[:, a:b, :], src).then_inc(ev("kv_staging"), 1)
                pool.tensor_copy(st_kvh[:, a:b, 0:L], src).then_inc(ev("kv_staging"), 1)
                pool.wait_ge(ev("kv_staging"), 2 * n + 2)
                pool.tensor_tensor(st_kvl[:, a:b, 0:L], st_kv[:, a:b, :], st_kvh[:, a:b, 0:L].bitcast(F32),
                                   ALU.subtract).then_inc(ev("kv_staged"), 1)

            pool.wait_ge(ev("b_done"), 1)
            pool.memset(st_kvh[:, :, L:L + 1].bitcast(F32), 1.0).then_inc(ev("kv_ones"), 1)
            pool.memset(st_kvl[:, :, L:L + 1].bitcast(F32), 0.0).then_inc(ev("kv_ones"), 1)

            def pool_low(i, j):
                pool.wait_ge(ev("probs"), i * BODY + (j + 1))
                pool.tensor_tensor(probs_l[:, SPLIT[j], :], probs[:, SLOT[j], :], probs_h[:, SPLIT[j], :].bitcast(F32),
                                   ALU.subtract).then_inc(ev("probs_low_pool"), 1)

            stage_kv(0, 0, 0)
            stage_kv(0, 0, 1)
            def queries_low(g):
                at_q = slice(g * GQ, (g + 1) * GQ)
                pool.wait_ge(ev("q_full"), g + 1)
                pool.tensor_tensor(q_lm[0:L, at_q], q_full[:, g, :], q_hh[0:L, at_q].bitcast(F32),
                                   ALU.subtract).then_inc(ev("q_low"), 1)

            queries_low(0)
            hs = slice(GH, 2 * GH)
            pool.wait_ge(ev("q_wide"), 2)
            for dst, half, k in ((q_lo, 0, 0), (q_hi_sin, 1, 2), (q_hi, 1, 1), (q_lo_sin, 0, 3)):
                pool.tensor_tensor(dst[:, hs, :], q_wide[:, half, :, :],
                                   rope_q[:, k, :].unsqueeze(1).broadcast_to([X_HALF, GH, S]),
                                   ALU.mult).then_inc(ev("q_rot_pool"), 1)
            pool.wait_ge(ev("q_rot_pool"), 4)
            pool.tensor_tensor(q_lo[:, hs, :], q_lo[:, hs, :], q_hi_sin[:, hs, :],
                               ALU.subtract).then_inc(ev("q_roped"), 1)
            pool.tensor_tensor(q_hi[:, hs, :], q_hi[:, hs, :], q_lo_sin[:, hs, :],
                               ALU.add).then_inc(ev("q_roped"), 1)

            queries_low(1)

            for j in LOW_POOL:
                pool_low(0, j)
            with pool.Fori(1, NPASS) as i:
                stage_kv(0, i, 0)
                stage_kv(0, i, 1)
                for j in LOW_POOL:
                    pool_low(i, j)
            for half in range(2):
                stage_kv(1, 0, half)
            with pool.Fori(1, NPASS) as i:
                for half in range(2):
                    stage_kv(1, i, half)
            norm_scale("e")
            norm_scale("f")

        @block.scalar
        def _(act):
            def softmax_exp(t):
                sc, nh = att[t]["sc"], att[t]["nh"]
                for u in range(2):
                    hs = slice(u * nh // 2, (u + 1) * nh // 2)
                    act.wait_ge(ev(t + "_shifted"), u + 1)
                    act.activation(sc[:, hs, :], sc[:, hs, :], ACT.Exp).then_inc(ev(t + "_exp"), 1)

            def probs_turned(t):
                pairs = att[t]["nh"] // 2
                for u in range(2):
                    act.wait_ge(ev(t + "_probsT_psum"), u + 1)
                    act.activation(att[t]["pt"][:, u * pairs // 2:(u + 1) * pairs // 2, :],
                                   bank(6 + u, pairs // 2 * P).rearrange("p (j q) -> p j q", j=pairs // 2),
                                   ACT.Copy).then_inc(ev(t + "_probsT"), 1)

            act.wait_ge(ev("dt_min"), 1)
            act.activation(dt_e, dt_col, ACT.Exp, bias=dt_min, scale=-1.0).then_inc(ev("dt_exp"), 1)
            act.activation(dt_row[:, :], dt_row[:, :], ACT.Exp, bias=dt_min, scale=-1.0,
                           accum_out=dt_sum).then_inc(ev("dt_exp"), 1)
            softmax_exp("a")
            act.preload_act_table(ACT.Sigmoid)
            probs_turned("a")
            for n in range(4):
                if n == 3:
                    act.wait_ge(ev("b_clipped"), 1)
                    act.activation(b_sig[:, :, :], b_clip[:, :, :], ACT.Sigmoid).then_inc(ev("b_sigmoid"), 1)
                act.wait_ge(ev("qk_fold_psum"), n + 1)
                act.activation(x_qk[:, n // 2, 8 * (n % 2):8 * (n % 2) + 8, :],
                               bank(QK_BANK[n], rows=slice(0, X_HALF)).rearrange("p (h d) -> p h d", h=8),
                               ACT.Copy).then_inc(ev("qk_fold"), 1)

            act.wait_ge(ev("c_logits"), 1)
            act.wait_ge(ev("temp_inv"), 1)
            act.activation(inh, bank(1, C_E), ACT.Sigmoid, scale=temp_inv).then_inc(ev("c_inh"), 1)
            act.preload_act_table(ACT.Exp)
            act.wait_ge(ev("c_dist"), 1)
            act.activation(w_zone, dist, ACT.Exp, scale=-1.0 / 0.1).then_inc(ev("c_exp"), 1)
            act.activation(fallback[:, 0:C_E], dist, ACT.Exp, scale=-1.0 / 0.3).then_inc(ev("c_exp"), 1)
            act.preload_act_table(ACT.Silu)
            act.wait_ge(ev("qk_fold_psum"), 4)
            for j in range(C_E // 2):
                if j == C_E // 2 - 1:
                    act.wait_ge(ev("lora_x_psum"), 1)
                    act.activation(lora_x[:, :, :], bank(6, 2 * S).rearrange("p (q s) -> p q s", q=2),
                                   ACT.Copy).then_inc(ev("lora_x"), 1)
                act.wait_ge(ev("c_gu"), j + 1)
                act.activation(c_mid[:, j, :], bank(2 + j, C_F), ACT.Silu).then_inc(ev("c_silu"), 1)
            def keys_high(n):
                w = min(4, NT - 4 * n) * P
                act.wait_ge(ev("keysT"), n + 1)
                act.activation(keys[0:L, n * BANK:n * BANK + w], bank(n % 2, w, rows=slice(0, L)),
                               ACT.Copy).then_inc(ev("keys_high"), 1)

            for n in range(2):
                act.wait_ge(ev("c_midT_psum"), n + 1)
                act.activation(c_midT[:, 2 * n:2 * n + 2, :, :],
                               bank(2 + n).rearrange("p (j f q) -> p j f q", j=2, f=2),
                               ACT.Copy).then_inc(ev("c_midT"), 1)
            act.wait_ge(ev("lora_m_psum"), 1)
            act.activation(lora_m[:, :], bank(7, S), ACT.Copy).then_inc(ev("lora_m"), 1)
            for n in range(KEYS_HALF - 1):
                keys_high(n)
            for n in range(2):
                act.wait_ge(ev("qhk_psum"), n + 1)
                act.activation(qhk[:, 8 * n:8 * n + 8, :], bank(QHK_BANK[n]).rearrange("p (h s) -> p h s", h=8),
                               ACT.Copy).then_inc(ev("qhk"), 1)
                if n == 0:
                    for k in range(KEYS_HALF - 1, KEYS_LAST):
                        keys_high(k)

            def queries_high(g):
                q, at_q = bank(Q_BANK[g], GQ, rows=slice(0, L)), slice(g * GQ, (g + 1) * GQ)
                act.wait_ge(ev("q_psum"), g + 1)
                act.activation(q_hh[0:L, at_q], q, ACT.Copy).then_inc(ev("q_high"), 1)
                if g:
                    act.activation(q_hh[L:2 * L, at_q], q, ACT.Copy).then_inc(ev("q_high_twice"), 1)

            def queries_full(g):
                act.activation(q_full[:, g, :], bank(Q_BANK[g], GQ, rows=slice(0, L)),
                               ACT.Copy).then_inc(ev("q_full"), 1)

            queries_high(0)
            for n in range(KEYS_LAST, KGROUPS):
                keys_high(n)
            queries_full(0)
            act.wait_ge(ev("qbig_psum"), 2)
            for half in range(2):
                act.activation(q_wide[:, half, :, :],
                               bank(QBIG_BANK[1][half], rows=slice(0, X_HALF)).rearrange("p (h s) -> p h s", h=GH),
                               ACT.Copy).then_inc(ev("q_wide"), 1)
            for n in range(X_H // 2):
                act.wait_ge(ev("wo_fold_psum"), n + 1)
                act.activation(x_wo[0:L, 2 * n:2 * n + 2, :],
                               bank(FOLD_BANK[n % 2], rows=slice(0, L)).rearrange("p (h d) -> p h d", h=2),
                               ACT.Copy).then_inc(ev("wo_fold"), 1)
            queries_high(1)
            queries_full(1)

            act.preload_act_table(ACT.Exp)
            for g in range(GRP):
                def exps(i):
                    for j in range(BODY):
                        t = i * BODY + (g * NT + j)
                        scores = bank(1 + SLOT[j], GQ)
                        act.wait_ge(ev("scores"), t + 1)
                        if not (isinstance(t, int) and t < SPLIT_AGE[j]):
                            act.wait_ge(ev("weighted"), t + (1 - SPLIT_AGE[j]))
                        act.activation(probs_h[:, SPLIT[j], :], scores, ACT.Exp).then_inc(ev("probs_high"), 1)
                        if not (isinstance(t, int) and t < SLOT_AGE[j]):
                            last = j - SLOT_AGE[j]
                            if last >= 0:
                                name, n = low_parts(g, i, last)
                            elif isinstance(i, int) and i == 0:
                                name, n = low_parts(g - 1, NPASS - 1, last + BODY)
                            else:
                                name, n = low_parts(g, i - 1, last + BODY)
                            act.wait_ge(ev(name), n)
                        act.activation(probs[:, SLOT[j], :], scores, ACT.Exp).then_inc(ev("probs"), 1)

                exps(0)
                with act.Fori(1, NPASS) as i:
                    exps(i)
                act.wait_ge(ev("weighted"), (g + 1) * NT)
                act.activation(ctx_un[:, g, :], bank(4 * g, GQ, rows=slice(0, L + 1)),
                               ACT.Copy).then_inc(ev("ctx_un"), 1)

            softmax_exp("e")
            probs_turned("e")

            act.wait_ge(ev("f_shift"), 1)
            act.activation(f_exp, bank(1, F_E), ACT.Exp, bias=f_shift).then_inc(ev("f_exp"), 1)
            act.preload_act_table(ACT.Silu)

            for u in range(F_STEPS):
                b = u % 2
                act.wait_ge(ev("f_gu"), u + 1)
                if u >= 2:
                    act.wait_ge(ev("f_midT_psum"), u - 1)
                gates = bank(2 + b, 4 * F_I).rearrange("p (j g f) -> p j g f", j=2, g=2)[:, :, 0, :]
                act.activation(f_mid[:, b, :, :], gates, ACT.Silu).then_inc(ev("f_silu"), 1)

        @block.vector
        def _(dve):
            def norm(t, src, dst):
                link(dve, dve.bn_stats(stats, src))
                link(dve, dve.bn_aggr(mean_var, stats))
                dve.tensor_scalar(var_eps, mean_var[:, 1:2], EPS, None, ALU.add).then_inc(ev("variance"), 1)
                dve.wait_ge(ev("rstd"), 1 + NORMS.index(t))
                dve.tensor_scalar(dst, src, mean_var[:, 0:1], rstd, ALU.subtract,
                                  ALU.mult).then_inc(ev("norm"), 1)

            def turned_twice(t, b=0):
                dve.wait_ge(ev(t + "_xT_psum"), 1)
                src = bank(b, 2 * S).rearrange("p (c s) -> p c s", c=DC).unsqueeze(2)
                dve.tensor_copy(xT[:, :, :, :], src.broadcast_to([P, DC, 2, S])).then_inc(ev(t + "_xT"), 1)

            def key_blocks(t, c):
                a = att[t]
                nh = a["nh"]
                blk = cst[:, a["blk"]:a["blk"] + nh].unsqueeze(2).broadcast_to([P, nh, S])
                dve.wait_ge(ev(t + "_k_psum"), 1)
                k = bank(1, S, c * S).unsqueeze(1).broadcast_to([P, nh, S])
                if t == "e":
                    ins = dve.scalar_tensor_tensor(a["kbd"][:, c, :, :], k, e_bias[:, DC + c:DC + c + 1], blk,
                                                   ALU.add, ALU.mult)
                else:
                    ins = dve.tensor_tensor(a["kbd"][:, c, :, :], k, blk, ALU.mult)
                ins.then_inc(ev(t + "_kbd"), 1)

            def value_blocks(t):
                nh, hd = att[t]["nh"], att[t]["hd"]
                par = cst[:, C_PAR:C_PAR + 2].unsqueeze(1).unsqueeze(3).broadcast_to([P, nh, 2, hd])
                split = "p (j e d) -> p j e d"
                dve.wait_ge(ev(t + "_v_psum"), 1)
                v = bank(2, D)
                if t == "e":
                    link(dve, dve.tensor_tensor(vbd[:, :], v, e_bv[:, :], ALU.add))
                    v = vbd[:, :]
                dve.tensor_tensor(vbd[:, :].rearrange(split, e=2, d=hd), v.rearrange(split, e=2, d=hd), par,
                                  ALU.mult).then_inc(ev(t + "_vbd"), 1)

            def queries(t):
                dve.wait_ge(ev(t + "_q_psum"), 1)
                if t == "e":
                    for c in range(DC):
                        dve.tensor_scalar(qT[:, c, :], bank(3, S, c * S), e_bias[:, c:c + 1], att[t]["scale"],
                                          ALU.add, ALU.mult).then_inc(ev(t + "_q"), 1)
                else:
                    dve.tensor_scalar(qT, bank(3, DC * S).rearrange("p (c s) -> p c s", c=DC), att[t]["scale"], None,
                                      ALU.mult).then_inc(ev(t + "_q"), 1)

            def softmax(t):
                a = att[t]
                nh, sc, hd = a["nh"], a["sc"], a["hd"]
                half = nh // 2

                def each(v, hs):
                    return v[:, hs].unsqueeze(2).broadcast_to([P, half, S])

                halves = (slice(0, half), slice(half, nh))
                dve.wait_ge(ev(t + "_scores"), DC)
                cap = cst[:, a["cap"]:a["cap"] + S].unsqueeze(1).broadcast_to([P, half, S])
                scores = ps[:, 4 * BANK:4 * BANK + nh * S].rearrange("p (h k) -> p h k", h=nh)
                capped = [mark(dve.tensor_tensor(sc[:, hs, :], scores[:, hs, :], cap, ALU.min)) for hs in halves]
                for u, hs in enumerate(halves):
                    dve.wait_ge(ev("dve_step"), capped[u])
                    link(dve, dve.tensor_reduce(row_max[:, hs], sc[:, hs, :], AX, ALU.max))
                    dve.tensor_tensor(sc[:, hs, :], sc[:, hs, :], each(row_max, hs),
                                      ALU.subtract).then_inc(ev(t + "_shifted"), 1)
                for u, hs in enumerate(halves):
                    dve.wait_ge(ev(t + "_exp"), u + 1)
                    link(dve, dve.tensor_reduce(row_sum[:, hs], sc[:, hs, :], AX, ALU.add))
                link(dve, dve.reciprocal(row_inv[:, 0:nh], row_sum[:, 0:nh]))
                dve.wait_ge(ev(t + "_o_psum"), 1)
                dve.tensor_tensor(oT[:, :].rearrange("p (h d) -> p h d", h=nh),
                                  bank(0, P).rearrange("p (h d) -> p h d", h=nh),
                                  row_inv[:, 0:nh].unsqueeze(2).broadcast_to([P, nh, hd]),
                                  ALU.mult).then_inc(ev(t + "_o"), 1)
                dve.wait_ge(ev(t + "_oT_psum"), 1)
                dve.tensor_copy(oT[:, :], bank(1, P)).then_inc(ev(t + "_oT"), 1)

            def add_halves(done, count, b, last):
                dve.wait_ge(ev(done), count)
                link(dve, dve.tensor_tensor(res[:, :], bank(b, D, rows=slice(0, S)), res[:, :], ALU.add))
                ins = dve.tensor_tensor(res[:, :], bank(b, D, rows=slice(S, 2 * S)), res[:, :], ALU.add)
                if last:
                    ins.then_inc(ev("result"), 1)
                else:
                    link(dve, ins)

            dve.memset(warm_data[:, :], 1.0).then_inc(ev("warm_data"), 1)

            loaded(dve, "x")
            norm("a", res[:, :], nrm[:, :])
            loaded(dve, "cst")
            for c in range(DC):
                key_blocks("a", c)
            value_blocks("a")
            turned_twice("a")
            queries("a")
            loaded(dve, "b")
            dve.tensor_reduce(dt_min, dt_row[:, :], AX, ALU.min).then_inc(ev("dt_min"), 1)
            dve.reciprocal(temp_inv, temp).then_inc(ev("temp_inv"), 1)
            softmax("a")
            dve.wait_ge(ev("dt_exp"), 2)
            link(dve, dve.reciprocal(dt_inv, dt_sum))
            link(dve, dve.tensor_scalar(dt_w, dt_e, dt_inv, None, ALU.mult))
            dve.wait_ge(ev("a_out"), 1)
            link(dve, dve.tensor_tensor(res[:, :], bank(2, D, rows=slice(0, S)), res[:, :], ALU.add))

            norm("b", res[:, :], nrm[:, :])
            dve.wait_ge(ev("norm"), 1 + NORMS.index("b"))
            norm("b2", nrm[:, :], nrm2[:, :])
            link(dve, dve.tensor_tensor(res[:, :], res[:, :], nrm[:, :], ALU.add))
            dve.wait_ge(ev("b_xT_psum"), 1)
            for c in range(DC):
                dve.tensor_scalar(xT[:, c, 0, :], bank(0, S, c * S), gamma[:, c:c + 1], beta[:, c:c + 1],
                                  ALU.mult, ALU.add).then_inc(ev("b_xT"), 1)
            proj = bank(1, 8 * S).rearrange("p (c s) -> p c s", c=8)
            dve.wait_ge(ev("b_proj"), 1)
            dve.tensor_scalar(b_clip[:, :, :], proj, -15.0, 15.0, ALU.max, ALU.min).then_inc(ev("b_clipped"), 1)
            link(dve, dve.tensor_tensor(b_z[:, :, :], proj[:, 0:4, :],
                                        dt_w.unsqueeze(2).broadcast_to([P, 4, S]), ALU.mult))
            dve.wait_ge(ev("b_clipped"), 1)
            link(dve, dve.tensor_tensor(b_z[:, :, :], b_z[:, :, :], b_clip[:, 4:8, :], ALU.mult))
            dve.wait_ge(ev("b_sigmoid"), 1)
            link(dve, dve.tensor_tensor(b_z[:, :, :], b_z[:, :, :], b_sig[:, 0:4, :], ALU.mult))
            dve.tensor_tensor(b_z[:, :, :], b_z[:, :, :], b_sig[:, 4:8, :], ALU.mult).then_inc(ev("b_gated"), 1)
            dve.wait_ge(ev("b_out"), 1)
            ins = dve.tensor_tensor(res[:, :], bank(0, D, rows=slice(0, S)), res[:, :], ALU.add)
            ins.then_inc(ev("b_done"), 1)
            dve.wait_ge(ev("b_done"), 1)

            norm("c", res[:, :], nrm[:, :])
            turned_twice("c")
            dve.wait_ge(ev("c_inh"), 1)
            dve.tensor_scalar(zone, inh, GOLDEN_LOWER, None, ALU.is_ge).then_inc(ev("c_zone"), 1)
            link(dve, dve.tensor_scalar(dist, inh, GOLDEN_CENTER, None, ALU.subtract))
            dve.scalar_tensor_tensor(dist, dist, -1.0, dist, ALU.mult, ALU.max).then_inc(ev("c_dist"), 1)
            dve.wait_ge(ev("c_zone"), 1)
            link(dve, dve.scalar_tensor_tensor(zone, inh, GOLDEN_UPPER, zone, ALU.is_le, ALU.mult))
            link(dve, dve.memset(fallback[:, C_E:14], -1.0))
            link(dve, dve.memset(taken, -1.0))
            dve.wait_ge(ev("c_exp"), 2)
            link(dve, dve.scalar_tensor_tensor(w_zone, w_zone, 1.0, zone, ALU.mult, ALU.mult, accum_out=w_sum))
            link(dve, dve.max(top, fallback))
            link(dve, dve.tensor_scalar(no_expert, w_sum, 1e-8, None, ALU.is_lt))
            link(dve, dve.tensor_copy(taken[:, 0:2], top[:, 0:2]))
            link(dve, dve.match_replace(left, taken, fallback, -2.0))
            link(dve, dve.scalar_tensor_tensor(left[:, 0:C_E], left[:, 0:C_E], -1.5, fallback[:, 0:C_E],
                                               ALU.is_lt, ALU.mult, accum_out=w_sum))
            link(dve, dve.tensor_scalar(w_sum, w_sum, 1e-8, None, ALU.max))
            link(dve, dve.reciprocal(w_sum, w_sum))
            link(dve, dve.tensor_scalar(left[:, 0:C_E], left[:, 0:C_E], w_sum, no_expert, ALU.mult, ALU.mult))
            link(dve, dve.tensor_scalar(no_expert, no_expert, -1.0, 1.0, ALU.mult, ALU.add))
            link(dve, dve.scalar_tensor_tensor(w_zone, w_zone, no_expert, left[:, 0:C_E], ALU.mult, ALU.add,
                                               accum_out=w_sum))
            link(dve, dve.tensor_scalar(w_sum, w_sum, 1e-8, None, ALU.max))
            link(dve, dve.reciprocal(w_sum, w_sum))
            for half in range(2):
                r = slice(half * S, half * S + S)
                link(dve, dve.tensor_scalar(w_c[r, :], w_zone.rearrange("p (j e) -> p e j", e=2)[r, half, :],
                                            w_sum[r, :], None, ALU.mult))
            for j in range(C_E // 2):
                dve.wait_ge(ev("c_silu"), j + 1)
                dve.scalar_tensor_tensor(c_mid[:, j, :], c_mid[:, j, :], w_c[:, C_PAIR[j]:C_PAIR[j] + 1],
                                         bank(2 + j, C_F, C_F),
                                         ALU.mult, ALU.mult).then_inc(ev("c_mid"), 1)

            def keys_low(n):
                w = min(4, NT - 4 * n) * P
                dve.wait_ge(ev("keys_high"), n + 1)
                dve.tensor_tensor(keys[L:2 * L, n * BANK:n * BANK + w], bank(n % 2, w, rows=slice(0, L)),
                                  keys[0:L, n * BANK:n * BANK + w].bitcast(F32),
                                  ALU.subtract).then_inc(ev("keys_low"), 1)

            for n in range(2):
                keys_low(n)
            add_halves("c_sum", 1, 4, False)

            def rotate():
                hs = slice(0, GH)

                def tab(k):
                    return rope_q[:, k, :].unsqueeze(1).broadcast_to([X_HALF, GH, S])

                lo, hi = (bank(b, rows=slice(0, X_HALF)).rearrange("p (h s) -> p h s", h=GH) for b in QBIG_BANK[0])
                dve.wait_ge(ev("qbig_psum"), 1)
                dve.tensor_tensor(q_lo[:, hs, :], lo, tab(0), ALU.mult).then_inc(ev("q_rot"), 1)
                dve.tensor_tensor(q_hi[:, hs, :], hi, tab(1), ALU.mult).then_inc(ev("q_rot"), 1)
                dve.tensor_tensor(q_hi_sin[:, hs, :], hi, tab(2), ALU.mult).then_inc(ev("q_rot"), 1)
                dve.tensor_tensor(q_lo_sin[:, hs, :], lo, tab(3), ALU.mult).then_inc(ev("q_rot"), 1)
                dve.wait_ge(ev("q_rot"), 4)
                dve.tensor_tensor(q_lo[:, hs, :], q_lo[:, hs, :], q_hi_sin[:, hs, :],
                                  ALU.subtract).then_inc(ev("q_roped"), 1)
                dve.tensor_tensor(q_hi[:, hs, :], q_hi[:, hs, :], q_lo_sin[:, hs, :],
                                  ALU.add).then_inc(ev("q_roped"), 1)

            norm("d", res[:, :], nrm[:, :])
            turned_twice("d", 5)
            for n in range(2, KEYS_HALF + 1):
                keys_low(n)
            dve.memset(st_h1[L:L + 2, :].bitcast(F32), 1.0).then_inc(ev("st_ones"), 1)
            rotate()
            for n in range(KEYS_HALF + 1, KGROUPS):
                if n == KEYS_LAST:
                    dve.wait_ge(ev("q_high"), 1)
                    dve.tensor_copy(q_hh[L:2 * L, 0:GQ], q_hh[0:L, 0:GQ].bitcast(F32)).then_inc(ev("q_high_twice"), 1)
                keys_low(n)

            def stage(g, i, half):
                a, b = HALVES[half]
                src = bass.ds(i * CHUNK + a * P, (b - a) * P) if not isinstance(i, int) else \
                    slice(i * CHUNK + a * P, i * CHUNK + b * P)
                free = i * BODY + (g * NT - (BODY - b))
                if not isinstance(free, int) or free > 0:
                    dve.wait_ge(ev("scores"), free)
                dve.tensor_copy(st_hl[:, a * P:b * P], keys[:, src].bitcast(F32)).then_inc(ev("staged"), 1)
                dve.tensor_copy(st_h1[0:L, a * P:b * P], keys[0:L, src].bitcast(F32)).then_inc(ev("staged"), 1)

            def maximum(g, i, m):
                n = i * 2 * QT + (g * 2 * QT * NPASS + m)
                j, k = m // 2, m % 2
                dst = key_max[:, j, bass.ds(i * 2 + k, 1)] if not isinstance(i, int) else \
                    key_max[:, j, 2 * i + k:2 * i + k + 1]
                dve.wait_ge(ev("max_scores"), n + 1)
                dve.tensor_reduce(dst, bank(MAX_BANK[m % 4], HALF), AX, ALU.max).then_inc(ev("key_max"), 1)

            def low(g, i, j):
                if g == 0 and j in LOW_POOL:
                    return
                t = i * BODY + (g * NT + j)
                dve.wait_ge(ev("probs"), t + 1)
                dve.tensor_tensor(probs_l[:, SPLIT[j], :], probs[:, SLOT[j], :],
                                  probs_h[:, SPLIT[j], :].bitcast(F32), ALU.subtract).then_inc(ev("probs_low"), 1)

            def shift(g):
                dve.wait_ge(ev("key_max"), (g + 1) * 2 * QT * NPASS)
                link(dve, dve.tensor_reduce(q_max[:, :], key_max[:, :, :], AX, ALU.max))
                link(dve, dve.tensor_copy(q_max_split[:, :, 0], q_max[:, :]))
                dve.tensor_tensor(q_max_split[:, :, 1], q_max[:, :], q_max_split[:, :, 0].bitcast(F32),
                                  ALU.subtract).then_inc(ev("q_max"), 1)
                if g == 0:
                    stage(0, 0, 0)
                dve.wait_ge(ev("q_max_row"), g + 1)
                dve.tensor_scalar(q_lm[L:L + 2, g * GQ:(g + 1) * GQ], bank(5, GQ, rows=slice(L, L + 2)), -1.0,
                                  None, ALU.mult).then_inc(ev("q_shift"), 1)

            def invert_sums(g):
                dve.wait_ge(ev("den_psum"), g + 1)
                if g:
                    dve.wait_ge(ev("den_row"), g)
                dve.reciprocal(den_inv[:, 0:QT], bank(5, QT)).then_inc(ev("den_inv"), 1)

            def weigh(g):
                dve.wait_ge(ev("den_row"), g + 1)
                dve.tensor_tensor(ctx_n[:, g, :], bank(6, GQ, rows=slice(0, L)), ctx_un[0:L, g, :],
                                  ALU.mult).then_inc(ev("ctx_n"), 1)

            for m in range(4):
                maximum(0, 0, m)
            for n in range(4, PEELED * 2 * QT):
                maximum(0, n // (2 * QT), n % (2 * QT))
            with dve.Fori(PEELED, NPASS) as i:
                for m in range(2 * QT):
                    maximum(0, i, m)
            shift(0)
            for g in range(GRP):
                def turn(i):
                    m = 0
                    for j in range(BODY):
                        if j == 1:
                            stage(g, i, 1)
                        if j == 5:
                            if not (isinstance(i, int) and i == NPASS - 1):
                                stage(g, i + 1, 0)
                            elif g + 1 < GRP:
                                stage(g + 1, 0, 0)
                        low(g, i, j)
                        if g + 1 < GRP:
                            for _ in range(MAX_AFTER[j]):
                                maximum(g + 1, i, m)
                                m += 1
                        if g and isinstance(i, int) and i == 0:
                            if j == 0:
                                invert_sums(g - 1)
                            if j == 3:
                                weigh(g - 1)

                turn(0)
                with dve.Fori(1, NPASS - 1) as i:
                    turn(i)
                turn(NPASS - 1)
                if g + 1 < GRP:
                    shift(g + 1)

            invert_sums(GRP - 1)
            weigh(GRP - 1)
            add_halves("d_sum", 1, 7, False)

            norm("e", res[:, :], nrm[:, :])
            loaded(dve, "ebias")
            link(dve, dve.tensor_tensor(res[:, :], res[:, :], e_bp[:, :], ALU.add))
            turned_twice("e")
            key_blocks("e", 0)
            queries("e")
            key_blocks("e", 1)
            value_blocks("e")
            softmax("e")
            dve.wait_ge(ev("e_out"), 1)
            link(dve, dve.tensor_tensor(res[:, :], bank(2, D, rows=slice(0, S)), res[:, :], ALU.add))

            norm("f", res[:, :], nrm[:, :])
            turned_twice("f")
            dve.wait_ge(ev("f_logits"), 1)
            link(dve, dve.tensor_reduce(f_shift, bank(1, F_E), AX, ALU.max))
            dve.tensor_scalar(f_shift, f_shift, -1.0, None, ALU.mult).then_inc(ev("f_shift"), 1)
            dve.wait_ge(ev("f_exp"), 1)
            link(dve, dve.max(top, f_exp))
            link(dve, dve.match_replace(f_left, top, f_exp, -1.0))
            link(dve, dve.scalar_tensor_tensor(f_left, f_left, 0.0, f_exp, ALU.is_lt, ALU.mult, accum_out=w_sum))
            link(dve, dve.reciprocal(w_sum, w_sum))
            for half in range(2):
                r = slice(half * S, half * S + S)
                link(dve, dve.tensor_scalar(w_f[r, :], f_left.rearrange("p (j e) -> p e j", e=2)[r, half, :],
                                            w_sum[r, :], None, ALU.mult))

            for u in range(F_STEPS):
                b = u % 2
                dve.wait_ge(ev("f_silu"), u + 1)
                for j in range(2):
                    dve.scalar_tensor_tensor(f_mid[:, b, j, :], f_mid[:, b, j, :], w_f[:, 2 * u + j:2 * u + j + 1],
                                             bank(2 + b, F_I, (2 * j + 1) * F_I), ALU.mult,
                                             ALU.mult).then_inc(ev("f_mid"), 1)
                dve.wait_ge(ev("f_midT_psum"), u + 1)
                if u >= 2:
                    dve.wait_ge(ev("f_down"), u - 1)
                dve.tensor_copy(f_midT[:, b, :, :], bank(6 + b, 2 * P, rows=slice(0, F_I)).rearrange(
                    "p (j q) -> p j q", j=2)).then_inc(ev("f_midT"), 1)
            add_halves("f_down", F_STEPS, 0, True)

        @block.tensor
        def _(pe):
            def keep_warm(n, b):
                for _ in range(n):
                    pe.matmul(bank(b), warm_data[:, :], warm_data[:, :].unsqueeze(1).broadcast_to([P, BANK // P, P]),
                              start=True, stop=True)

            def turn_x(t, src, norm, b=0, warm=(0, 7)):
                pe.wait_ge(ev("norm"), 1 + NORMS.index(norm))
                for c in range(DC):
                    ins = pe.transpose(bank(b, S, c * S), src[:, c * P:(c + 1) * P], ident[0:S, 0:S])
                ins.then_inc(ev(t + "_xT_psum"), 1)
                keep_warm(*warm)

            def mask_scores(t):
                add = cst[:, att[t]["add"]:att[t]["add"] + S].unsqueeze(1).broadcast_to([P, BANK // S, S])
                for k in range(att[t]["nh"] * S // BANK):
                    pe.matmul(bank(4 + k), ident, add, start=True, stop=False)

            def small_attention(t):
                a = att[t]
                nh, hd, pt = a["nh"], a["hd"], a["pt"]
                pairs = nh // 2
                pe.wait_ge(ev(t + "_q"), DC if t == "e" else 1)
                for c in range(DC):
                    pe.wait_ge(ev(t + "_kbd"), c + 1)
                    kc = a["kbd"][:, c, :, :].rearrange("p h k -> p (h k)")
                    for k in range(nh * S // BANK):
                        ins = pe.matmul(bank(4 + k, rows=slice(c * S, c * S + S)), qT[:, c, :],
                                        kc[:, k * BANK:(k + 1) * BANK], start=False, stop=True)
                    ins.then_inc(ev(t + "_scores"), 1)
                if t == "a":
                    fold_keys(0)
                keep_warm(W[t + "_softmax"], 3)
                sc = a["sc"][:, :, :].rearrange("p h k -> p (h k)")
                for u in range(2):
                    pe.wait_ge(ev(t + "_exp"), u + 1)
                    for j in range(u * pairs // 2, (u + 1) * pairs // 2):
                        ins = pe.transpose(bank(6 + u, P, (j % (pairs // 2)) * P), sc[:, j * P:(j + 1) * P], ident)
                    ins.then_inc(ev(t + "_probsT_psum"), 1)
                    keep_warm(W[t + "_probs"], 3)
                pe.wait_ge(ev(t + "_vbd"), 1)
                w = 2 * hd
                for j in range(pairs):
                    pe.wait_ge(ev(t + "_probsT"), 2 * j // pairs + 1)
                    for c in range(DC):
                        ins = pe.matmul(bank(0, w, j * w, rows=slice(c * S, c * S + S)), pt[:, j, c * S:c * S + S],
                                        vbd[:, c * P + j * w:c * P + (j + 1) * w], start=True, stop=True)
                ins.then_inc(ev(t + "_o_psum"), 1)
                keep_warm(W[t + "_o"], 3)
                pe.wait_ge(ev(t + "_o"), 1)
                pe.transpose(bank(1, P), oT[:, :], ident).then_inc(ev(t + "_oT_psum"), 1)
                keep_warm(W[t + "_oT"], 3)
                pe.wait_ge(ev(t + "_oT"), 1)
                if t == "a":
                    loaded(pe, "awo")
                for c in range(DC):
                    ins = pe.matmul(bank(2, D, rows=slice(0, S)), oT[:, c * S:(c + 1) * S], a["wo"][:, c, :],
                                    start=(c == 0), stop=(c == DC - 1))
                ins.then_inc(ev(t + "_out"), 1)

            def fold_keys(n):
                half, hh = n // 2, n % 2
                r = slice(hh * S, hh * S + S)
                loaded(pe, "wr")
                for h in range(8):
                    ins = pe.matmul(bank(QK_BANK[n], L, h * L, rows=slice(0, X_HALF)),
                                    x_wqr[r, h, half * X_HALF:(half + 1) * X_HALF], x_wkr[r, h, :],
                                    start=True, stop=True)
                ins.then_inc(ev("qk_fold_psum"), 1)

            pe.wait_ge(ev("warm_data"), 1)
            keep_warm(W["start"], 7)
            loaded(pe, "actx")
            loaded(pe, "awkv")
            for c in range(DC):
                ins = pe.matmul(bank(1, S, c * S), a_wkv[:, c * P:(c + 1) * P], a_ctx[:, 0, :],
                                start=True, stop=True)
            ins.then_inc(ev("a_k_psum"), 1)
            pe.matmul(bank(2, D), a_ctx[:, :, :].rearrange("p e s -> p (e s)"), a_wkv[:, D:2 * D],
                      start=True, stop=True).then_inc(ev("a_v_psum"), 1)
            loaded(pe, "cst")
            turn_x("a", nrm, "a")
            mask_scores("a")
            loaded(pe, "awq")
            pe.wait_ge(ev("a_xT"), 1)
            for c in range(DC):
                for d in range(DC):
                    ins = pe.matmul(bank(3, S, c * S), a_wq[:, d, c * P:(c + 1) * P], xT[:, d, 0, :],
                                    start=(d == 0), stop=(d == DC - 1))
            ins.then_inc(ev("a_q_psum"), 1)
            small_attention("a")
            fold_keys(1)
            fold_keys(2)
            keep_warm(W["b_norm"], 0)

            turn_x("b", nrm2, "b2", warm=(W["xT"], 1))
            loaded(pe, "bw")
            pe.wait_ge(ev("b_xT"), DC)
            for e in range(2 * B_INNER // P):
                for d in range(DC):
                    ins = pe.matmul(bank(1, S, e * S), b_win[:, d, e * P:(e + 1) * P], xT[:, d, 0, :],
                                    start=(d == 0), stop=(d == DC - 1))
            ins.then_inc(ev("b_proj"), 1)
            pe.wait_ge(ev("qk_fold"), 1)
            fold_keys(3)
            keep_warm(W["b_gate"], 0)
            pe.wait_ge(ev("b_gated"), 1)
            for e in range(B_INNER // P):
                ins = pe.matmul(bank(0, D, rows=slice(0, S)), b_z[:, e, :], b_wout[:, e, :],
                                start=(e == 0), stop=(e == B_INNER // P - 1))
            ins.then_inc(ev("b_out"), 1)

            keep_warm(W["c_norm"], 1)
            turn_x("c", nrm, "c", warm=(W["xT"], 1))
            pe.wait_ge(ev("c_xT"), 1)
            for d in range(DC):
                ins = pe.matmul(bank(1, C_E), xT[:, d, :, :].rearrange("p e s -> p (e s)"), c_wr[:, d, :],
                                start=(d == 0), stop=(d == DC - 1))
            ins.then_inc(ev("c_logits"), 1)
            pe.wait_ge(ev("qk_fold"), 4)
            loaded(pe, "cgu_first")
            for j in range(C_E // 2):
                if j == C_E // 4:
                    loaded(pe, "lora")
                    for q in range(2):
                        for d in range(DC):
                            for e in range(C_LORA):
                                ins = pe.matmul(bank(6, S, q * S, rows=slice(e * C_R, (e + 1) * C_R)),
                                                lora_in[:, d, e, q, :], xT[:, d, 0, :], start=(d == 0),
                                                stop=(d == DC - 1))
                    ins.then_inc(ev("lora_x_psum"), 1)
                    loaded(pe, "cgu")
                for d in range(DC):
                    for e in range(2):
                        ins = pe.matmul(bank(2 + j, rows=slice(e * S, e * S + S)), xT[:, d, 0, :],
                                        l0_gu[:, d, 2 * j + e, :], start=(d == 0),
                                        stop=(d == DC - 1 and j < C_E // 2 - 1))
                if j == C_E // 2 - 1:
                    pe.wait_ge(ev("lora_x"), 1)
                    for q in range(2):
                        for e in range(C_LORA):
                            r = slice(e * C_R, (e + 1) * C_R)
                            ins = pe.matmul(bank(2 + j, C_F, q * C_F, rows=slice(e * S, e * S + S)), lora_x[r, q, :],
                                            lora_out[r, q, :], start=False, stop=(q == 1))
                ins.then_inc(ev("c_gu"), 1)

            def turn_keys(n):
                if n >= 2:
                    pe.wait_ge(ev("keys_low"), n - 1)
                for t in range(4 * n, min(4 * n + 4, NT)):
                    ins = pe.transpose(bank(n % 2, P, (t % 4) * P, rows=slice(0, L)), kv[:, t, :], ident)
                ins.then_inc(ev("keysT"), 1)

            for n in range(2):
                pe.wait_ge(ev("c_mid"), 2 * n + 2)
                for j in range(2 * n, 2 * n + 2):
                    for f in range(2):
                        ins = pe.transpose(bank(2 + n, P, (j % 2) * 2 * P + f * P), c_mid[:, j, f * P:(f + 1) * P],
                                           ident)
                ins.then_inc(ev("c_midT_psum"), 1)
            pe.wait_ge(ev("roped"), 2)
            for n in range(2):
                turn_keys(n)
            pe.wait_ge(ev("c_midT"), 2)
            for f in range(2):
                for e in range(C_LORA):
                    ins = pe.matmul(bank(7, S, rows=slice(e * C_R, (e + 1) * C_R)), lora_mid[:, f, e, :],
                                    c_midT[:, C_E // 2 - 1, f, e * S:e * S + S], start=(f == 0), stop=(f == 1))
            ins.then_inc(ev("lora_m_psum"), 1)
            loaded(pe, "cdown")
            for j in range(C_E // 2):
                pe.wait_ge(ev("c_midT"), j // 2 + 1)
                for f in range(2):
                    for e in range(2):
                        ins = pe.matmul(bank(4, D, rows=slice(e * S, e * S + S)), c_midT[:, j, f, e * S:e * S + S],
                                        l0_down[:, f, 2 * j + e, :], start=(j + f == 0),
                                        stop=False)
            pe.wait_ge(ev("lora_m"), 1)
            for e in range(C_LORA):
                r = slice(e * C_R, (e + 1) * C_R)
                ins = pe.matmul(bank(4, D, rows=slice(e * S, e * S + S)), lora_m[r, :], lora_out[r, 2, :],
                                start=False, stop=True)
            ins.then_inc(ev("c_sum"), 1)
            for n in range(2, KEYS_FIRST):
                turn_keys(n)
                if n == 3:
                    keep_warm(W["d_norm"], 6)

            turn_x("d", nrm, "d", 5, warm=(W["d_xT"], 7))
            loaded(pe, "wq")
            pe.wait_ge(ev("d_xT"), 1)

            def first_queries(g, keys):
                for h in range(GH):
                    for d in range(DC):
                        col = (g * GH + h) * X_K
                        ins = pe.matmul(bank(QHK_BANK[g], S, h * S), x_wq[:, d, col:col + X_K], xT[:, d, 0, :],
                                        start=(d == 0), stop=(d == DC - 1))
                    if h == GH - 1:
                        ins.then_inc(ev("qhk_psum"), 1)
                    if h % 2 and keys + h // 2 < (KEYS_LAST if g else KEYS_HALF):
                        turn_keys(keys + h // 2)

            def wide_queries(g, part=range(GH)):
                pe.wait_ge(ev("qhk"), g + 1)
                for h in part:
                    for half in range(2):
                        ins = pe.matmul(bank(QBIG_BANK[g][half], S, h * S, rows=slice(0, X_HALF)),
                                        x_kcq[:, g * GH + h, half * X_HALF:(half + 1) * X_HALF],
                                        qhk[:, g * GH + h, :], start=True, stop=True)
                if GH - 1 in part:
                    ins.then_inc(ev("qbig_psum"), 1)

            def last_queries(g):
                pe.wait_ge(ev("q_roped"), 2 * (g + 1))
                for h in range(g * GH, (g + 1) * GH):
                    for half, q in ((0, q_lo), (1, q_hi)):
                        ins = pe.matmul(bank(Q_BANK[g], S, (h % GH) * S, rows=slice(0, L)), x_qk[:, half, h, :],
                                        q[:, h, :], start=(half == 0), stop=(half == 1))
                ins.then_inc(ev("q_psum"), 1)

            first_queries(0, KEYS_FIRST)
            turn_keys(KEYS_HALF)
            loaded(pe, "kcq")
            wide_queries(0)
            first_queries(1, KEYS_HALF + 1)
            last_queries(0)
            for n in range(KEYS_LAST, KGROUPS):
                turn_keys(n)
            pe.wait_ge(ev("qhk"), 2)

            def max_scores(g, i, m):
                n = i * 2 * QT + (g * 2 * QT * NPASS + m)
                j, k = m // 2, m % 2
                if not isinstance(n, int) or n >= 4:
                    pe.wait_ge(ev("key_max"), n - 3)
                src = bass.ds(i * CHUNK + k * HALF, HALF) if not isinstance(i, int) else \
                    slice(i * CHUNK + k * HALF, i * CHUNK + (k + 1) * HALF)
                pe.matmul(bank(MAX_BANK[m % 4], HALF), q_hh[:, g * GQ + j * P:g * GQ + (j + 1) * P], keys[:, src],
                          start=True, stop=True).then_inc(ev("max_scores"), 1)

            def max_row(g):
                pe.wait_ge(ev("q_max"), g + 1)
                for j in range(QT):
                    ins = pe.matmul(bank(5, P, j * P, rows=slice(L, L + 2)), q_max_split[:, j, :].bitcast(F32), ident,
                                    start=True, stop=True)
                ins.then_inc(ev("q_max_row"), 1)

            def sums(g):
                pe.wait_ge(ev("ctx_un"), g + 1)
                for n in range(QT):
                    ins = pe.matmul(bank(5, 1, n), ctx_un[L:L + 1, g, n * P:(n + 1) * P],
                                    cst[L:L + 1, C_ONE:C_ONE + 1], start=True, stop=True)
                ins.then_inc(ev("den_psum"), 1)

            def sums_row(g):
                pe.wait_ge(ev("den_inv"), g + 1)
                for j in range(QT):
                    ins = pe.matmul(bank(6, P, j * P, rows=slice(0, L)), den_inv[:, j:j + 1].broadcast_to([P, L]), ident,
                                    start=True, stop=True)
                ins.then_inc(ev("den_row"), 1)

            def output(g, heads=range(GH)):
                pe.wait_ge(ev("ctx_n"), g + 1)
                for h in heads:
                    r = slice((h % 2) * S, (h % 2) * S + S)
                    ins = pe.matmul(bank(7, D, rows=r), ctx_n[:, g, h * S:(h + 1) * S], x_wo[0:L, g * GH + h, :],
                                    start=(g == 0 and h < 2), stop=(g == GRP - 1 and h >= GH - 2))
                if g == GRP - 1:
                    ins.then_inc(ev("d_sum"), 1)

            def fold_output(n):
                if n >= 2:
                    pe.wait_ge(ev("wo_fold"), n - 1)
                for h in range(2):
                    ins = pe.matmul(bank(FOLD_BANK[n % 2], D, h * D, rows=slice(0, L)), x_kckv[:, 2 * n + h, :],
                                    x_wo[:, 2 * n + h, :], start=True, stop=True)
                ins.then_inc(ev("wo_fold_psum"), 1)

            pe.wait_ge(ev("q_high"), 1)
            pe.wait_ge(ev("q_high_twice"), 1)
            for m in range(4):
                max_scores(0, 0, m)
            pe.wait_ge(ev("keys_low"), KGROUPS)
            wide_queries(1, range(GH // 2))
            for m in range(4, 6):
                max_scores(0, 0, m)
            wide_queries(1, range(GH // 2, GH))
            loaded(pe, "wo")
            pe.wait_ge(ev("q_full"), 1)
            for n in range(6, PEELED * 2 * QT):
                if n in FOLD_BEFORE:
                    fold_output(FOLD_BEFORE.index(n))
                if n == QUERIES_BEFORE:
                    last_queries(1)
                max_scores(0, n // (2 * QT), n % (2 * QT))
            with pe.Fori(PEELED, NPASS) as i:
                for m in range(2 * QT):
                    max_scores(0, i, m)
            pe.wait_ge(ev("wo_fold"), X_H // 2)
            pe.wait_ge(ev("q_low"), GRP)
            keep_warm(W["max"], 1)
            max_row(0)
            keep_warm(W["max_row"], 1)
            for g in range(GRP):
                at_q = slice(g * GQ, (g + 1) * GQ)

                def weight(t, i, j, first, last):
                    acc, p_h, p_l = bank(4 * g, GQ, rows=slice(0, L + 1)), probs_h[:, SPLIT[j], :], probs_l[:, SPLIT[j], :]
                    pe.wait_ge(ev("probs_high"), t + 1)
                    pe.matmul(acc, st_kvh[:, j, :], p_h, start=first, stop=False)
                    pe.matmul(acc, st_kvl[:, j, :], p_h, start=False, stop=False)
                    name, n = low_parts(g, i, j)
                    pe.wait_ge(ev(name), n)
                    pe.matmul(acc, st_kvh[:, j, :], p_l, start=False, stop=last).then_inc(ev("weighted"), 1)

                def scores_begin(i, j):
                    t = i * BODY + (g * NT + j)
                    if j in (0, 4):
                        pe.wait_ge(ev("staged"), i * 4 + (g * 4 * NPASS + (2 if j == 0 else 4)))
                    if not (isinstance(t, int) and t < SLOT_AGE[j]):
                        pe.wait_ge(ev("probs"), t + (1 - SLOT_AGE[j]))
                    pe.matmul(bank(1 + SLOT[j], GQ), st_hl[:, j * P:(j + 1) * P], q_hh[:, at_q], start=True, stop=False)

                def passes(i):
                    first = isinstance(i, int) and i == 0
                    m = 0
                    for j in range(BODY):
                        t = i * BODY + (g * NT + j)
                        if not (first and j <= LAG):
                            scores_begin(i, j)
                        pe.matmul(bank(1 + SLOT[j], GQ), st_h1[0:L + 2, j * P:(j + 1) * P], q_lm[0:L + 2, at_q], start=False,
                                  stop=True).then_inc(ev("scores"), 1)
                        if g and first and j == LAG:
                            sums(g - 1)
                        if not (first and j < LAG):
                            if (j - LAG) % BODY in (0, 4):
                                pe.wait_ge(ev("kv_staged"), i * 2 + (g * 2 * NPASS + (1 if j == LAG else 2)))
                            weight(t - LAG, i if j >= LAG else i - 1, (j - LAG) % BODY, first and j == LAG, False)
                        if g + 1 < GRP:
                            for _ in range(MAX_AFTER[j]):
                                max_scores(g + 1, i, m)
                                m += 1
                        if g and first:
                            if j == 3:
                                sums_row(g - 1)

                for j in range(LAG + 1):
                    scores_begin(0, j)
                pe.wait_ge(ev("q_shift"), g + 1)
                if g == 0:
                    pe.wait_ge(ev("st_ones"), 1)
                    pe.wait_ge(ev("kv_ones"), 2)
                passes(0)
                with pe.Fori(1, NPASS) as i:
                    passes(i)
                for j in range(BODY - LAG, BODY):
                    weight(g * NT + NT - BODY + j, NPASS - 1, j, False, j == BODY - 1)
                if g + 1 < GRP:
                    pe.wait_ge(ev("key_max"), (g + 2) * 2 * QT * NPASS - 3)
                    keep_warm(W["next_max"], 6)
                    max_row(g + 1)
                    keep_warm(W["max_row"], 6)

            output(0, range(0, 4))
            sums(GRP - 1)
            output(0, range(4, 6))
            sums_row(GRP - 1)
            output(0, range(6, GH))
            output(GRP - 1)

            mask_scores("e")
            keep_warm(W["e_norm"], 6)
            turn_x("e", nrm, "e", warm=(W["e_xT"], 6))
            loaded(pe, "ew")
            pe.wait_ge(ev("e_xT"), 1)
            for name, b, col in (("k", 1, D), ("q", 3, 0)):
                for c in range(DC):
                    for d in range(DC):
                        ins = pe.matmul(bank(b, S, c * S), e_w[:, d, col + c * P:col + (c + 1) * P],
                                        xT[:, d, 0, :], start=(d == 0), stop=(d == DC - 1))
                ins.then_inc(ev(f"e_{name}_psum"), 1)
            for d in range(DC):
                ins = pe.matmul(bank(2, D), xT[:, d, :, :].rearrange("p e s -> p (e s)"), e_w[:, d, 2 * D:3 * D],
                                start=(d == 0), stop=(d == DC - 1))
            ins.then_inc(ev("e_v_psum"), 1)
            small_attention("e")

            keep_warm(W["f_norm"], 5)
            turn_x("f", nrm, "f", warm=(W["xT"], 5))
            loaded(pe, "fwr")
            pe.wait_ge(ev("f_xT"), 1)
            for d in range(DC):
                ins = pe.matmul(bank(1, F_E), xT[:, d, :, :].rearrange("p e s -> p (e s)"), f_wr[:, d, :],
                                start=(d == 0), stop=(d == DC - 1))
            ins.then_inc(ev("f_logits"), 1)
            loaded(pe, "fgu")
            loaded(pe, "fdown")

            def gate_up(u):
                if u >= 2:
                    pe.wait_ge(ev("f_mid"), 2 * u - 2)
                for d in range(DC):
                    for e in range(2):
                        ins = pe.matmul(bank(2 + u % 2, 4 * F_I, rows=slice(e * S, e * S + S)), xT[:, d, 0, :],
                                        l1_gu[:, d, 2 * u + e, :], start=(d == 0), stop=(d == DC - 1))
                ins.then_inc(ev("f_gu"), 1)

            def turn_mid(u):
                if u >= 2:
                    pe.wait_ge(ev("f_midT"), u - 1)
                for j in range(2):
                    pe.wait_ge(ev("f_mid"), 2 * u + j + 1)
                    ins = pe.transpose(bank(6 + u % 2, P, j * P, rows=slice(0, F_I)), f_mid[:, u % 2, j, :], ident)
                ins.then_inc(ev("f_midT_psum"), 1)

            def down(u):
                pe.wait_ge(ev("f_midT"), u + 1)
                for j in range(2):
                    for e in range(2):
                        ins = pe.matmul(bank(0, D, rows=slice(e * S, e * S + S)), f_midT[:, u % 2, j, e * S:e * S + S],
                                        l1_down[:, 4 * u + 2 * j + e, :], start=(u + j == 0),
                                        stop=(u == F_STEPS - 1 and j == 1))
                ins.then_inc(ev("f_down"), 1)

            gate_up(0)
            for u in range(F_STEPS):
                if u + 1 < F_STEPS:
                    gate_up(u + 1)
                if u:
                    down(u - 1)
                turn_mid(u)
            down(F_STEPS - 1)


def kernel(**inputs):
    import concourse.bacc as _bacc
    from concourse.bass_utils import run_bass_kernel_spmd as _run

    a = {k: np.asarray(v) for k, v in inputs.items()}

    def rows(w):
        return w.reshape((w.shape[0] // P, P) + w.shape[1:]).swapaxes(0, 1)

    def halves(w):
        n = w.shape[0] // 2
        return w.reshape(2, n, *w.shape[1:]).transpose(0, 2, 1, 3).reshape(2 * w.shape[1], n, w.shape[2])

    sin, cos = rope(CTX, L, 1)
    table = np.stack([sin, cos])
    lora_in = np.stack([a["L0_ffn_Ga"], a["L0_ffn_Ua"]], 1)
    lora_out = np.stack([a["L0_ffn_Gb"], a["L0_ffn_Ub"], a["L0_ffn_Db"]], 2)
    order = [2 * p + e for p in C_PAIR for e in range(2)]
    f_gu = np.concatenate([a["L1_ffn_w_gate"], a["L1_ffn_w_up"]], 2)
    data = {
        "x": a["x"][0],
        "cst": constants(),
        "ctx_t": a["ctx_512"][0, :S].T,
        "a_wkv": a["L0_xattn_Wkv_expand"].T,
        "a_wq": rows(a["L0_xattn_Wq"].T),
        "a_wo": rows(a["L0_xattn_Wout"].T),
        "dt": a["L0_attn_dt"],
        "columns": np.concatenate([rows(a[k]) for k in ("L0_attn_gamma", "L0_attn_beta", "L0_attn_dt")] +
                                  [rows(a["L1_attn_b_attn"][:2 * D]), rows(a["L0_ffn_Wr"]).reshape(P, DC * C_E)], 1),
        "temp": a["L0_ffn_temperature"],
        "b_win": rows(a["L0_attn_W_in"].T),
        "b_wout": rows(a["L0_attn_W_out"].T),
        "lora_in": rows(lora_in.transpose(2, 0, 1, 3)),
        "lora_mid": rows(a["L0_ffn_Da"].swapaxes(0, 1)),
        "lora_out": lora_out.reshape(P, 3, D),
        "c_gu": rows(np.concatenate([a["L0_ffn_Wg"], a["L0_ffn_Wu"]], 2)[order].swapaxes(0, 1)),
        "c_down": rows(a["L0_ffn_Wd"][order].swapaxes(0, 1)),
        "ctx": a["ctx_512"][0].reshape(P, NT, L),
        "rope": table.reshape(2, P, NT, L // 2).swapaxes(0, 1),
        "x_wqr": halves(a["L1_xattn_W_qr"].swapaxes(1, 2)),
        "x_wkr": halves(a["L1_xattn_W_kr"].swapaxes(1, 2)),
        "x_kckv": a["L1_xattn_w_kc_kv"].swapaxes(0, 1),
        "x_wo": rows(a["L1_xattn_Wo"].T),
        "x_wq": rows(a["L1_xattn_Wq"].T),
        "x_kcq": a["L1_xattn_w_kc_q"].swapaxes(0, 1),
        "f_wr": rows(a["L1_ffn_router_w"].T),
        "e_b": a["L1_attn_b_attn"],
        "e_bp": a["L1_attn_b_proj"],
        "e_w": rows(a["L1_attn_W_attn"]),
        "e_wp": rows(a["L1_attn_W_proj"]),
        "f_gu": rows(f_gu.reshape(F_STEPS, 2, 2, D, 2 * F_I).transpose(3, 0, 2, 1, 4).reshape(D, F_E // 2, 4 * F_I)),
        "f_down": a["L1_ffn_w_down"].swapaxes(0, 1),
    }
    data = {k: np.ascontiguousarray(v) for k, v in data.items()}
    nc = _bacc.Bacc("TRN2", target_bir_lowering=False, num_devices=1)
    dram = {k: nc.dram_tensor(k, v.shape, F32, kind="ExternalInput").ap() for k, v in data.items()}
    out = nc.dram_tensor("out", (S, D), F32, kind="ExternalOutput").ap()
    build(nc, dram, out)
    r = _run(nc, [data], core_ids=[0])
    return r.results[0]["out"].reshape(1, S, D)
```
